# Optimizing a Trainium2 kernel written in Bass

```python
import numpy as np
import jax
import jax.numpy as jnp

def _softmax(x, axis=-1):
    return jax.nn.softmax(x, axis=axis)

def _gelu(x):
    return jax.nn.gelu(x, approximate=True)

def _silu(x):
    return jax.nn.silu(x)

def _sigmoid(x):
    return jax.nn.sigmoid(x)

def _layernorm(x, axis=-1, eps=1e-05):
    m = jnp.mean(x, axis=axis, keepdims=True)
    v = jnp.var(x, axis=axis, keepdims=True)
    return (x - m) / jnp.sqrt(v + eps)

def _scatter_add(tgt, idx, src, axis=0):
    return tgt.at[idx].add(src)

def _segment_sum(src, seg, n):
    return jax.ops.segment_sum(src, seg, n)
kernel_name = 'mk_xattn_ffn_d2_seqx_r4_b0ce83'

def setup_inputs(seed: int=0):
    np.random.seed(seed)
    _w = jnp.asarray

    def _rec_inputs():
        import jax
        import jax.numpy as jnp
        _rk = jax.random.key(seed)
        x = -0.0003929 + 0.9999 * jax.random.normal(jax.random.fold_in(_rk, 1), (16, 128, 256), jnp.float32)
        _lenS = 128 - jax.random.randint(jax.random.fold_in(_rk, 7), (16,), 0, max(1, 128 // 4) + 1, jnp.int32)
        _lenS2 = 128 - jax.random.randint(jax.random.fold_in(_rk, 8), (16,), 0, max(1, 128 // 4) + 1, jnp.int32)
        _ctx_768P = jax.random.normal(jax.random.fold_in(_rk, 11), (16, 16, 192), jnp.float32)
        _ctx_768c = jax.random.dirichlet(jax.random.fold_in(_rk, 511), 0.3 * jnp.ones((16,), jnp.float32), (16, 128))
        _ctx_768t = jnp.einsum('bsk,bkd->bsd', _ctx_768c, _ctx_768P)
        _ctx_768t = _ctx_768t * jax.lax.rsqrt(jnp.mean(jnp.square(_ctx_768t)) + 1e-12) * 0.953939
        ctx_768 = -7.36909e-05 + 0.999899 * (_ctx_768t + 0.3 * jax.random.normal(jax.random.fold_in(_rk, 611), (16, 128, 192), jnp.float32))
        return (x, ctx_768)
    x, ctx_768 = _rec_inputs()

    def _L0_xattn_setup():
        import jax, jax.numpy as jnp
        import numpy as np
        EPS = 1e-05

        def layernorm(x, g, b):
            mu = jnp.mean(x, axis=-1, keepdims=True)
            var = jnp.mean(jnp.square(x - mu), axis=-1, keepdims=True)
            return (x - mu) * jax.lax.rsqrt(var + EPS) * g + b
        key = jax.random.key(seed)
        ks = jax.random.split(key, 12)
        B, L1, L2 = (8, 512, 512)
        D1, D2, E = (256, 192, 256)
        s1, s2, se = (D1 ** (-0.5), D2 ** (-0.5), E ** (-0.5))
        return {'modality1': jax.random.normal(ks[0], (B, L1, D1), jnp.float32), 'modality2': jax.random.normal(ks[1], (B, L2, D2), jnp.float32), 'ln1_g': jnp.ones((D1,), jnp.float32), 'ln1_b': jnp.zeros((D1,), jnp.float32), 'ln2_g': jnp.ones((D2,), jnp.float32), 'ln2_b': jnp.zeros((D2,), jnp.float32), 'Wq': jax.random.normal(ks[2], (D1, E), jnp.float32) * s1, 'bq': jax.random.normal(ks[3], (E,), jnp.float32) * 0.01, 'Wk': jax.random.normal(ks[4], (D2, E), jnp.float32) * s2, 'bk': jax.random.normal(ks[5], (E,), jnp.float32) * 0.01, 'Wv': jax.random.normal(ks[6], (D2, E), jnp.float32) * s2, 'bv': jax.random.normal(ks[7], (E,), jnp.float32) * 0.01, 'Wo': jax.random.normal(ks[8], (E, D1), jnp.float32) * se, 'bo': jax.random.normal(ks[9], (D1,), jnp.float32) * 0.01}
    _L0_xattn_all = _L0_xattn_setup()
    _L0_xattn_in = {k: v for k, v in _L0_xattn_all.items() if k in ('ln1_g', 'ln1_b', 'ln2_g', 'ln2_b', 'Wq', 'bq', 'Wk', 'bk', 'Wv', 'bv', 'Wo', 'bo')}
    del _L0_xattn_all

    def _L0_ffn_setup():
        import jax, jax.numpy as jnp
        import numpy as np
        D_MODEL = 256
        NUM_SLOTS = 64
        TOP_K = 8
        B, T = (4, 1024)

        def _forward(x, slot_init, slot_scale, w1, b1, w2, b2, gru_wih, gru_whh, gru_bih, gru_bhh, wv, bv, wo, bo, tau):
            Bn, Tn, D = x.shape
            Sn = slot_init.shape[0]
            S = jnp.broadcast_to((slot_init * slot_scale)[None], (Bn, Sn, D)).astype(x.dtype)
            slot_mean = S.mean(axis=1, keepdims=True)
            ctx = jnp.concatenate([x, jnp.broadcast_to(slot_mean, x.shape)], axis=-1)
            h = jax.nn.gelu(ctx @ w1.T + b1, approximate=False)
            route_logits = (h @ w2.T + b2) / (jnp.abs(tau) + 0.1)
            topk_vals, topk_idx = jax.lax.top_k(route_logits, TOP_K)
            topk_w = jax.nn.softmax(topk_vals, axis=-1)
            alpha = jnp.sum(topk_w[..., None] * jax.nn.one_hot(topk_idx, Sn, dtype=x.dtype), axis=-2)
            slot_input = jnp.einsum('bts,btd->bsd', alpha, x)
            slot_wsum = alpha.sum(axis=1) + 1e-08
            gi = (slot_input / slot_wsum[..., None]).reshape(Bn * Sn, D)
            hs = S.reshape(Bn * Sn, D)
            gx = gi @ gru_wih.T + gru_bih
            gh = hs @ gru_whh.T + gru_bhh
            xr, xz, xn = jnp.split(gx, 3, axis=-1)
            hr, hz, hn = jnp.split(gh, 3, axis=-1)
            r = jax.nn.sigmoid(xr + hr)
            z = jax.nn.sigmoid(xz + hz)
            n = jnp.tanh(xn + r * hn)
            h_new = (1.0 - z) * n + z * hs
            S_new = h_new.reshape(Bn, Sn, D)
            slot_values = S_new @ wv.T + bv
            out = jnp.einsum('bts,bsd->btd', alpha, slot_values)
            return out @ wo.T + bo
        key = jax.random.key(seed)
        ks = jax.random.split(key, 16)
        D, S = (D_MODEL, NUM_SLOTS)
        H = D // 2
        sc = lambda fan_in: 1.0 / np.sqrt(fan_in)
        inp = {'x': jax.random.normal(ks[0], (B, T, D), dtype=jnp.float32), 'slot_init': jax.random.normal(ks[1], (S, D), dtype=jnp.float32) * 0.1, 'slot_scale': jnp.ones((S, 1), dtype=jnp.float32), 'w1': jax.random.normal(ks[2], (H, 2 * D), dtype=jnp.float32) * sc(2 * D), 'b1': jnp.zeros((H,), dtype=jnp.float32), 'w2': jax.random.normal(ks[3], (S, H), dtype=jnp.float32) * sc(H), 'b2': jnp.zeros((S,), dtype=jnp.float32), 'gru_wih': jax.random.normal(ks[4], (3 * D, D), dtype=jnp.float32) * sc(D), 'gru_whh': jax.random.normal(ks[5], (3 * D, D), dtype=jnp.float32) * sc(D), 'gru_bih': jnp.zeros((3 * D,), dtype=jnp.float32), 'gru_bhh': jnp.zeros((3 * D,), dtype=jnp.float32), 'wv': jax.random.normal(ks[6], (D, D), dtype=jnp.float32) * sc(D), 'bv': jnp.zeros((D,), dtype=jnp.float32), 'wo': jax.random.normal(ks[7], (D, D), dtype=jnp.float32) * sc(D), 'bo': jnp.zeros((D,), dtype=jnp.float32), 'tau': jnp.ones((1,), dtype=jnp.float32)}
        return inp
    _L0_ffn_all = _L0_ffn_setup()
    _L0_ffn_in = {k: v for k, v in _L0_ffn_all.items() if k in ('slot_init', 'slot_scale', 'w1', 'b1', 'w2', 'b2', 'gru_wih', 'gru_whh', 'gru_bih', 'gru_bhh', 'wv', 'bv', 'wo', 'bo', 'tau')}
    del _L0_ffn_all

    def _L1_xattn_setup():
        import jax, jax.numpy as jnp
        import numpy as np
        IMAGE_DIM = 256
        TEXT_DIM = 192
        NUM_HEADS = 16
        HEAD_DIM = IMAGE_DIM // NUM_HEADS
        key = jax.random.key(seed)
        ks = jax.random.split(key, 14)
        B, N, M = (4, 1024, 128)
        s_img = 1.0 / np.sqrt(IMAGE_DIM)
        s_txt = 1.0 / np.sqrt(TEXT_DIM)
        s_ff = 1.0 / np.sqrt(2 * IMAGE_DIM)
        return {'x': jax.random.normal(ks[0], (B, N, IMAGE_DIM), jnp.float32), 'y': jax.random.normal(ks[1], (B, M, TEXT_DIM), jnp.float32), 'Wq': jax.random.normal(ks[2], (IMAGE_DIM, IMAGE_DIM), jnp.float32) * s_img, 'bq': jax.random.normal(ks[3], (IMAGE_DIM,), jnp.float32) * s_img, 'Wk': jax.random.normal(ks[4], (TEXT_DIM, IMAGE_DIM), jnp.float32) * s_txt, 'bk': jax.random.normal(ks[5], (IMAGE_DIM,), jnp.float32) * s_txt, 'Wv': jax.random.normal(ks[6], (TEXT_DIM, IMAGE_DIM), jnp.float32) * s_txt, 'bv': jax.random.normal(ks[7], (IMAGE_DIM,), jnp.float32) * s_txt, 'W1': jax.random.normal(ks[8], (IMAGE_DIM, 2 * IMAGE_DIM), jnp.float32) * s_img, 'b1': jax.random.normal(ks[9], (2 * IMAGE_DIM,), jnp.float32) * s_img, 'W2': jax.random.normal(ks[10], (2 * IMAGE_DIM, IMAGE_DIM), jnp.float32) * s_ff, 'b2': jax.random.normal(ks[11], (IMAGE_DIM,), jnp.float32) * s_ff}
    _L1_xattn_all = _L1_xattn_setup()
    _L1_xattn_in = {k: v for k, v in _L1_xattn_all.items() if k in ('Wq', 'bq', 'Wk', 'bk', 'Wv', 'bv', 'W1', 'b1', 'W2', 'b2')}
    del _L1_xattn_all

    def _L1_ffn_setup():
        import jax, jax.numpy as jnp
        import numpy as np
        N_EXPERTS = 8
        N_GROUP = 4
        TOPK_GROUP = 2
        TOP_K = 2
        HIDDEN = 256
        INTER = 512
        B, S = (1, 256)

        def _grouped_topk(scores):
            T, E = scores.shape
            per_group = E // N_GROUP
            group_scores = scores.reshape(T, N_GROUP, per_group).max(-1)
            _, gidx = jax.lax.top_k(group_scores, TOPK_GROUP)
            gmask = jnp.zeros((T, N_GROUP), scores.dtype).at[jnp.arange(T)[:, None], gidx].set(1.0)
            smask = jnp.repeat(gmask, per_group, axis=1)
            masked = jnp.where(smask > 0, scores, 0.0)
            topk_w, topk_ids = jax.lax.top_k(masked, TOP_K)
            topk_w = topk_w / topk_w.sum(-1, keepdims=True)
            return (topk_ids, topk_w)
        key = jax.random.key(seed)
        k1, k2, k3, k4 = jax.random.split(key, 4)
        return {'hidden_states': jax.random.normal(k1, (B, S, HIDDEN), jnp.float32), 'gate_w': jax.random.normal(k2, (N_EXPERTS, HIDDEN), jnp.float32) * 0.02, 'w13_weight': jax.random.normal(k3, (N_EXPERTS, 2 * INTER, HIDDEN), jnp.float32) * 0.02, 'w2_weight': jax.random.normal(k4, (N_EXPERTS, HIDDEN, INTER), jnp.float32) * 0.02}
    _L1_ffn_all = _L1_ffn_setup()
    _L1_ffn_in = {k: v for k, v in _L1_ffn_all.items() if k in ('gate_w', 'w13_weight', 'w2_weight')}
    del _L1_ffn_all
    return {'x': x, 'ctx_768': ctx_768, 'L0_xattn_ln1_g': _L0_xattn_in['ln1_g'], 'L0_xattn_ln1_b': _L0_xattn_in['ln1_b'], 'L0_xattn_ln2_g': _L0_xattn_in['ln2_g'], 'L0_xattn_ln2_b': _L0_xattn_in['ln2_b'], 'L0_xattn_Wq': _L0_xattn_in['Wq'], 'L0_xattn_bq': _L0_xattn_in['bq'], 'L0_xattn_Wk': _L0_xattn_in['Wk'], 'L0_xattn_bk': _L0_xattn_in['bk'], 'L0_xattn_Wv': _L0_xattn_in['Wv'], 'L0_xattn_bv': _L0_xattn_in['bv'], 'L0_xattn_Wo': _L0_xattn_in['Wo'], 'L0_xattn_bo': _L0_xattn_in['bo'], 'L0_ffn_slot_init': _L0_ffn_in['slot_init'], 'L0_ffn_slot_scale': _L0_ffn_in['slot_scale'], 'L0_ffn_w1': _L0_ffn_in['w1'], 'L0_ffn_b1': _L0_ffn_in['b1'], 'L0_ffn_w2': _L0_ffn_in['w2'], 'L0_ffn_b2': _L0_ffn_in['b2'], 'L0_ffn_gru_wih': _L0_ffn_in['gru_wih'], 'L0_ffn_gru_whh': _L0_ffn_in['gru_whh'], 'L0_ffn_gru_bih': _L0_ffn_in['gru_bih'], 'L0_ffn_gru_bhh': _L0_ffn_in['gru_bhh'], 'L0_ffn_wv': _L0_ffn_in['wv'], 'L0_ffn_bv': _L0_ffn_in['bv'], 'L0_ffn_wo': _L0_ffn_in['wo'], 'L0_ffn_bo': _L0_ffn_in['bo'], 'L0_ffn_tau': _L0_ffn_in['tau'], 'L1_xattn_Wq': _L1_xattn_in['Wq'], 'L1_xattn_bq': _L1_xattn_in['bq'], 'L1_xattn_Wk': _L1_xattn_in['Wk'], 'L1_xattn_bk': _L1_xattn_in['bk'], 'L1_xattn_Wv': _L1_xattn_in['Wv'], 'L1_xattn_bv': _L1_xattn_in['bv'], 'L1_xattn_W1': _L1_xattn_in['W1'], 'L1_xattn_b1': _L1_xattn_in['b1'], 'L1_xattn_W2': _L1_xattn_in['W2'], 'L1_xattn_b2': _L1_xattn_in['b2'], 'L1_ffn_gate_w': _L1_ffn_in['gate_w'], 'L1_ffn_w13_weight': _L1_ffn_in['w13_weight'], 'L1_ffn_w2_weight': _L1_ffn_in['w2_weight']}

def reference(x, ctx_768, L0_xattn_ln1_g, L0_xattn_ln1_b, L0_xattn_ln2_g, L0_xattn_ln2_b, L0_xattn_Wq, L0_xattn_bq, L0_xattn_Wk, L0_xattn_bk, L0_xattn_Wv, L0_xattn_bv, L0_xattn_Wo, L0_xattn_bo, L0_ffn_slot_init, L0_ffn_slot_scale, L0_ffn_w1, L0_ffn_b1, L0_ffn_w2, L0_ffn_b2, L0_ffn_gru_wih, L0_ffn_gru_whh, L0_ffn_gru_bih, L0_ffn_gru_bhh, L0_ffn_wv, L0_ffn_bv, L0_ffn_wo, L0_ffn_bo, L0_ffn_tau, L1_xattn_Wq, L1_xattn_bq, L1_xattn_Wk, L1_xattn_bk, L1_xattn_Wv, L1_xattn_bv, L1_xattn_W1, L1_xattn_b1, L1_xattn_W2, L1_xattn_b2, L1_ffn_gate_w, L1_ffn_w13_weight, L1_ffn_w2_weight):
    import jax
    import jax.numpy as jnp

    def _L0_xattn_ref(modality1, modality2, ln1_g, ln1_b, ln2_g, ln2_b, Wq, bq, Wk, bk, Wv, bv, Wo, bo):
        import jax, jax.numpy as jnp
        import numpy as np
        EPS = 1e-05

        def layernorm(x, g, b):
            mu = jnp.mean(x, axis=-1, keepdims=True)
            var = jnp.mean(jnp.square(x - mu), axis=-1, keepdims=True)
            return (x - mu) * jax.lax.rsqrt(var + EPS) * g + b
        E = Wq.shape[1]
        scaling = E ** (-0.5)
        x1 = layernorm(modality1, ln1_g, ln1_b)
        x2 = layernorm(modality2, ln2_g, ln2_b)
        q = x1 @ Wq + bq
        k = x2 @ Wk + bk
        v = x2 @ Wv + bv
        scores = jnp.einsum('bqe,bke->bqk', q, k) * scaling
        attn = jax.nn.softmax(scores, axis=-1)
        ctx = jnp.einsum('bqk,bke->bqe', attn, v)
        return ctx @ Wo + bo

    def _L0_ffn_ref(x, slot_init, slot_scale, w1, b1, w2, b2, gru_wih, gru_whh, gru_bih, gru_bhh, wv, bv, wo, bo, tau):
        import jax, jax.numpy as jnp
        import numpy as np
        D_MODEL = 256
        NUM_SLOTS = 64
        TOP_K = 8
        B, T = (4, 1024)

        def _forward(x, slot_init, slot_scale, w1, b1, w2, b2, gru_wih, gru_whh, gru_bih, gru_bhh, wv, bv, wo, bo, tau):
            Bn, Tn, D = x.shape
            Sn = slot_init.shape[0]
            S = jnp.broadcast_to((slot_init * slot_scale)[None], (Bn, Sn, D)).astype(x.dtype)
            slot_mean = S.mean(axis=1, keepdims=True)
            ctx = jnp.concatenate([x, jnp.broadcast_to(slot_mean, x.shape)], axis=-1)
            h = jax.nn.gelu(ctx @ w1.T + b1, approximate=False)
            route_logits = (h @ w2.T + b2) / (jnp.abs(tau) + 0.1)
            topk_vals, topk_idx = jax.lax.top_k(route_logits, TOP_K)
            topk_w = jax.nn.softmax(topk_vals, axis=-1)
            alpha = jnp.sum(topk_w[..., None] * jax.nn.one_hot(topk_idx, Sn, dtype=x.dtype), axis=-2)
            slot_input = jnp.einsum('bts,btd->bsd', alpha, x)
            slot_wsum = alpha.sum(axis=1) + 1e-08
            gi = (slot_input / slot_wsum[..., None]).reshape(Bn * Sn, D)
            hs = S.reshape(Bn * Sn, D)
            gx = gi @ gru_wih.T + gru_bih
            gh = hs @ gru_whh.T + gru_bhh
            xr, xz, xn = jnp.split(gx, 3, axis=-1)
            hr, hz, hn = jnp.split(gh, 3, axis=-1)
            r = jax.nn.sigmoid(xr + hr)
            z = jax.nn.sigmoid(xz + hz)
            n = jnp.tanh(xn + r * hn)
            h_new = (1.0 - z) * n + z * hs
            S_new = h_new.reshape(Bn, Sn, D)
            slot_values = S_new @ wv.T + bv
            out = jnp.einsum('bts,bsd->btd', alpha, slot_values)
            return out @ wo.T + bo
        return _forward(x, slot_init, slot_scale, w1, b1, w2, b2, gru_wih, gru_whh, gru_bih, gru_bhh, wv, bv, wo, bo, tau)

    def _L1_xattn_ref(x, y, Wq, bq, Wk, bk, Wv, bv, W1, b1, W2, b2):
        import jax, jax.numpy as jnp
        import numpy as np
        IMAGE_DIM = 256
        TEXT_DIM = 192
        NUM_HEADS = 16
        HEAD_DIM = IMAGE_DIM // NUM_HEADS
        B, N, _ = x.shape
        M = y.shape[1]
        q = (x @ Wq + bq).reshape(B, N, NUM_HEADS, HEAD_DIM)
        k = (y @ Wk + bk).reshape(B, M, NUM_HEADS, HEAD_DIM)
        v = (y @ Wv + bv).reshape(B, M, NUM_HEADS, HEAD_DIM)
        scale = 1.0 / np.sqrt(HEAD_DIM)
        scores = jnp.einsum('bnhd,bmhd->bhnm', q, k) * scale
        attn = jax.nn.softmax(scores, axis=-1)
        out = jnp.einsum('bhnm,bmhd->bnhd', attn, v).reshape(B, N, IMAGE_DIM)
        h = jax.nn.relu(out @ W1 + b1)
        return h @ W2 + b2

    def _L1_ffn_ref(hidden_states, gate_w, w13_weight, w2_weight):
        import jax, jax.numpy as jnp
        import numpy as np
        N_EXPERTS = 8
        N_GROUP = 4
        TOPK_GROUP = 2
        TOP_K = 2
        HIDDEN = 256
        INTER = 512
        B, S = (1, 256)

        def _grouped_topk(scores):
            T, E = scores.shape
            per_group = E // N_GROUP
            group_scores = scores.reshape(T, N_GROUP, per_group).max(-1)
            _, gidx = jax.lax.top_k(group_scores, TOPK_GROUP)
            gmask = jnp.zeros((T, N_GROUP), scores.dtype).at[jnp.arange(T)[:, None], gidx].set(1.0)
            smask = jnp.repeat(gmask, per_group, axis=1)
            masked = jnp.where(smask > 0, scores, 0.0)
            topk_w, topk_ids = jax.lax.top_k(masked, TOP_K)
            topk_w = topk_w / topk_w.sum(-1, keepdims=True)
            return (topk_ids, topk_w)
        Bm, Sm, H = hidden_states.shape
        x = hidden_states.reshape(-1, H)
        T = x.shape[0]
        scores = jax.nn.softmax(x @ gate_w.T, axis=-1)
        topk_ids, topk_w = _grouped_topk(scores)
        combine = jnp.zeros((T, N_EXPERTS), x.dtype).at[jnp.arange(T)[:, None], topk_ids].add(topk_w)
        gu = jnp.einsum('th,eih->tei', x, w13_weight)
        gate, up = (gu[..., :INTER], gu[..., INTER:])
        act = jax.nn.silu(gate) * up
        act = act * combine[:, :, None]
        out = jnp.einsum('tei,ehi->th', act, w2_weight)
        return out.reshape(Bm, Sm, H)
    x = x + _L0_xattn_ref(_layernorm(x, axis=-1), ctx_768, L0_xattn_ln1_g, L0_xattn_ln1_b, L0_xattn_ln2_g, L0_xattn_ln2_b, L0_xattn_Wq, L0_xattn_bq, L0_xattn_Wk, L0_xattn_bk, L0_xattn_Wv, L0_xattn_bv, L0_xattn_Wo, L0_xattn_bo)
    x = x + _L0_ffn_ref(_layernorm(x, axis=-1), L0_ffn_slot_init, L0_ffn_slot_scale, L0_ffn_w1, L0_ffn_b1, L0_ffn_w2, L0_ffn_b2, L0_ffn_gru_wih, L0_ffn_gru_whh, L0_ffn_gru_bih, L0_ffn_gru_bhh, L0_ffn_wv, L0_ffn_bv, L0_ffn_wo, L0_ffn_bo, L0_ffn_tau)
    x = x + _L1_xattn_ref(_layernorm(x, axis=-1), ctx_768, L1_xattn_Wq, L1_xattn_bq, L1_xattn_Wk, L1_xattn_bk, L1_xattn_Wv, L1_xattn_bv, L1_xattn_W1, L1_xattn_b1, L1_xattn_W2, L1_xattn_b2)
    x = x + _L1_ffn_ref(_layernorm(x, axis=-1), L1_ffn_gate_w, L1_ffn_w13_weight, L1_ffn_w2_weight)
    return x

_drawn_inputs = setup_inputs


def setup_inputs(seed=0):
    import zlib

    import numpy as np

    out = dict(_drawn_inputs(seed))
    spreads = {'L0_xattn_ln1_g': (1.0, 0.2),
     'L0_xattn_ln1_b': (0.0, 0.385),
     'L0_xattn_ln2_g': (1.0, 0.2),
     'L0_xattn_ln2_b': (0.0, 0.1),
     'L0_ffn_slot_scale': (1.0, 0.6),
     'L0_ffn_b1': (0.0, 0.483),
     'L0_ffn_b2': (0.0, 0.425),
     'L0_ffn_gru_bih': (0.0, 0.1),
     'L0_ffn_gru_bhh': (0.0, 0.451),
     'L0_ffn_bv': (0.0, 0.1),
     'L0_ffn_bo': (0.0, 0.1)}
    factors = {'L0_xattn_bq': 8.0,
     'L0_xattn_bk': 8.0,
     'L0_xattn_bv': 6.303,
     'L0_xattn_bo': 5.743,
     'L0_ffn_slot_init': 3.094,
     'L0_ffn_gru_whh': 7.542,
     'L1_xattn_bq': 7.514,
     'L1_xattn_bk': 8.0,
     'L1_ffn_gate_w': 4.861,
     'L1_ffn_w13_weight': 4.167,
     'L1_ffn_w2_weight': 4.177}
    for name, (base, spread) in spreads.items():
        noise = np.random.default_rng([zlib.crc32(name.encode()), seed]).standard_normal(out[name].shape)
        drawn = base * np.exp(spread * noise) if base else spread * noise
        out[name] = jnp.asarray(drawn.astype(out[name].dtype))
    for name, factor in factors.items():
        out[name] = (out[name] * factor).astype(out[name].dtype)
    return out
```

```python
from contextlib import ExitStack

import numpy as np
import concourse.bass as bass
from concourse import mybir

F32 = mybir.dt.float32
ALU = mybir.AluOpType
ACT = mybir.ActivationFunctionType
AXX = mybir.AxisListType.X

P = 128
B, S, D = 16, 128, 256
DC = 192
KD = D // P
GB = 4
GT = GB * S
NG = B // GB
PAIR = 2
NSLOT, TOPK = 64, 8
NH, HD = 16, 16
HT8 = P // HD
H1 = 2 * D
NE, INTER = 8, 512
NGRP, NPICK = 4, 2
NT = B * S * NPICK // P + NE - 1
EPS = 1e-5
NEG = -3.0e38


def columns(parts):
    at, out = 0, {}
    for name, n in parts:
        out[name] = (at, n)
        at += n
    return out, at


KEEP, KEEP_N = columns([
    ("ident", P), ("ones", P), ("ones_half", 2 * 32), ("head_mask", HT8), ("half_mask", 2),
    ("w1", 4 * P), ("w2", NSLOT), ("wih", KD * 3 * D), ("aWq", KD * D), ("aWk", KD * D), ("aWv", KD * D),
    ("aW1", KD * H1), ("aW2", H1 // P * D), ("gate", KD * NE),
    ("ln1_g", KD), ("ln1_b", KD), ("ln2_g", KD), ("ln2_b", KD), ("bq", KD), ("bv", KD),
    ("upper", P), ("before_group", NGRP * NGRP), ("before_expert", NE * NE), ("tile_start", B), ("tile_no", NT),
    ("b1", 1), ("bih", 6), ("bhh", 6), ("fbv", KD), ("abq", KD), ("abk", KD), ("ab1", H1 // P),
])
FOLD, FOLD_N = columns([
    ("WqT", KD * D), ("WkT", KD * D), ("Wq", KD * D), ("Wo", KD * D), ("WvT", KD * D), ("Wv", KD * D),
    ("whh", KD * 3 * D), ("fwv", KD * D), ("fwoT", KD * D), ("slots", KD * NSLOT),
])
ROWS, ROWS_N = columns([
    ("bo", D), ("slot_scale", NSLOT), ("b2", NSLOT), ("tau", 1), ("fbo", D), ("abv", D), ("ab2", D),
])


def build(nc, x_d, ctx_d, ctxT_d, keep_d, fold_d, rows_d, experts_d, x3_d, xh_d, sent_d, y_d, out_d):
    with ExitStack() as stack:
        def sb(name, shape, dt=F32):
            return stack.enter_context(nc.sbuf_tensor(name, shape, dt))

        def sem(name):
            return stack.enter_context(nc.semaphore(name))

        ps = stack.enter_context(nc.psum_tensor("ps", [P, 8, 512], F32))

        EXP_N = KD * 2 * INTER + INTER // P * D
        experts = sb("experts", [P, NE * EXP_N])
        carve_at = [NE // 2 * EXP_N]

        def carve(n):
            at = carve_at[0]
            carve_at[0] += n
            assert carve_at[0] <= NE * EXP_N
            return experts[:, at:at + n]

        keep = sb("keep", [P, KEEP_N])
        rows = sb("rows", [P, ROWS_N])
        ring = sb("ring", [P, 6 * 1024])

        def kept(name, t=1):
            at, n = KEEP[name]
            v = keep[:, at:at + n]
            return v.rearrange("p (t n) -> p t n", t=t) if t > 1 else v

        def fold(name, t=KD):
            at, n = FOLD[name]
            return ring[:, at:at + n].rearrange("p (t n) -> p t n", t=t)

        def row(name):
            at, n = ROWS[name]
            return rows[:, at:at + n]

        assert FOLD_N <= 6 * 1024
        ident, ones = kept("ident"), kept("ones")

        qk = sb("qk", [P, KD, D])
        vo = sb("vo", [P, KD, D])
        vo_row = sb("vo_row", [P, D])
        q_col = sb("q_col", [P, KD])
        u_col = sb("u_col", [P, KD])
        w_col = sb("w_col", [P, KD])
        spread = sb("spread", [P, 2 * KD, P])
        slots = sb("slots", [P, KD, NSLOT])
        slot_mean = sb("slot_mean", [P, KD])
        b1_col = sb("b1_col", [P, 1])
        inv_tau = sb("inv_tau", [P, 1])
        b_rz = sb("b_rz", [P, 6])
        gh = sb("gh", [P, 6, NSLOT])
        fvo = sb("fvo", [P, KD, D])
        fvo_row = sb("fvo_row", [P, D])

        ab = [carve(2048) for _ in range(PAIR)]
        a, b = [v[:, 0:1024] for v in ab], [v[:, 1024:2048] for v in ab]
        XT, c, d, e = ([carve(1024) for _ in range(PAIR)] for _ in range(4))
        X = [sb(f"X{j}", [P, GB, D]) for j in range(PAIR)]
        XH = [sb(f"XH{j}", [P, GB, D]) for j in range(PAIR)]
        f = [sb(f"f{j}", [P, 1024]) for j in range(PAIR)]
        V1 = [sb(f"V1{j}", [P, GB, 2, D]) for j in range(PAIR)]

        def two(buf, t):
            return [v.rearrange("p (t n) -> p t n", t=t) for v in buf]

        xT = two(XT, KD)
        C = [v[:, 0:GB * DC].rearrange("p (t n) -> p t n", t=GB) for v in a]
        CH, CT, Q, V = two(b, GB), two(c, KD), two(d, KD), two(e, GB)
        PR = [v[:, 0:512].rearrange("p (t n) -> p t n", t=GB) for v in f]
        PT = [v[:, 512:1024].rearrange("p (t n) -> p t n", t=GB) for v in f]
        HT = [v[:, 0:512] for v in f]
        LG, LK, EX, MK = ([v[:, 256 * n:256 * n + 256].rearrange("p (t n) -> p t n", t=GB) for v in a] for n in range(4))
        AL = [v[:, 0:256].rearrange("p (t n) -> p t n", t=GB) for v in b]
        RW = [v[:, 256:512] for v in b]
        AT = [v[:, 512:1024].rearrange("p (h o n) -> p h o n", h=2, o=2) for v in b]
        GI = [v[:, 0:512].rearrange("p (k n) -> p k n", k=KD) for v in c]
        NN = [v[:, 512:1024].rearrange("p (k n) -> p k n", k=KD) for v in c]
        RZ = [v.rearrange("p (g n) -> p g n", g=2) for v in d]
        DF = [v[:, 0:512].rearrange("p (k n) -> p k n", k=KD) for v in e]
        SN = [v[:, 512:1024].rearrange("p (k n) -> p k n", k=KD) for v in e]
        SV = [v[:, 512:1024].rearrange("p (h n) -> p h n", h=2) for v in f]
        YT, KT, Q1, OT = two(c, KD), two(a, KD), two(d, KD), two(e, KD)
        HF = two(ab, H1 // P)
        KB = [ring[:, 1024 * n:1024 * n + 1024].rearrange("p (h n) -> p h n", h=HT8) for n in range(2)]
        PP = [ring[:, 1024 * n:1024 * n + 1024].rearrange("p (h n) -> p h n", h=HT8) for n in range(2, 4)]
        PQ = [ring[:, 1024 * n:1024 * n + 1024].rearrange("p (h n) -> p h n", h=HT8) for n in range(4, 6)]

        stat = [sb(f"stat{j}", [P, GB, 6]) for j in range(PAIR)]
        norms = ("xh", "ch", "xh2", "xh3", "xh4")
        mv = {m: [sb(f"mv_{m}{j}", [P, GB, 2]) for j in range(PAIR)] for m in norms}
        var = {m: [sb(f"var_{m}{j}", [P, GB]) for j in range(PAIR)] for m in norms}
        minus_half = sb("minus_half", [P, GB])
        rt = [sb(f"rt{j}", [P, GB]) for j in range(PAIR)]
        nm = [sb(f"nm{j}", [P, GB]) for j in range(PAIR)]
        sm = [sb(f"sm{j}", [P, GB]) for j in range(PAIR)]
        m8 = [sb(f"m8{j}", [P, GB, 8]) for j in range(PAIR)]
        mx = [sb(f"mx{n}", [P, HT8]) for n in range(2)]
        rc = [sb(f"rc{n}", [P, P]) for n in range(2)]
        gl = sb("gl", [P, B, NE])

        XA = ring[:, 0:B * D].rearrange("p (b n) -> p b n", b=B)
        cmp1, cmp2 = (V1[0][:, 2 * h:2 * h + 2, :, :].rearrange("p t o n -> p (t o n)") for h in range(2))
        spare = [V1[1][:, :, :, :].rearrange("p t o n -> p (t o n)")[:, 128 * n:128 * n + 128] for n in range(16)]
        prob, masked, first, second, picked, sums, sums2, total, place, work = (v.rearrange("p (b e) -> p b e", b=B) for v in spare[:10])
        g_top, r4, g_ok = (v[:, 0:B * NGRP].rearrange("p (b g) -> p b g", b=B) for v in spare[10:13])
        cols = spare[13]
        g_max, n_tiles, t_off, t_end, e_flt = cols[:, 0:B], cols[:, B:B + NE], cols[:, 24:32], cols[:, 32:40], cols[:, 40:40 + NT]
        pos = spare[14][:, 0:2 * B].rearrange("p (k b) -> p k b", k=2)
        w_sum = spare[14][:, 2 * B:3 * B]
        weight = sb("weight", [P, 2, B])
        pos_i = sb("pos_i", [P, 2, B], mybir.dt.int32)
        e_id = sb("e_id", [P, NT], mybir.dt.int32)
        zero = sb("zero", [P, D])
        at = KEEP["wih"][0]
        assert KEEP["aW2"][0] + KEEP["aW2"][1] - at >= 2 * (2 * D + 2 * INTER)
        XI = [keep[:, at + D * n:at + D * n + D] for n in range(2)]
        XIT = [keep[:, at + D * n:at + D * n + D].rearrange("p (k n) -> p k n", k=KD) for n in range(2, 4)]
        at += 4 * D
        HA = [keep[:, at + INTER * n:at + INTER * n + INTER] for n in range(2)]
        HAT = [keep[:, at + INTER * n:at + INTER * n + INTER].rearrange("p (k n) -> p k n", k=INTER // P) for n in range(2, 4)]
        YO = [f[0][:, D * n:D * n + D] for n in range(2)]
        got = [ring[:, 2 * D * n:2 * D * n + 2 * D] for n in range(12)]
        got += [V1[0][:, n, :, :].rearrange("p o n -> p (o n)") for n in range(4)]
        back = [(XH[0], 0), (XH[1], 0), (X[0], 0), (X[1], 0)]

        keep_in, fold_in, rows_in = sem("keep_in"), sem("fold_in"), sem("rows_in")
        x_in, c_in, y_in = ([sem(f"{t}{j}") for j in range(PAIR)] for t in ("x_in", "c_in", "y_in"))
        names = ("xh ch ch_pad xT_ps xT cT_ps cT q_ps q v_ps v s_ps nm p pT_ps pT o_ps "
                 "xh2 xT2_ps xT2 h_ps h lg_ps top ex al aT_ps aT si_ps gi gx_ps rz rz_act n_pre n_act sn sv_ps sv fo_ps "
                 "xh3 xb xT3_ps xT3 k_ps k v1_ps v1 q1_ps q1 f_ps f y_ps xh4 xT4_ps xT4 gl_ps "
                 "kb sc_ps sub exp pt_ps pt ot_ps ot")
        names += "".join(f" var_{m} rs_{m}" for m in norms)
        s = {n: sem("s_" + n) for n in names.split()}
        fold_ps, fold_ok = sem("fold_ps"), sem("fold_ok")
        v1_zero, half_set = sem("v1_zero"), sem("half_set")
        through = [sem(f"through{j}") for j in range(PAIR)]
        stored = [sem(f"stored{j}") for j in range(PAIR)]

        zero_set, sent_zero = sem("zero_set"), sem("sent_zero")
        early_in, late_in = ([sem(f"expert_in{n}") for n in range(h * NE // 2, (h + 1) * NE // 2)] for h in range(2))
        xa_in, rows_back = sem("xa_in"), sem("rows_back")
        g_diff, g_exp, picks, counted, routed = (sem(t) for t in ("g_diff", "g_exp", "picks", "counted", "routed"))
        rows_sent = sem("rows_sent")
        xi_in = [sem(f"xi_in{u}") for u in range(2)]
        y_out = [sem(f"y_out{u}") for u in range(2)]
        xt_ps, xt, gu_ps, silu, act_ok, ha_ps, ha, y_ps, y_ok = (
            sem("e_" + t) for t in ("xt_ps", "xt", "gu_ps", "silu", "act_ok", "ha_ps", "ha", "y_ps", "y_ok"))
        got_in = [sem(f"got_in{g}") for g in range(NG)]
        final, out_done = sem("final"), sem("out_done")

        x_g = x_d.rearrange("(g b) p d -> g p b d", b=GB)
        c_g = ctx_d.rearrange("(g b) p d -> g p b d", b=GB)
        o_g, x3_g, xh_g = (t.rearrange("(g b) p d -> g p b d", b=GB) for t in (out_d, x3_d, xh_d))
        sent_t, y_t = (t.rearrange("(t p) d -> t p d", p=P) for t in (sent_d, y_d))

        XT_PS, Y_PS = ps[:, 4, 0:D], [ps[:, 5 + u, 0:D] for u in range(2)]

        block = stack.enter_context(nc.Block())

        def bank(j, k):
            return ps[:, 4 * j + k, :]

        @block.sync
        def _(sp):
            sp.dma_start(ring[:, 0:FOLD_N], fold_d).then_inc(fold_in, 16)
            sp.dma_start(keep[:, :], keep_d).then_inc(keep_in, 16)
            sp.dma_start(rows[:, :], rows_d.partition_broadcast(P)).then_inc(rows_in, 16)
            for j in range(PAIR):
                sp.sem_inc(through[j], 1)
            with sp.Fori(0, NG // PAIR) as i:
                for j in range(PAIR):
                    n = PAIR * i + j
                    sp.wait_ge(through[j], i + 1)
                    sp.dma_start(X[j][:, :, :], x_g[n]).then_inc(x_in[j], 16)
                    sp.dma_start(C[j], c_g[n]).then_inc(c_in[j], 16)
                for j in range(PAIR):
                    n = PAIR * i + j
                    sp.wait_ge(s["sn"], n + 1)
                    sp.dma_start(YT[j], ctxT_d[n]).then_inc(y_in[j], 16)
                for j in range(PAIR):
                    n = PAIR * i + j
                    sp.wait_ge(s["xh4"], n + 1)
                    sp.dma_start(x3_g[n], X[j][:, :, :]).then_inc(stored[j], 16)
                    sp.dma_start(xh_g[n], XH[j][:, :, :]).then_inc(stored[j], 16)
            for j in range(PAIR):
                sp.wait_ge(through[j], 1 + NG // PAIR)
            sp.dma_start(XA, xh_d.rearrange("b p d -> p b d")).then_inc(xa_in, 16)
            for n in range(NE // 2):
                sp.dma_start(experts[:, (NE // 2 + n) * EXP_N:(NE // 2 + n + 1) * EXP_N], experts_d[NE // 2 + n]).then_inc(late_in[n], 16)
            for j in range(PAIR):
                sp.dma_start(XH[j][:, :, :], x3_g[j]).then_inc(rows_back, 16)
            sp.wait_ge(rows_sent, 16 * NPICK * B)
            for u in range(2):
                sp.dma_start(XI[u], sent_t[u]).then_inc(xi_in[u], 16)

            def step(t, u, more):
                if more:
                    sp.wait_ge(xt_ps, t + 1)
                    sp.dma_start(XI[u], sent_t[t + 2]).then_inc(xi_in[u], 16)
                sp.wait_ge(y_ok, t + 3)
                sp.dma_start(y_t[t], YO[u]).then_inc(y_out[u], 16)

            with sp.Fori(0, (NT - 3) // 2) as i:
                for u in range(2):
                    step(2 * i + u, u, True)
            for t in range(NT - 3, NT):
                step(t, t % 2, t + 2 < NT)
            for g in range(NG):
                sp.wait_ge(final, g + 1)
                sp.dma_start(o_g[g], back[g][0][:, :, :]).then_inc(out_done, 16)
            sp.wait_ge(out_done, 16 * NG)

        @block.gpsimd
        def _(pool):
            for j in range(PAIR):
                pool.memset(V1[j][:, :, :, :], 0.0).then_inc(v1_zero, 1)
            pool.memset(zero[:, :], 0.0).then_inc(zero_set, 1)
            pool.memset(minus_half[:, :], -0.5).then_inc(half_set, 1)
            pool.wait_ge(half_set, 1)

            def root(j, n, name):
                pool.wait_ge(s["var_" + name], n + 1)
                pool.tensor_tensor(var[name][j][:, :], var[name][j][:, :], minus_half[:, :], ALU.pow).then_inc(s["rs_" + name], 1)

            with pool.Fori(0, NG // PAIR) as i:
                for j in range(PAIR):
                    n = PAIR * i + j
                    root(j, n, "xh")
                    pool.memset(CH[j][:, :, DC:D], 0.0).then_inc(s["ch_pad"], 1)
                    root(j, n, "ch")
                for name in ("xh2", "xh3"):
                    for j in range(PAIR):
                        root(j, PAIR * i + j, name)
                for j in range(PAIR):
                    n = PAIR * i + j
                    pool.wait_ge(s["xh3"], n + 1)
                    pool.tensor_tensor(X[j][:, :, :], X[j][:, :, :],
                                       row("ab2").unsqueeze(1).broadcast_to([P, GB, D]), ALU.add).then_inc(s["xb"], 1)
                for j in range(PAIR):
                    n = PAIR * i + j
                    pool.wait_ge(s["k"], n + 1)
                    for u in range(2 * GB):
                        bb, t = u // 2, u % 2
                        unit = 2 * GB * n + u
                        if j or u >= 2:
                            pool.wait_ge(s["sc_ps"], unit - 1)
                        pool.tensor_tensor(KB[u % 2], KT[j][:, t, bb * S:(bb + 1) * S].unsqueeze(1).broadcast_to([P, HT8, S]),
                                           kept("head_mask").unsqueeze(2).broadcast_to([P, HT8, S]), ALU.mult).then_inc(s["kb"], 1)
                for j in range(PAIR):
                    root(j, PAIR * i + j, "xh4")
            pool.wait_ge(routed, 1)
            pool.wait_ge(xa_in, 16)
            pool.wait_ge(sent_zero, 16)
            for k in range(NPICK):
                for t in range(B):
                    pool.indirect_dma_start(out=sent_d, out_offset=bass.IndirectOffsetOnAxis(ap=pos_i[:, k, t:t + 1], axis=0),
                                            in_=XA[:, t, :], in_offset=None).then_inc(rows_sent, 16)
            pool.wait_ge(y_out[0], 16 + 16 * ((NT + 1) // 2))
            pool.wait_ge(y_out[1], 16 + 16 * (NT // 2))
            for t in range(B):
                for k in range(NPICK):
                    pool.indirect_dma_start(out=got[t][:, k * D:(k + 1) * D], out_offset=None, in_=y_d,
                                            in_offset=bass.IndirectOffsetOnAxis(ap=pos_i[:, k, t:t + 1], axis=0)).then_inc(got_in[t // GB], 16)

        @block.scalar
        def _(act):
            for u in range(2):
                act.sem_inc(y_out[u], 16)
            act.sem_inc(y_ok, 2)
            act.wait_ge(zero_set, 1)
            act.dma_start(sent_t.rearrange("t p d -> p t d"), zero[:, :].unsqueeze(1).broadcast_to([P, NT, D])).then_inc(sent_zero, 16)
            for n in range(NE // 2):
                act.dma_start(experts[:, n * EXP_N:(n + 1) * EXP_N], experts_d[n]).then_inc(early_in[n], 16)
            act.wait_ge(keep_in, 16)
            act.wait_ge(fold_ok, 1)
            with act.Fori(0, NG // PAIR) as i:
                for j in range(PAIR):
                    n = PAIR * i + j
                    act.wait_ge(s["xT_ps"], n + 1)
                    act.copy(xT[j], ps[:, 4 * j:4 * j + 2, :]).then_inc(s["xT"], 1)
                for j in range(PAIR):
                    n = PAIR * i + j
                    act.wait_ge(s["q_ps"], n + 1)
                    for t in range(KD):
                        ins = act.activation(Q[j][:, t, :], bank(j, t), ACT.Identity, bias=q_col[:, t:t + 1],
                                             scale=kept("ln2_g")[:, t:t + 1])
                    ins.then_inc(s["q"], 1)
                for j in range(PAIR):
                    n = PAIR * i + j
                    act.wait_ge(s["nm"], n + 1)
                    for t in range(GB):
                        ins = act.activation(PR[j][:, t, :], bank(j, 0)[:, t * S:(t + 1) * S], ACT.Exp, bias=nm[j][:, t:t + 1],
                                             scale=float(D) ** -0.5, accum_out=sm[j][:, t:t + 1])
                    ins.then_inc(s["p"], 1)
                for j in range(PAIR):
                    n = PAIR * i + j
                    act.wait_ge(s["pT_ps"], n + 1)
                    act.copy(PT[j], bank(j, 1).rearrange("p (t n) -> p t n", t=GB)).then_inc(s["pT"], 1)
                for j in range(PAIR):
                    n = PAIR * i + j
                    act.wait_ge(s["xT2_ps"], n + 1)
                    act.copy(xT[j], ps[:, 4 * j:4 * j + 2, :]).then_inc(s["xT2"], 1)
                for j in range(PAIR):
                    n = PAIR * i + j
                    act.wait_ge(s["h_ps"], n + 1)
                    act.activation(HT[j], bank(j, 2), ACT.Gelu, bias=b1_col[:, 0:1], scale=1.0).then_inc(s["h"], 1)
                for j in range(PAIR):
                    n = PAIR * i + j
                    act.wait_ge(s["top"], n + 1)
                    for t in range(GB):
                        ins = act.activation(EX[j][:, t, :], LG[j][:, t, :], ACT.Exp, bias=nm[j][:, t:t + 1], scale=inv_tau[:, 0:1])
                    ins.then_inc(s["ex"], 1)
                for j in range(PAIR):
                    n = PAIR * i + j
                    act.wait_ge(s["aT_ps"], n + 1)
                    for o in range(2):
                        ins = act.activation(AT[j][:, :, o, :], bank(j, 0)[:, 0:2 * P].rearrange("p (h n) -> p h n", h=2),
                                             ACT.Copy, scale=kept("half_mask")[:, o:o + 1])
                    ins.then_inc(s["aT"], 1)
                for j in range(PAIR):
                    n = PAIR * i + j
                    act.wait_ge(s["rz"], n + 1)
                    act.activation(RZ[j], RZ[j], ACT.Sigmoid).then_inc(s["rz_act"], 1)
                for j in range(PAIR):
                    n = PAIR * i + j
                    act.wait_ge(s["n_pre"], n + 1)
                    for t in range(KD):
                        ins = act.activation(NN[j][:, t, :], NN[j][:, t, :], ACT.Tanh, bias=kept("bih")[:, 4 + t:5 + t], scale=1.0)
                    ins.then_inc(s["n_act"], 1)
                for j in range(PAIR):
                    n = PAIR * i + j
                    act.wait_ge(s["xT3_ps"], n + 1)
                    act.copy(xT[j], ps[:, 4 * j:4 * j + 2, :]).then_inc(s["xT3"], 1)
                for j in range(PAIR):
                    n = PAIR * i + j
                    act.wait_ge(s["q1_ps"], n + 1)
                    for t in range(KD):
                        ins = act.activation(Q1[j][:, t, :], bank(j, t), ACT.Identity, bias=kept("abq")[:, t:t + 1], scale=1.0)
                    ins.then_inc(s["q1"], 1)
                for j in range(PAIR):
                    n = PAIR * i + j
                    for u in range(2 * GB):
                        unit = 2 * GB * n + u
                        act.wait_ge(s["sub"], unit + 1)
                        act.activation(PP[u % 2], PP[u % 2], ACT.Exp, scale=float(HD) ** -0.5).then_inc(s["exp"], 1)
                        act.wait_ge(s["pt_ps"], unit + 1)
                        if j or u >= 2:
                            act.wait_ge(s["ot_ps"], unit - 1)
                        act.copy(PQ[u % 2], ps[:, 2:4, :].rearrange("p t (h n) -> p (t h) n", h=4)).then_inc(s["pt"], 1)
                for j in range(PAIR):
                    n = PAIR * i + j
                    act.wait_ge(s["f_ps"], n + 1)
                    for m in range(H1 // P):
                        ins = act.activation(HF[j][:, m, :], bank(j, m), ACT.Relu, bias=kept("ab1")[:, m:m + 1], scale=1.0)
                    ins.then_inc(s["f"], 1)
                for j in range(PAIR):
                    n = PAIR * i + j
                    act.wait_ge(s["xT4_ps"], n + 1)
                    act.copy(xT[j], ps[:, 4 * j + 2:4 * j + 4, :]).then_inc(s["xT4"], 1)
            act.wait_ge(g_diff, 1)
            act.activation(prob, prob, ACT.Exp).then_inc(g_exp, 1)

            def head(t, u):
                act.wait_ge(xt_ps, t + 1)
                act.copy(XIT[u], XT_PS.rearrange("p (k n) -> p k n", k=KD)).then_inc(xt, 1)
                act.wait_ge(gu_ps, t + 1)
                act.activation(HA[u], ps[:, 2 * u, :], ACT.Silu).then_inc(silu, 1)

            def tail(t, u, m):
                act.wait_ge(y_ps, t + 1)
                act.wait_ge(y_out[u], 16 * (m + 1))
                act.copy(YO[u], Y_PS[u]).then_inc(y_ok, 1)

            head(0, 0)
            with act.Fori(0, (NT - 1) // 2) as i:
                for u in range(2):
                    head(2 * i + u + 1, 1 - u)
                    tail(2 * i + u, u, i)
            tail(NT - 1, 0, (NT - 1) // 2)

        @block.tensor
        def _(pe):
            def mm(out, pairs):
                for k, (w, m) in enumerate(pairs):
                    ins = pe.matmul(out, w, m, start=(k == 0), stop=(k == len(pairs) - 1))
                return ins

            def turn(out, t):
                return pe.transpose(out, t, ident)

            pe.wait_ge(fold_in, 16)
            pe.wait_ge(keep_in, 16)
            WqT, WkT, Wq, Wo, WvT, Wv = (fold(t) for t in ("WqT", "WkT", "Wq", "Wo", "WvT", "Wv"))
            w1 = kept("w1", 4)
            for m in range(KD):
                mm(ps[:, 0, m * D:(m + 1) * D], [(WqT[:, k, m * P:(m + 1) * P], WkT[:, k, :]) for k in range(KD)])
                mm(ps[:, 1, m * D:(m + 1) * D], [(WvT[:, k, m * P:(m + 1) * P], Wo[:, k, :]) for k in range(KD)])
                mm(ps[:, 2, m:m + 1], [(Wq[:, k, m * P:(m + 1) * P], kept("ln1_b")[:, k:k + 1]) for k in range(KD)])
                mm(ps[:, 2, 2 + m:3 + m], [(Wv[:, k, m * P:(m + 1) * P], kept("ln2_b")[:, k:k + 1]) for k in range(KD)])
                ins = mm(ps[:, 3, m * D:(m + 1) * D], [(fold("fwv")[:, k, m * P:(m + 1) * P], fold("fwoT")[:, k, :]) for k in range(KD)])
            ins.then_inc(fold_ps, 1)
            pe.wait_ge(fold_ok, 1)
            for m in range(KD):
                mm(ps[:, 4, m:m + 1], [(WkT[:, k, m * P:(m + 1) * P], u_col[:, k:k + 1]) for k in range(KD)])
            mm(ps[:, 4, 4:5], [(w1[:, 2 + k, :], slot_mean[:, k:k + 1]) for k in range(KD)])
            mm(ps[:, 5, 0:D], [(spread[:, k, :], Wo[:, k, :]) for k in range(KD)])
            mm(ps[:, 5, D:2 * D], [(spread[:, 2 + k, :], fold("fwoT")[:, k, :]) for k in range(KD)])
            for m in range(6):
                ins = mm(ps[:, 6, m * NSLOT:(m + 1) * NSLOT], [(fold("whh")[:, k, m * P:(m + 1) * P], slots[:, k, :]) for k in range(KD)])
            ins.then_inc(fold_ps, 1)
            pe.wait_ge(fold_ok, 2)
            with pe.Fori(0, NG // PAIR) as i:
                for j in range(PAIR):
                    n = PAIR * i + j
                    pe.wait_ge(s["xh"], n + 1)
                    for k in range(KD):
                        for t in range(GB):
                            ins = turn(bank(j, k)[:, t * S:(t + 1) * S], XH[j][:, t, k * P:(k + 1) * P])
                    ins.then_inc(s["xT_ps"], 1)
                for j in range(PAIR):
                    n = PAIR * i + j
                    pe.wait_ge(s["ch"], n + 1)
                    pe.wait_ge(s["ch_pad"], n + 1)
                    for k in range(KD):
                        for t in range(GB):
                            ins = turn(bank(j, 2 + k)[:, t * S:(t + 1) * S], CH[j][:, t, k * P:(k + 1) * P])
                    ins.then_inc(s["cT_ps"], 1)
                for j in range(PAIR):
                    n = PAIR * i + j
                    pe.wait_ge(s["xT"], n + 1)
                    for m in range(KD):
                        ins = mm(bank(j, m), [(qk[:, k, m * P:(m + 1) * P], xT[j][:, k, :]) for k in range(KD)])
                    ins.then_inc(s["q_ps"], 1)
                for j in range(PAIR):
                    n = PAIR * i + j
                    pe.wait_ge(s["cT"], n + 1)
                    for t in range(GB):
                        ins = mm(bank(j, 2 + t // 2)[:, t % 2 * D:(t % 2 + 1) * D],
                                 [(CT[j][:, k, t * S:(t + 1) * S], vo[:, k, :]) for k in range(KD)])
                    ins.then_inc(s["v_ps"], 1)
                for j in range(PAIR):
                    n = PAIR * i + j
                    pe.wait_ge(s["q"], n + 1)
                    for t in range(GB):
                        tok = slice(t * S, (t + 1) * S)
                        ins = mm(bank(j, 0)[:, tok], [(Q[j][:, k, tok], CT[j][:, k, tok]) for k in range(KD)])
                    ins.then_inc(s["s_ps"], 1)
                for j in range(PAIR):
                    n = PAIR * i + j
                    pe.wait_ge(s["p"], n + 1)
                    for t in range(GB):
                        ins = turn(bank(j, 1)[:, t * S:(t + 1) * S], PR[j][:, t, :])
                    ins.then_inc(s["pT_ps"], 1)
                for j in range(PAIR):
                    n = PAIR * i + j
                    pe.wait_ge(s["pT"], n + 1)
                    pe.wait_ge(s["v"], n + 1)
                    for t in range(GB):
                        ins = mm(bank(j, 2 + t // 2)[:, t % 2 * D:(t % 2 + 1) * D], [(PT[j][:, t, :], V[j][:, t, :])])
                    ins.then_inc(s["o_ps"], 1)
                for j in range(PAIR):
                    n = PAIR * i + j
                    pe.wait_ge(s["xh2"], n + 1)
                    for k in range(KD):
                        for t in range(GB):
                            ins = turn(bank(j, k)[:, t * S:(t + 1) * S], XH[j][:, t, k * P:(k + 1) * P])
                    ins.then_inc(s["xT2_ps"], 1)
                for j in range(PAIR):
                    n = PAIR * i + j
                    pe.wait_ge(s["xT2"], n + 1)
                    mm(bank(j, 2), [(w1[:, k, :], xT[j][:, k, :]) for k in range(KD)]).then_inc(s["h_ps"], 1)
                for j in range(PAIR):
                    n = PAIR * i + j
                    pe.wait_ge(s["h"], n + 1)
                    for t in range(GB):
                        ins = mm(bank(j, 3)[:, t * NSLOT:(t + 1) * NSLOT], [(HT[j][:, t * S:(t + 1) * S], kept("w2"))])
                    ins.then_inc(s["lg_ps"], 1)
                for j in range(PAIR):
                    n = PAIR * i + j
                    pe.wait_ge(s["al"], n + 1)
                    for h in range(2):
                        ins = turn(bank(j, 0)[:, h * P:(h + 1) * P], AL[j][:, 2 * h:2 * h + 2, :].rearrange("p t n -> p (t n)"))
                    ins.then_inc(s["aT_ps"], 1)
                    for k in range(KD):
                        for t in range(GB):
                            at = (k * GB + t) * NSLOT
                            mm(bank(j, 1)[:, at:at + NSLOT], [(XH[j][:, t, k * P:(k + 1) * P], AL[j][:, t, :])])
                    mm(bank(j, 2)[:, 0:GB * NSLOT], [(ones, AL[j].rearrange("p t n -> p (t n)"))]).then_inc(s["si_ps"], 1)
                for j in range(PAIR):
                    n = PAIR * i + j
                    pe.wait_ge(s["aT"], n + 1)
                    pe.wait_ge(s["gi"], n + 1)
                    for g, o in enumerate((0, 3, 1)):
                        for m in range(KD):
                            at = (g * KD + m) * P
                            ins = mm(bank(j, o)[:, m * 256:(m + 1) * 256],
                                     [(kept("wih", KD)[:, k, at:at + P], GI[j][:, k, :]) for k in range(KD)])
                    ins.then_inc(s["gx_ps"], 1)
                for j in range(PAIR):
                    n = PAIR * i + j
                    pe.wait_ge(s["sn"], n + 1)
                    for h in range(2):
                        ins = mm(bank(j, 2)[:, h * D:(h + 1) * D], [(SN[j][:, k, h * P:(h + 1) * P], fvo[:, k, :]) for k in range(KD)])
                    ins.then_inc(s["sv_ps"], 1)
                for j in range(PAIR):
                    n = PAIR * i + j
                    pe.wait_ge(s["sv"], n + 1)
                    for t in range(GB):
                        ins = mm(bank(j, 0 if t < 2 else 1)[:, t % 2 * D:(t % 2 + 1) * D], [(AT[j][:, t // 2, t % 2, :], SV[j][:, t // 2, :])])
                    ins.then_inc(s["fo_ps"], 1)
                for j in range(PAIR):
                    n = PAIR * i + j
                    pe.wait_ge(y_in[j], 16 * (i + 1))
                    for m in range(KD):
                        ins = mm(bank(j, 2 + m), [(kept("aWk", KD)[:, k, m * P:(m + 1) * P], YT[j][:, k, :]) for k in range(KD)])
                    ins.then_inc(s["k_ps"], 1)
                for j in range(PAIR):
                    n = PAIR * i + j
                    pe.wait_ge(s["k"], n + 1)
                    for t in range(GB):
                        ins = mm(bank(j, 2 + t // 2)[:, t % 2 * D:(t % 2 + 1) * D],
                                 [(YT[j][:, k, t * S:(t + 1) * S], kept("aWv", KD)[:, k, :]) for k in range(KD)])
                    ins.then_inc(s["v1_ps"], 1)
                for j in range(PAIR):
                    n = PAIR * i + j
                    pe.wait_ge(s["xh3"], n + 1)
                    for k in range(KD):
                        for t in range(GB):
                            ins = turn(bank(j, k)[:, t * S:(t + 1) * S], XH[j][:, t, k * P:(k + 1) * P])
                    ins.then_inc(s["xT3_ps"], 1)
                for j in range(PAIR):
                    n = PAIR * i + j
                    pe.wait_ge(s["xT3"], n + 1)
                    for m in range(KD):
                        ins = mm(bank(j, m), [(kept("aWq", KD)[:, k, m * P:(m + 1) * P], xT[j][:, k, :]) for k in range(KD)])
                    ins.then_inc(s["q1_ps"], 1)
                pe.wait_ge(s["q1"], PAIR * i + PAIR)
                pe.wait_ge(s["v1"], PAIR * i + PAIR)
                for j in range(PAIR):
                    n = PAIR * i + j

                    def score(u):
                        unit = 2 * GB * n + u
                        bb, t = u // 2, u % 2
                        pe.wait_ge(s["kb"], unit + 1)
                        if j or u >= 2:
                            pe.wait_ge(s["sub"], unit - 1)
                        for h in range(2):
                            ins = mm(ps[:, 4 * (u % 2) + h, :], [(Q1[j][:, t, bb * S:(bb + 1) * S],
                                                                 KB[u % 2][:, 4 * h:4 * h + 4, :].rearrange("p h n -> p (h n)"))])
                        ins.then_inc(s["sc_ps"], 1)

                    def attend(u):
                        unit = 2 * GB * n + u
                        bb, t = u // 2, u % 2
                        pe.wait_ge(s["exp"], unit + 1)
                        if j or u:
                            pe.wait_ge(s["pt"], unit)
                        for h in range(HT8):
                            ins = turn(ps[:, 2 + h // 4, h % 4 * S:(h % 4 + 1) * S], PP[u % 2][:, h, :])
                        ins.then_inc(s["pt_ps"], 1)

                    def gather(u):
                        unit = 2 * GB * n + u
                        bb, t = u // 2, u % 2
                        pe.wait_ge(s["pt"], unit + 1)
                        if j or u >= 2:
                            pe.wait_ge(s["ot"], unit - 1)
                        for st in range(4):
                            out = ps[32 * st:32 * st + 32, 6 + u % 2, :]
                            mm(out[:, 0:S], [(V1[j][:, bb, o, 32 * (4 * t + st):32 * (4 * t + st) + 32], PQ[u % 2][:, 2 * st + o, :]) for o in range(2)])
                            ins = mm(out[:, S:2 * S], [(kept("ones_half", 2)[:, o, :], PQ[u % 2][:, 2 * st + o, :]) for o in range(2)])
                        ins.then_inc(s["ot_ps"], 1)

                    score(0)
                    for u in range(2 * GB):
                        if u + 1 < 2 * GB:
                            score(u + 1)
                        attend(u)
                        if u:
                            gather(u - 1)
                    gather(2 * GB - 1)
                pe.wait_ge(s["ot"], 2 * GB * PAIR * (i + 1))
                for j in range(PAIR):
                    n = PAIR * i + j
                    for m in range(H1 // P):
                        ins = mm(bank(j, m), [(kept("aW1", KD)[:, k, m * P:(m + 1) * P], OT[j][:, k, :]) for k in range(KD)])
                    ins.then_inc(s["f_ps"], 1)
                for j in range(PAIR):
                    n = PAIR * i + j
                    pe.wait_ge(s["f"], n + 1)
                    for t in range(GB):
                        ins = mm(bank(j, t // 2)[:, t % 2 * D:(t % 2 + 1) * D],
                                 [(HF[j][:, k, t * S:(t + 1) * S], kept("aW2", H1 // P)[:, k, :]) for k in range(H1 // P)])
                    ins.then_inc(s["y_ps"], 1)
                for j in range(PAIR):
                    n = PAIR * i + j
                    pe.wait_ge(s["xh4"], n + 1)
                    for k in range(KD):
                        for t in range(GB):
                            ins = turn(bank(j, 2 + k)[:, t * S:(t + 1) * S], XH[j][:, t, k * P:(k + 1) * P])
                    ins.then_inc(s["xT4_ps"], 1)
                for j in range(PAIR):
                    n = PAIR * i + j
                    pe.wait_ge(s["xT4"], n + 1)
                    for t in range(GB):
                        ins = mm(bank(j, 0)[:, t * NE:(t + 1) * NE], [(xT[j][:, k, t * S:(t + 1) * S], kept("gate", KD)[:, k, :]) for k in range(KD)])
                    ins.then_inc(s["gl_ps"], 1)
            pe.wait_ge(picks, 1)
            flat = picked.rearrange("p b e -> p (b e)")
            mm(ps[:, 0, 0:B * NE], [(kept("upper"), flat)])
            mm(ps[:, 1, 0:B * NE], [(ones, flat)]).then_inc(counted, 1)
            for n in range(NE // 2):
                pe.wait_ge(early_in[n], 16)
                pe.wait_ge(late_in[n], 16)
            pe.wait_ge(routed, 1)

            def head(t, u, m):
                pe.wait_ge(xi_in[u], 16 * (m + 1))
                if not (isinstance(t, int) and t == 0):
                    pe.wait_ge(xt, t)
                for k in range(KD):
                    ins = turn(XT_PS[:, k * P:(k + 1) * P], XI[u][:, k * P:(k + 1) * P])
                ins.then_inc(xt_ps, 1)
                at = pe.value_load(e_id[0:1, bass.ds(t, 1)], min_val=0, max_val=NE - 1) * EXP_N
                pe.wait_ge(xt, t + 1)
                for g in range(2):
                    for k in range(KD):
                        ins = pe.matmul(ps[:, 2 * u + g, :], XIT[u][:, k, :], experts[:, bass.ds(at + (2 * k + g) * INTER, INTER)],
                                        start=(k == 0), stop=(k == KD - 1))
                ins.then_inc(gu_ps, 1)
                return at

            def tail(t, u):
                pe.wait_ge(act_ok, t + 1)
                for k in range(INTER // P):
                    ins = turn(ps[:, 7, k * P:(k + 1) * P], HA[u][:, k * P:(k + 1) * P])
                ins.then_inc(ha_ps, 1)
                at = pe.value_load(e_id[0:1, bass.ds(t, 1)], min_val=0, max_val=NE - 1) * EXP_N
                pe.wait_ge(y_ok, t + 1)
                pe.wait_ge(ha, t + 1)
                for k in range(INTER // P):
                    ins = pe.matmul(Y_PS[u], HAT[u][:, k, :], experts[:, bass.ds(at + 2 * KD * INTER + k * D, D)],
                                    start=(k == 0), stop=(k == INTER // P - 1))
                ins.then_inc(y_ps, 1)

            head(0, 0, 0)
            with pe.Fori(0, (NT - 1) // 2) as i:
                for u in range(2):
                    head(2 * i + u + 1, 1 - u, i + u)
                    tail(2 * i + u, u)
            tail(NT - 1, 0)

        @block.vector
        def _(dve):
            settle = dve.drain

            def spread_of(j, src, width, name, scale=1.0, eps=EPS):
                for t in range(GB):
                    dve.bn_stats(stat[j][:, t, :], src[:, t, 0:width])
                settle()
                for t in range(GB):
                    dve.bn_aggr(mv[name][j][:, t, :], stat[j][:, t, :])
                settle()
                dve.tensor_scalar(var[name][j][:, :], mv[name][j][:, :, 1], scale, eps, ALU.mult, ALU.add).then_inc(s["var_" + name], 1)

            def norm(j, n, src, out, width, name):
                dve.wait_ge(s["rs_" + name], n + 1)
                for t in range(GB):
                    ins = dve.tensor_scalar(out[:, t, 0:width], src[:, t, 0:width], mv[name][j][:, t, 0:1], var[name][j][:, t:t + 1],
                                            ALU.subtract, ALU.mult)
                ins.then_inc(s[name], 1)

            dve.wait_ge(rows_in, 16)
            dve.wait_ge(fold_in, 16)
            dve.wait_ge(keep_in, 16)
            dve.tensor_tensor(slots[:, :, :], fold("slots"), row("slot_scale").unsqueeze(1).broadcast_to([P, KD, NSLOT]), ALU.mult)
            dve.tensor_scalar(inv_tau[:, :], row("tau"), -1.0, None, ALU.mult)
            dve.tensor_copy(b_rz[:, :], kept("bhh"))
            settle()
            dve.tensor_tensor(inv_tau[:, :], inv_tau[:, :], row("tau"), ALU.max)
            settle()
            dve.tensor_scalar(inv_tau[:, :], inv_tau[:, :], 0.1, None, ALU.add)
            settle()
            dve.tensor_reduce(slot_mean[:, :], slots[:, :, :], AXX, ALU.add)
            dve.reciprocal(inv_tau[:, :], inv_tau[:, :])
            dve.tensor_tensor(b_rz[:, 0:4], b_rz[:, 0:4], kept("bih")[:, 0:4], ALU.add)
            settle()
            dve.tensor_scalar(slot_mean[:, :], slot_mean[:, :], 1.0 / NSLOT, None, ALU.mult)
            dve.wait_ge(fold_ps, 1)
            for m in range(KD):
                dve.tensor_scalar(qk[:, m, :], ps[:, 0, m * D:(m + 1) * D], kept("ln1_g")[:, m:m + 1], None, ALU.mult)
                dve.tensor_scalar(vo[:, m, :], ps[:, 1, m * D:(m + 1) * D], kept("ln2_g")[:, m:m + 1], None, ALU.mult)
            dve.tensor_copy(fvo[:, :, :], ps[:, 3, :].rearrange("p (k n) -> p k n", k=KD))
            dve.tensor_tensor(u_col[:, :], ps[:, 2, 0:KD], kept("bq"), ALU.add)
            dve.tensor_tensor(w_col[:, :], ps[:, 2, 2:2 + KD], kept("bv"), ALU.add)
            settle()
            for k in range(KD):
                dve.tensor_scalar(spread[:, k, :], ones, w_col[:, k:k + 1], None, ALU.mult)
                ins = dve.tensor_scalar(spread[:, 2 + k, :], ones, kept("fbv")[:, k:k + 1], None, ALU.mult)
            settle()
            dve.tensor_copy(rt[0][:, 0:1], w_col[:, 0:1]).then_inc(fold_ok, 1)
            dve.wait_ge(fold_ps, 2)
            dve.tensor_tensor(q_col[:, :], ps[:, 4, 0:KD], kept("ln2_g"), ALU.mult)
            dve.tensor_tensor(b1_col[:, :], ps[:, 4, 4:5], kept("b1"), ALU.add)
            dve.tensor_tensor(vo_row[:, :], ps[:, 5, 0:D], row("bo"), ALU.add)
            dve.tensor_tensor(fvo_row[:, :], ps[:, 5, D:2 * D], row("fbo"), ALU.add)
            dve.tensor_tensor(gh[:, :, :], ps[:, 6, 0:6 * NSLOT].rearrange("p (m n) -> p m n", m=6),
                              b_rz[:, :].unsqueeze(2).broadcast_to([P, 6, NSLOT]), ALU.add)
            settle()
            dve.tensor_copy(rt[0][:, 0:1], w_col[:, 0:1]).then_inc(fold_ok, 1)
            settle()

            with dve.Fori(0, NG // PAIR) as i:
                for j in range(PAIR):
                    n = PAIR * i + j
                    dve.wait_ge(x_in[j], 16 * (i + 1))
                    spread_of(j, X[j], D, "xh", 1.0 + EPS, EPS * EPS)
                    settle()
                    dve.wait_ge(c_in[j], 16 * (i + 1))
                    spread_of(j, C[j], DC, "ch")
                    norm(j, n, X[j], XH[j], D, "xh")
                    norm(j, n, C[j], CH[j], DC, "ch")
                    settle()
                for j in range(PAIR):
                    n = PAIR * i + j
                    dve.wait_ge(s["cT_ps"], n + 1)
                    dve.tensor_copy(CT[j], ps[:, 4 * j + 2:4 * j + 4, :]).then_inc(s["cT"], 1)
                for j in range(PAIR):
                    n = PAIR * i + j
                    dve.wait_ge(s["v_ps"], n + 1)
                    dve.tensor_tensor(V[j], ps[:, 4 * j + 2:4 * j + 4, :].rearrange("p t (h n) -> p (t h) n", h=2),
                                      vo_row[:, :].unsqueeze(1).broadcast_to([P, GB, D]), ALU.add).then_inc(s["v"], 1)
                for j in range(PAIR):
                    n = PAIR * i + j
                    dve.wait_ge(s["s_ps"], n + 1)
                    dve.tensor_reduce(nm[j][:, :], bank(j, 0).rearrange("p (t n) -> p t n", t=GB), AXX, ALU.max)
                    settle()
                    dve.tensor_scalar(nm[j][:, :], nm[j][:, :], -float(D) ** -0.5, None, ALU.mult).then_inc(s["nm"], 1)
                for j in range(PAIR):
                    n = PAIR * i + j
                    dve.wait_ge(s["p"], n + 1)
                    dve.reciprocal(sm[j][:, :], sm[j][:, :])
                    settle()
                    dve.wait_ge(s["o_ps"], n + 1)
                    for t in range(GB):
                        dve.scalar_tensor_tensor(X[j][:, t, :], bank(j, 2 + t // 2)[:, t % 2 * D:(t % 2 + 1) * D],
                                                 sm[j][:, t:t + 1], X[j][:, t, :], ALU.mult, ALU.add)
                    settle()
                    spread_of(j, X[j], D, "xh2")
                    settle()
                for j in range(PAIR):
                    norm(j, PAIR * i + j, X[j], XH[j], D, "xh2")
                settle()
                for j in range(PAIR):
                    n = PAIR * i + j
                    dve.wait_ge(s["lg_ps"], n + 1)
                    dve.tensor_tensor(LG[j], bank(j, 3)[:, 0:GB * NSLOT].rearrange("p (t n) -> p t n", t=GB),
                                      row("b2").unsqueeze(1).broadcast_to([P, GB, NSLOT]), ALU.add)
                    settle()
                    for t in range(GB):
                        dve.max(m8[j][:, t, :], LG[j][:, t, :])
                    settle()
                    for t in range(GB):
                        dve.match_replace(LK[j][:, t, :], m8[j][:, t, :], LG[j][:, t, :], NEG)
                    dve.tensor_scalar(nm[j][:, :], m8[j][:, :, 0], inv_tau[:, 0:1], -1.0, ALU.mult, ALU.mult).then_inc(s["top"], 1)
                for j in range(PAIR):
                    n = PAIR * i + j
                    settle()
                    dve.tensor_tensor(MK[j], LK[j], LG[j], ALU.is_lt)
                    settle()
                    dve.wait_ge(s["ex"], n + 1)
                    dve.tensor_tensor(EX[j], EX[j], MK[j], ALU.mult)
                    settle()
                    dve.tensor_reduce(sm[j][:, :], EX[j], AXX, ALU.add)
                    settle()
                    dve.reciprocal(sm[j][:, :], sm[j][:, :])
                    settle()
                    dve.tensor_tensor(AL[j], EX[j], sm[j][:, :].unsqueeze(2).broadcast_to([P, GB, NSLOT]), ALU.mult).then_inc(s["al"], 1)
                for j in range(PAIR):
                    n = PAIR * i + j
                    dve.wait_ge(s["si_ps"], n + 1)
                    dve.tensor_scalar(RW[j], bank(j, 2)[:, 0:256], 1e-8, None, ALU.add)
                    settle()
                    dve.reciprocal(RW[j], RW[j])
                    settle()
                    dve.tensor_tensor(GI[j], bank(j, 1).rearrange("p (k n) -> p k n", k=KD),
                                      RW[j].unsqueeze(1).broadcast_to([P, KD, 256]), ALU.mult).then_inc(s["gi"], 1)
                for j in range(PAIR):
                    n = PAIR * i + j
                    dve.wait_ge(s["gx_ps"], n + 1)
                    for g, o in enumerate((0, 3)):
                        for k in range(KD):
                            ins = dve.tensor_tensor(RZ[j][:, g, k * 256:(k + 1) * 256].rearrange("p (t n) -> p t n", t=GB),
                                                    bank(j, o)[:, k * 256:(k + 1) * 256].rearrange("p (t n) -> p t n", t=GB),
                                                    gh[:, g * KD + k, :].unsqueeze(1).broadcast_to([P, GB, NSLOT]), ALU.add)
                    ins.then_inc(s["rz"], 1)
                for j in range(PAIR):
                    n = PAIR * i + j
                    dve.wait_ge(s["rz_act"], n + 1)
                    for k in range(KD):
                        dve.tensor_tensor(NN[j][:, k, :].rearrange("p (t n) -> p t n", t=GB),
                                          RZ[j][:, 0, k * 256:(k + 1) * 256].rearrange("p (t n) -> p t n", t=GB),
                                          gh[:, 4 + k, :].unsqueeze(1).broadcast_to([P, GB, NSLOT]), ALU.mult)
                    settle()
                    dve.tensor_tensor(NN[j], NN[j], bank(j, 1).rearrange("p (k n) -> p k n", k=KD), ALU.add).then_inc(s["n_pre"], 1)
                for j in range(PAIR):
                    n = PAIR * i + j
                    dve.wait_ge(s["n_act"], n + 1)
                    for k in range(KD):
                        dve.tensor_tensor(DF[j][:, k, :].rearrange("p (t n) -> p t n", t=GB),
                                          slots[:, k, :].unsqueeze(1).broadcast_to([P, GB, NSLOT]),
                                          NN[j][:, k, :].rearrange("p (t n) -> p t n", t=GB), ALU.subtract)
                    settle()
                    dve.tensor_tensor(DF[j], DF[j], RZ[j][:, 1, :].rearrange("p (k n) -> p k n", k=KD), ALU.mult)
                    settle()
                    dve.tensor_tensor(SN[j], DF[j], NN[j], ALU.add).then_inc(s["sn"], 1)
                for j in range(PAIR):
                    n = PAIR * i + j
                    dve.wait_ge(s["sv_ps"], n + 1)
                    dve.tensor_tensor(SV[j], bank(j, 2).rearrange("p (h n) -> p h n", h=2),
                                      fvo_row[:, :].unsqueeze(1).broadcast_to([P, 2, D]), ALU.add).then_inc(s["sv"], 1)
                for j in range(PAIR):
                    n = PAIR * i + j
                    dve.wait_ge(s["fo_ps"], n + 1)
                    dve.tensor_tensor(X[j][:, :, :], X[j][:, :, :], ps[:, 4 * j:4 * j + 2, :].rearrange("p t (h n) -> p (t h) n", h=2), ALU.add)
                    settle()
                    spread_of(j, X[j], D, "xh3")
                    settle()
                for j in range(PAIR):
                    norm(j, PAIR * i + j, X[j], XH[j], D, "xh3")
                settle()
                for j in range(PAIR):
                    n = PAIR * i + j
                    dve.wait_ge(s["k_ps"], n + 1)
                    for k in range(KD):
                        ins = dve.tensor_scalar(KT[j][:, k, :], bank(j, 2 + k), kept("abk")[:, k:k + 1], None, ALU.add)
                    ins.then_inc(s["k"], 1)
                for j in range(PAIR):
                    n = PAIR * i + j
                    dve.wait_ge(s["v1_ps"], n + 1)
                    dve.wait_ge(v1_zero, PAIR)
                    for t in range(GB):
                        for o in range(2):
                            half = lambda v: v.rearrange("p (h n) -> p h n", n=32)[:, :, o * HD:(o + 1) * HD]
                            ins = dve.tensor_tensor(half(V1[j][:, t, o, :]), half(bank(j, 2 + t // 2)[:, t % 2 * D:(t % 2 + 1) * D]),
                                                    half(row("abv")), ALU.add)
                    ins.then_inc(s["v1"], 1)
                for j in range(PAIR):
                    n = PAIR * i + j

                    def shift(u):
                        unit = 2 * GB * n + u
                        sc = ps[:, 4 * (u % 2):4 * (u % 2) + 2, :].rearrange("p t (h n) -> p (t h) n", h=4)
                        dve.wait_ge(s["sc_ps"], unit + 1)
                        dve.tensor_reduce(mx[u % 2][:, :], sc, AXX, ALU.max)
                        settle()
                        if j or u >= 2:
                            dve.wait_ge(s["pt_ps"], unit - 1)
                        dve.tensor_tensor(PP[u % 2], sc, mx[u % 2][:, :].unsqueeze(2).broadcast_to([P, HT8, S]), ALU.subtract).then_inc(s["sub"], 1)

                    def divide(u):
                        unit = 2 * GB * n + u
                        bb, t = u // 2, u % 2
                        dve.wait_ge(s["ot_ps"], unit + 1)
                        dve.reciprocal(rc[u % 2][:, :], ps[:, 6 + u % 2, S:2 * S])
                        settle()
                        dve.tensor_tensor(OT[j][:, t, bb * S:(bb + 1) * S], ps[:, 6 + u % 2, 0:S], rc[u % 2][:, :], ALU.mult).then_inc(s["ot"], 1)

                    for u in range(2 * GB):
                        shift(u)
                        if u >= 2:
                            divide(u - 2)
                    divide(2 * GB - 2)
                    divide(2 * GB - 1)
                for j in range(PAIR):
                    n = PAIR * i + j
                    dve.wait_ge(s["xb"], n + 1)
                    dve.wait_ge(s["y_ps"], n + 1)
                    dve.tensor_tensor(X[j][:, :, :], X[j][:, :, :], ps[:, 4 * j:4 * j + 2, :].rearrange("p t (h n) -> p (t h) n", h=2), ALU.add)
                    settle()
                    spread_of(j, X[j], D, "xh4")
                    settle()
                for j in range(PAIR):
                    norm(j, PAIR * i + j, X[j], XH[j], D, "xh4")
                settle()
                for j in range(PAIR):
                    n = PAIR * i + j
                    dve.wait_ge(stored[j], 32 * (i + 1))
                    dve.wait_ge(s["gl_ps"], n + 1)
                    dve.tensor_copy(gl[:, bass.ds(n * GB, GB), :], bank(j, 0)[:, 0:GB * NE].rearrange("p (t n) -> p t n", t=GB)).then_inc(through[j], 1)
            settle()
            def over(v, n):
                return v.unsqueeze(2).broadcast_to([P, B, n])

            def ranks(v, n, before, out):
                one, two_ = (t[:, 0:B * n * n].rearrange("p (b e o) -> p b e o", b=B, e=n) for t in (cmp1, cmp2))
                other, own = v.unsqueeze(2).broadcast_to([P, B, n, n]), v.unsqueeze(3).broadcast_to([P, B, n, n])
                dve.tensor_tensor(one, other, own, ALU.is_gt)
                dve.tensor_tensor(two_, other, own, ALU.is_equal)
                settle()
                dve.tensor_tensor(two_, two_, kept(before, n).unsqueeze(1).broadcast_to([P, B, n, n]), ALU.mult)
                settle()
                dve.tensor_tensor(one, one, two_, ALU.add)
                settle()
                dve.tensor_reduce(out, one, AXX, ALU.add)
                settle()

            dve.tensor_reduce(g_max, gl[:, :, :], AXX, ALU.max)
            settle()
            dve.tensor_tensor(prob, gl[:, :, :], over(g_max, NE), ALU.subtract).then_inc(g_diff, 1)
            dve.wait_ge(g_exp, 1)
            dve.tensor_reduce(g_max, prob, AXX, ALU.add)
            settle()
            dve.reciprocal(g_max, g_max)
            settle()
            dve.tensor_tensor(prob, prob, over(g_max, NE), ALU.mult)
            settle()
            in_groups = lambda v: v.rearrange("p b (g e) -> p b g e", g=NGRP)
            dve.tensor_reduce(g_top, in_groups(prob), AXX, ALU.max)
            settle()
            ranks(g_top, NGRP, "before_group", r4)
            dve.tensor_scalar(g_ok, r4, float(NPICK), None, ALU.is_lt)
            settle()
            dve.tensor_tensor(in_groups(masked), in_groups(prob), g_ok.unsqueeze(3).broadcast_to([P, B, NGRP, NE // NGRP]), ALU.mult)
            settle()
            ranks(masked, NE, "before_expert", work)
            dve.tensor_scalar(picked, work, float(NPICK), None, ALU.is_lt).then_inc(picks, 1)
            dve.tensor_scalar(first, work, 0.0, None, ALU.is_equal)
            dve.tensor_scalar(second, work, 1.0, None, ALU.is_equal)
            settle()
            for k, which in enumerate((first, second)):
                dve.tensor_tensor(work, masked, which, ALU.mult)
                settle()
                dve.tensor_reduce(weight[:, k, :], work, AXX, ALU.add)
                settle()
            dve.tensor_tensor(w_sum, weight[:, 0, :], weight[:, 1, :], ALU.add)
            settle()
            dve.reciprocal(w_sum, w_sum)
            settle()
            dve.tensor_tensor(weight[:, :, :], weight[:, :, :], w_sum.unsqueeze(1).broadcast_to([P, 2, B]), ALU.mult)
            dve.wait_ge(counted, 1)
            dve.tensor_copy(total, ps[:, 1, 0:B * NE].rearrange("p (b e) -> p b e", b=B))
            settle()
            here, there, step = total, sums, 1
            while step < B:
                dve.tensor_copy(there[:, 0:step, :], here[:, 0:step, :])
                dve.tensor_tensor(there[:, step:B, :], here[:, step:B, :], here[:, 0:B - step, :], ALU.add)
                settle()
                here, there, step = there, (sums2 if there is sums else sums), 2 * step
            c816 = cmp1[:, 0:NE * B].rearrange("p (e t) -> p e t", e=NE)
            dve.tensor_tensor(c816, here[:, B - 1, :].unsqueeze(2).broadcast_to([P, NE, B]),
                              kept("tile_start").unsqueeze(1).broadcast_to([P, NE, B]), ALU.is_gt)
            settle()
            dve.tensor_reduce(n_tiles, c816, AXX, ALU.add)
            settle()
            c88 = cmp1[:, 0:NE * NE].rearrange("p (e o) -> p e o", e=NE)
            dve.tensor_tensor(c88, kept("before_expert", NE), n_tiles.unsqueeze(1).broadcast_to([P, NE, NE]), ALU.mult)
            settle()
            dve.tensor_reduce(t_off, c88, AXX, ALU.add)
            settle()
            dve.tensor_tensor(t_end, t_off, n_tiles, ALU.add)
            dve.tensor_scalar(t_off, t_off, float(P), None, ALU.mult)
            settle()
            ct8 = cmp1[:, 0:NT * NE].rearrange("p (t e) -> p t e", t=NT)
            dve.tensor_tensor(ct8, t_end.unsqueeze(1).broadcast_to([P, NT, NE]), kept("tile_no").unsqueeze(2).broadcast_to([P, NT, NE]), ALU.is_le)
            dve.tensor_tensor(place, here, total, ALU.subtract)
            settle()
            dve.tensor_reduce(e_flt, ct8, AXX, ALU.add)
            dve.tensor_tensor(place, place, ps[:, 0, 0:B * NE].rearrange("p (b e) -> p b e", b=B), ALU.add)
            settle()
            dve.tensor_scalar(e_id[:, :], e_flt, float(NE - 1), None, ALU.min)
            dve.tensor_tensor(place, place, t_off.unsqueeze(1).broadcast_to([P, B, NE]), ALU.add)
            settle()
            for k, which in enumerate((first, second)):
                dve.tensor_tensor(work, place, which, ALU.mult)
                settle()
                dve.tensor_reduce(pos[:, k, :], work, AXX, ALU.add)
                settle()
            dve.tensor_copy(pos_i[:, :, :], pos).then_inc(routed, 1)

            def tail(t, u):
                dve.wait_ge(ha_ps, t + 1)
                dve.tensor_copy(HAT[u], ps[:, 7, :].rearrange("p (k n) -> p k n", k=INTER // P)).then_inc(ha, 1)

            def gated(t, u):
                dve.wait_ge(silu, t + 1)
                dve.tensor_tensor(HA[u], HA[u], ps[:, 2 * u + 1, :], ALU.mult).then_inc(act_ok, 1)

            gated(0, 0)
            with dve.Fori(0, (NT - 1) // 2) as i:
                for u in range(2):
                    tail(2 * i + u, u)
                    gated(2 * i + u + 1, 1 - u)
            tail(NT - 1, 0)
            dve.wait_ge(rows_back, 32)
            for g in range(NG):
                dve.wait_ge(got_in[g], 16 * NPICK * GB)
                for k in range(NPICK):
                    for t in range(GB):
                        v = back[g][0][:, t, :]
                        ins = dve.scalar_tensor_tensor(v, got[g * GB + t][:, k * D:(k + 1) * D], weight[:, k, g * GB + t:g * GB + t + 1], v,
                                                       ALU.mult, ALU.add)
                    settle()
                dve.tensor_copy(g_max, g_max).then_inc(final, 1)


def packed(parts, width, arrays):
    out = np.zeros((P, width), np.float32)
    for name, (at, n) in parts.items():
        out[:, at:at + n] = np.reshape(arrays[name], (P, n))
    return out


def tiles(w):
    k = -(-w.shape[0] // P)
    full = np.zeros((k * P, w.shape[1]), w.dtype)
    full[:w.shape[0]] = w
    return full.reshape(k, P, w.shape[1]).transpose(1, 0, 2)


def wide(w, n):
    full = np.zeros((w.shape[0], n), w.dtype)
    full[:, :w.shape[1]] = w
    return full


def kernel(**inputs):
    import concourse.bacc as bacc
    from concourse.bass_utils import run_bass_kernel_spmd

    v = {k: np.asarray(a) for k, a in inputs.items()}
    A, Fn, L, M = (lambda n: v["L0_xattn_" + n]), (lambda n: v["L0_ffn_" + n]), (lambda n: v["L1_xattn_" + n]), (lambda n: v["L1_ffn_" + n])
    col = lambda w: tiles(w.reshape(-1, 1))[:, :, 0]
    half = np.zeros((P, 2, 32), np.float32)
    half[:, 0, :HD] = 1
    half[:, 1, HD:] = 1
    keep = packed(KEEP, KEEP_N, {
        "ident": np.eye(P, dtype=np.float32), "ones": np.ones((P, P), np.float32), "ones_half": half,
        "head_mask": np.kron(np.eye(HT8, dtype=np.float32), np.ones((HD, 1), np.float32)),
        "half_mask": np.kron(np.eye(2, dtype=np.float32), np.ones((NSLOT, 1), np.float32)),
        "w1": tiles(Fn("w1").T), "w2": Fn("w2").T, "wih": tiles(Fn("gru_wih").T),
        "aWq": tiles(L("Wq")), "aWk": tiles(L("Wk")), "aWv": tiles(L("Wv")), "aW1": tiles(L("W1")), "aW2": tiles(L("W2")),
        "gate": tiles(M("gate_w").T),
        "upper": np.triu(np.ones((P, P), np.float32), 1),
        "before_group": np.tile(np.tril(np.ones((NGRP, NGRP), np.float32), -1).reshape(1, -1), (P, 1)),
        "before_expert": np.tile(np.tril(np.ones((NE, NE), np.float32), -1).reshape(1, -1), (P, 1)),
        "tile_start": np.tile(P * np.arange(B, dtype=np.float32), (P, 1)), "tile_no": np.tile(np.arange(NT, dtype=np.float32), (P, 1)),
        "ln1_g": col(A("ln1_g")), "ln1_b": col(A("ln1_b")), "ln2_g": col(A("ln2_g")), "ln2_b": col(A("ln2_b")),
        "bq": col(A("bq")), "bv": col(A("bv")), "b1": col(Fn("b1")), "bih": col(Fn("gru_bih")), "bhh": col(Fn("gru_bhh")),
        "fbv": col(Fn("bv")), "abq": col(L("bq")), "abk": col(L("bk")), "ab1": col(L("b1")),
    })
    fold = packed(FOLD, FOLD_N, {
        "WqT": tiles(A("Wq").T), "WkT": tiles(wide(A("Wk").T, D)), "Wq": tiles(A("Wq")), "Wo": tiles(A("Wo")),
        "WvT": tiles(wide(A("Wv").T, D)), "Wv": tiles(A("Wv")), "whh": tiles(Fn("gru_whh").T),
        "fwv": tiles(Fn("wv")), "fwoT": tiles(Fn("wo").T), "slots": tiles(Fn("slot_init").T),
    })
    rows = np.zeros((ROWS_N,), np.float32)
    for name, a in (("bo", A("bo")), ("slot_scale", Fn("slot_scale")), ("b2", Fn("b2")), ("tau", Fn("tau")),
                    ("fbo", Fn("bo")), ("abv", L("bv")), ("ab2", L("b2"))):
        at, n = ROWS[name]
        rows[at:at + n] = a.reshape(-1)
    ctx = v["ctx_768"]
    ctxT = tiles(ctx.reshape(B * S, DC).T).reshape(P, KD, NG, GT).transpose(2, 0, 1, 3)
    experts = np.concatenate([
        M("w13_weight").transpose(0, 2, 1).reshape(NE, KD, P, 2 * INTER).transpose(0, 2, 1, 3).reshape(NE, P, -1),
        M("w2_weight").transpose(0, 2, 1).reshape(NE, INTER // P, P, D).transpose(0, 2, 1, 3).reshape(NE, P, -1)], axis=2)
    arrays = {"x": v["x"], "ctx": ctx, "ctxT": ctxT, "keep": keep, "fold": fold, "rows": rows, "experts": experts}

    nc = bacc.Bacc("TRN2", target_bir_lowering=False, num_devices=1)
    args, feed = [], {}
    for name, a in arrays.items():
        a = np.ascontiguousarray(a)
        feed["in_" + name] = a
        args.append(nc.dram_tensor("in_" + name, a.shape, mybir.dt.from_np(a.dtype), kind="ExternalInput").ap())
    out = nc.dram_tensor("out_x", (B, S, D), F32, kind="ExternalOutput").ap()
    scratch = [nc.dram_tensor(name, shape, F32, kind="Internal").ap()
               for name, shape in (("rows3", (B, S, D)), ("normed3", (B, S, D)), ("dispatched", (NT * P, D)), ("answers", (NT * P, D)))]
    build(nc, *args, *scratch, out)
    r = run_bass_kernel_spmd(nc, [feed], core_ids=[0])
    return r.results[0]["out_x"]
```

```python
from contextlib import ExitStack

import numpy as np
import concourse.bass as bass
from concourse import mybir

F32 = mybir.dt.float32
ALU = mybir.AluOpType
ACT = mybir.ActivationFunctionType
AXX = mybir.AxisListType.X

P = 128
B, S, D = 16, 128, 256
DC = 192
KD = D // P
GB = 4
GT = GB * S
NG = B // GB
PAIR = 2
NSLOT, TOPK = 64, 8
NH, HD = 16, 16
HT8 = P // HD
H1 = 2 * D
NE, INTER = 8, 512
NGRP, NPICK = 4, 2
ROW = 268
NT = B * S * NPICK // P + NE - 1
EPS = 1e-5
NEG = -3.0e38


def columns(parts):
    at, out = 0, {}
    for name, n in parts:
        out[name] = (at, n)
        at += n
    return out, at


KEEP, KEEP_N = columns([
    ("ident", P), ("ones", P), ("ones_half", 2 * 32), ("head_mask", HT8), ("half_mask", 2),
    ("w1", 4 * P), ("w2", NSLOT), ("wih", KD * 3 * D), ("aWq", KD * D), ("aWk", KD * D), ("aWv", KD * D),
    ("aW1", KD * H1), ("aW2", H1 // P * D), ("gate", KD * NE),
    ("ln1_g", KD), ("ln1_b", KD), ("ln2_g", KD), ("ln2_b", KD), ("bq", KD), ("bv", KD),
    ("upper", P), ("before_group", NGRP * NGRP), ("before_expert", NE * NE), ("tile_start", B), ("tile_no", NT), ("expert_no", NE), ("row_no", B), ("spare_no", 1),
    ("b1", 1), ("bih", 6), ("bhh", 6), ("fbv", KD), ("abq", KD), ("abk", KD), ("ab1", H1 // P),
])
FOLD, FOLD_N = columns([
    ("WqT", KD * D), ("WkT", KD * D), ("Wq", KD * D), ("Wo", KD * D), ("WvT", KD * D), ("Wv", KD * D),
    ("whh", KD * 3 * D), ("fwv", KD * D), ("fwoT", KD * D), ("slots", KD * NSLOT),
])
ROWS, ROWS_N = columns([
    ("bo", D), ("slot_scale", NSLOT), ("b2", NSLOT), ("tau", 1), ("fbo", D), ("abv", D), ("ab2", D),
])


def build(nc, x_d, ctx_d, ctxT_d, keep_d, fold_d, rows_d, experts_d, x3_d, xh_d, sent_d, out_d):
    with ExitStack() as stack:
        def sb(name, shape, dt=F32):
            return stack.enter_context(nc.sbuf_tensor(name, shape, dt))

        def sem(name):
            return stack.enter_context(nc.semaphore(name))

        ps = stack.enter_context(nc.psum_tensor("ps", [P, 8, 512], F32))

        EXP_N = KD * 2 * INTER + INTER // P * D
        experts = sb("experts", [P, NE * EXP_N])
        carve_at = [NE // 2 * EXP_N]

        def carve(n):
            at = carve_at[0]
            carve_at[0] += n
            assert carve_at[0] <= NE * EXP_N
            return experts[:, at:at + n]

        keep = sb("keep", [P, KEEP_N])
        rows = sb("rows", [P, ROWS_N])
        ring = sb("ring", [P, 6 * 1024])

        def kept(name, t=1):
            at, n = KEEP[name]
            v = keep[:, at:at + n]
            return v.rearrange("p (t n) -> p t n", t=t) if t > 1 else v

        def fold(name, t=KD):
            at, n = FOLD[name]
            return ring[:, at:at + n].rearrange("p (t n) -> p t n", t=t)

        def row(name):
            at, n = ROWS[name]
            return rows[:, at:at + n]

        assert FOLD_N <= 6 * 1024
        ident, ones = kept("ident"), kept("ones")

        qk = sb("qk", [P, KD, D])
        vo = sb("vo", [P, KD, D])
        vo_row = sb("vo_row", [P, D])
        q_col = sb("q_col", [P, KD])
        u_col = sb("u_col", [P, KD])
        w_col = sb("w_col", [P, KD])
        spread = sb("spread", [P, 2 * KD, P])
        slots = sb("slots", [P, KD, NSLOT])
        slot_mean = sb("slot_mean", [P, KD])
        b1_col = sb("b1_col", [P, 1])
        inv_tau = sb("inv_tau", [P, 1])
        b_rz = sb("b_rz", [P, 6])
        gh = sb("gh", [P, 6, NSLOT])
        fvo = sb("fvo", [P, KD, D])
        fvo_row = sb("fvo_row", [P, D])

        ab = [carve(2048) for _ in range(PAIR)]
        a, b = [v[:, 0:1024] for v in ab], [v[:, 1024:2048] for v in ab]
        XT, c, d, e = ([carve(1024) for _ in range(PAIR)] for _ in range(4))
        X = [sb(f"X{j}", [P, GB, D]) for j in range(PAIR)]
        XH = [sb(f"XH{j}", [P, GB, D]) for j in range(PAIR)]
        f = [sb(f"f{j}", [P, 1024]) for j in range(PAIR)]
        V1 = [sb(f"V1{j}", [P, GB, 2, D]) for j in range(PAIR)]

        def two(buf, t):
            return [v.rearrange("p (t n) -> p t n", t=t) for v in buf]

        xT = two(XT, KD)
        C = [v[:, 0:GB * DC].rearrange("p (t n) -> p t n", t=GB) for v in a]
        CH, CT, Q, V = two(b, GB), two(c, KD), two(d, KD), two(e, GB)
        PR = [v[:, 0:512].rearrange("p (t n) -> p t n", t=GB) for v in f]
        PT = [v[:, 512:1024].rearrange("p (t n) -> p t n", t=GB) for v in f]
        HT = [v[:, 0:512] for v in f]
        LG, LK, EX, MK = ([v[:, 256 * n:256 * n + 256].rearrange("p (t n) -> p t n", t=GB) for v in a] for n in range(4))
        AL = [v[:, 0:256].rearrange("p (t n) -> p t n", t=GB) for v in b]
        RW = [v[:, 256:512] for v in b]
        AT = [v[:, 512:1024].rearrange("p (h o n) -> p h o n", h=2, o=2) for v in b]
        GI = [v[:, 0:512].rearrange("p (k n) -> p k n", k=KD) for v in c]
        NN = [v[:, 512:1024].rearrange("p (k n) -> p k n", k=KD) for v in c]
        RZ = [v.rearrange("p (g n) -> p g n", g=2) for v in d]
        DF = [v[:, 0:512].rearrange("p (k n) -> p k n", k=KD) for v in e]
        SN = [v[:, 512:1024].rearrange("p (k n) -> p k n", k=KD) for v in e]
        SV = [v[:, 512:1024].rearrange("p (h n) -> p h n", h=2) for v in f]
        YT, KT, Q1, OT = two(c, KD), two(a, KD), two(d, KD), two(e, KD)
        HF = two(ab, H1 // P)
        KB = [ring[:, 1024 * n:1024 * n + 1024].rearrange("p (h n) -> p h n", h=HT8) for n in range(2)]
        PP = [ring[:, 1024 * n:1024 * n + 1024].rearrange("p (h n) -> p h n", h=HT8) for n in range(2, 4)]
        PQ = [ring[:, 1024 * n:1024 * n + 1024].rearrange("p (h n) -> p h n", h=HT8) for n in range(4, 6)]

        stat = [sb(f"stat{j}", [P, GB, 6]) for j in range(PAIR)]
        norms = ("xh", "ch", "xh2", "xh3", "xh4")
        mv = {m: [sb(f"mv_{m}{j}", [P, GB, 2]) for j in range(PAIR)] for m in norms}
        var = {m: [sb(f"var_{m}{j}", [P, GB]) for j in range(PAIR)] for m in norms}
        minus_half = sb("minus_half", [P, GB])
        rt = [sb(f"rt{j}", [P, GB]) for j in range(PAIR)]
        nm = [sb(f"nm{j}", [P, GB]) for j in range(PAIR)]
        sm = [sb(f"sm{j}", [P, GB]) for j in range(PAIR)]
        m8 = [sb(f"m8{j}", [P, GB, 8]) for j in range(PAIR)]
        mx = [sb(f"mx{n}", [P, HT8]) for n in range(2)]
        rc = [sb(f"rc{n}", [P, P]) for n in range(2)]
        gl = sb("gl", [P, B, NE])

        XA = ring[:, 0:B * ROW].rearrange("p (b n) -> p b n", b=B)
        cmp1, cmp2 = (V1[0][:, 2 * h:2 * h + 2, :, :].rearrange("p t o n -> p (t o n)") for h in range(2))
        spare = [V1[1][:, :, :, :].rearrange("p t o n -> p (t o n)")[:, 128 * n:128 * n + 128] for n in range(16)]
        prob, masked, first, second, picked, sums, sums2, total, place, work = (v.rearrange("p (b e) -> p b e", b=B) for v in spare[:10])
        g_top, r4, g_ok = (v[:, 0:B * NGRP].rearrange("p (b g) -> p b g", b=B) for v in spare[10:13])
        cols = spare[13]
        g_max, n_tiles, t_off, t_end, e_flt = cols[:, 0:B], cols[:, B:B + NE], cols[:, 24:32], cols[:, 32:40], cols[:, 40:40 + NT]
        pos = spare[14][:, 0:2 * B].rearrange("p (k b) -> p k b", k=2)
        w_sum = spare[14][:, 2 * B:3 * B]
        e_min = spare[15][:, 0:NT]
        pos_i = sb("pos_i", [P, 2, B], mybir.dt.int32)
        e_id = sb("e_id", [P, NT], mybir.dt.int32)
        blank = sb("blank", [P, ROW])
        tile_hot = sb("tile_hot", [P, NT, NE])
        row_no = sb("row_no", [P, NT])
        row_w = [sb(f"row_w{u}", [P, 1]) for u in range(2)]
        row_w8 = [sb(f"row_w8{u}", [P, NE]) for u in range(2)]
        row_i = [sb(f"row_i{u}", [P, 1], mybir.dt.int32) for u in range(2)]
        at = KEEP["wih"][0]
        assert KEEP["aW2"][0] + KEEP["aW2"][1] - at >= 2 * (ROW + D + 2 * INTER)
        XI = [keep[:, at + ROW * n:at + ROW * (n + 1)] for n in range(2)]
        at += 2 * ROW
        XIT = [keep[:, at + D * n:at + D * n + D].rearrange("p (k n) -> p k n", k=KD) for n in range(2)]
        at += 2 * D
        HA = [keep[:, at + INTER * n:at + INTER * n + INTER] for n in range(2)]
        HAT = [keep[:, at + INTER * n:at + INTER * n + INTER].rearrange("p (k n) -> p k n", k=INTER // P) for n in range(2, 4)]
        YO = [f[0][:, D * n:D * n + D] for n in range(2)]

        keep_in, fold_in, rows_in = sem("keep_in"), sem("fold_in"), sem("rows_in")
        x_in, c_in, y_in = ([sem(f"{t}{j}") for j in range(PAIR)] for t in ("x_in", "c_in", "y_in"))
        names = ("xh ch ch_pad xT_ps xT cT_ps cT q_ps q v_ps v s_ps nm p pT_ps pT o_ps "
                 "xh2 xT2_ps xT2 h_ps h lg_ps top ex al aT_ps aT si_ps gi gx_ps rz rz_act n_pre n_act sn sv_ps sv fo_ps "
                 "xh3 xb xT3_ps xT3 k_ps k v1_ps v1 q1_ps q1 f_ps f y_ps xh4 xT4_ps xT4 gl_ps "
                 "kb sc_ps sub exp pt_ps pt ot_ps ot")
        names += "".join(f" var_{m} rs_{m}" for m in norms)
        s = {n: sem("s_" + n) for n in names.split()}
        fold_ps, fold_ok = sem("fold_ps"), sem("fold_ok")
        v1_zero, half_set = sem("v1_zero"), sem("half_set")
        through = [sem(f"through{j}") for j in range(PAIR)]
        stored = [sem(f"stored{j}") for j in range(PAIR)]

        blank_set, sent_blank, spare_blank = sem("blank_set"), sem("sent_blank"), sem("spare_blank")
        early_in, late_in = ([sem(f"expert_in{n}") for n in range(h * NE // 2, (h + 1) * NE // 2)] for h in range(2))
        xa_in, xa_ok = sem("xa_in"), sem("xa_ok")
        g_diff, g_exp, picks, counted, routed = (sem(t) for t in ("g_diff", "g_exp", "picks", "counted", "routed"))
        rows_sent = sem("rows_sent")
        xi_in = [sem(f"xi_in{u}") for u in range(2)]
        xt_ps, xt, gu_ps, silu, act_ok, ha_ps, ha, y_ps, y_ok, picked_ok, no_ok, turns, added = (
            sem("e_" + t) for t in ("xt_ps", "xt", "gu_ps", "silu", "act_ok", "ha_ps", "ha", "y_ps", "y_ok", "picked_ok", "no_ok", "turns", "added"))
        out_done = sem("out_done")

        x_g = x_d.rearrange("(g b) p d -> g p b d", b=GB)
        c_g = ctx_d.rearrange("(g b) p d -> g p b d", b=GB)
        o_g, x3_g, xh_g = (t.rearrange("(g b) p d -> g p b d", b=GB) for t in (out_d, x3_d[0:B * S, :].rearrange("(b p) d -> b p d", b=B), xh_d))
        sent_t = sent_d.rearrange("(t p) d -> t p d", p=P)

        XT_PS, Y_PS = ps[:, 4, 0:D], [ps[:, 5 + u, 0:D] for u in range(2)]

        def tiles_of(eng, step):
            with eng.Fori(0, (NT - 3) // 2) as m:
                step(2 * m + 1, 1, m)
                step(2 * m + 2, 0, m + 1)

        block = stack.enter_context(nc.Block())

        def bank(j, k):
            return ps[:, 4 * j + k, :]

        @block.sync
        def _(sp):
            sp.dma_start(ring[:, 0:FOLD_N], fold_d).then_inc(fold_in, 16)
            sp.dma_start(keep[:, :], keep_d).then_inc(keep_in, 16)
            sp.dma_start(rows[:, :], rows_d.partition_broadcast(P)).then_inc(rows_in, 16)
            for j in range(PAIR):
                sp.sem_inc(through[j], 1)
            with sp.Fori(0, NG // PAIR) as i:
                for j in range(PAIR):
                    n = PAIR * i + j
                    sp.wait_ge(through[j], i + 1)
                    sp.dma_start(X[j][:, :, :], x_g[n]).then_inc(x_in[j], 16)
                    sp.dma_start(C[j], c_g[n]).then_inc(c_in[j], 16)
                for j in range(PAIR):
                    n = PAIR * i + j
                    sp.wait_ge(s["sn"], n + 1)
                    sp.dma_start(YT[j], ctxT_d[n]).then_inc(y_in[j], 16)
                for j in range(PAIR):
                    n = PAIR * i + j
                    sp.wait_ge(s["xh4"], n + 1)
                    sp.dma_start(x3_g[n], X[j][:, :, :]).then_inc(stored[j], 16)
                    sp.dma_start(xh_g[n], XH[j][:, :, :]).then_inc(stored[j], 16)
            for j in range(PAIR):
                sp.wait_ge(through[j], 1 + NG // PAIR)
            sp.dma_start(XA[:, :, 0:D], xh_d.rearrange("b p d -> p b d")).then_inc(xa_in, 16)
            for n in range(NE // 2):
                sp.dma_start(experts[:, (NE // 2 + n) * EXP_N:(NE // 2 + n + 1) * EXP_N], experts_d[NE // 2 + n]).then_inc(late_in[n], 16)
            sp.wait_ge(rows_sent, 16 * NPICK * B)
            for u in range(2):
                sp.dma_start(XI[u], sent_t[u]).then_inc(xi_in[u], 16)

            def step(t, u, half):
                sp.wait_ge(picked_ok, t + 1)
                sp.wait_ge(xt_ps, t + 1)
                sp.dma_start(XI[u], sent_t[t + 2]).then_inc(xi_in[u], 16)

            step(0, 0, 0)
            tiles_of(sp, step)
            sp.wait_ge(added, 16 * NT)
            sp.dma_start(out_d.rearrange("(g b) p d -> g (b p d)", g=B), x3_d[0:B * S, :].rearrange("(g p) d -> g (p d)", g=B)).then_inc(out_done, 16)
            sp.wait_ge(out_done, 16)

        @block.gpsimd
        def _(pool):
            for j in range(PAIR):
                pool.memset(V1[j][:, :, :, :], 0.0).then_inc(v1_zero, 1)
            pool.memset(blank[:, :], 0.0).then_inc(blank_set, 1)
            pool.wait_ge(blank_set, 1)
            pool.wait_ge(keep_in, 16)
            pool.tensor_copy(blank[:, D:D + 1], kept("spare_no")).then_inc(blank_set, 1)
            pool.memset(minus_half[:, :], -0.5).then_inc(half_set, 1)
            pool.wait_ge(half_set, 1)

            def root(j, n, name):
                pool.wait_ge(s["var_" + name], n + 1)
                pool.tensor_tensor(var[name][j][:, :], var[name][j][:, :], minus_half[:, :], ALU.pow).then_inc(s["rs_" + name], 1)

            with pool.Fori(0, NG // PAIR) as i:
                for j in range(PAIR):
                    n = PAIR * i + j
                    root(j, n, "xh")
                    pool.memset(CH[j][:, :, DC:D], 0.0).then_inc(s["ch_pad"], 1)
                    root(j, n, "ch")
                for name in ("xh2", "xh3"):
                    for j in range(PAIR):
                        root(j, PAIR * i + j, name)
                for j in range(PAIR):
                    n = PAIR * i + j
                    pool.wait_ge(s["xh3"], n + 1)
                    pool.tensor_tensor(X[j][:, :, :], X[j][:, :, :],
                                       row("ab2").unsqueeze(1).broadcast_to([P, GB, D]), ALU.add).then_inc(s["xb"], 1)
                for j in range(PAIR):
                    n = PAIR * i + j
                    pool.wait_ge(s["k"], n + 1)
                    for u in range(2 * GB):
                        bb, t = u // 2, u % 2
                        unit = 2 * GB * n + u
                        if j or u >= 2:
                            pool.wait_ge(s["sc_ps"], unit - 1)
                        pool.tensor_tensor(KB[u % 2], KT[j][:, t, bb * S:(bb + 1) * S].unsqueeze(1).broadcast_to([P, HT8, S]),
                                           kept("head_mask").unsqueeze(2).broadcast_to([P, HT8, S]), ALU.mult).then_inc(s["kb"], 1)
                for j in range(PAIR):
                    root(j, PAIR * i + j, "xh4")
            pool.wait_ge(xa_in, 16)
            pool.wait_ge(xa_ok, 1)
            pool.wait_ge(routed, 1)
            pool.wait_ge(sent_blank, 16)
            for k in range(NPICK):
                for t in range(B):
                    pool.indirect_dma_start(out=sent_d, out_offset=bass.IndirectOffsetOnAxis(ap=pos_i[:, k, t:t + 1], axis=0),
                                            in_=XA[:, t, :], in_offset=None).then_inc(rows_sent, 16)

            def add(t, u, half):
                pool.wait_ge(y_ok, t + 3)
                if not isinstance(t, int) or t:
                    pool.wait_ge(added, 16 * t)
                pool.wait_ge(no_ok, t + 1)
                pool.sem_inc(turns, 1)
                pool.indirect_dma_start(out=x3_d, out_offset=bass.IndirectOffsetOnAxis(ap=row_i[u][:, 0:1], axis=0),
                                        in_=YO[u], in_offset=None, compute_op=ALU.add).then_inc(added, 16)

            pool.wait_ge(spare_blank, 16)
            add(0, 0, 0)
            tiles_of(pool, add)
            for t in range(NT - 2, NT):
                add(t, t % 2, t // 2)

        @block.scalar
        def _(act):
            act.sem_inc(turns, 1)
            act.sem_inc(y_ok, 2)
            act.wait_ge(blank_set, 2)
            act.dma_start(sent_t.rearrange("t p d -> p t d"), blank[:, :].unsqueeze(1).broadcast_to([P, NT, ROW])).then_inc(sent_blank, 16)
            act.dma_start(x3_d[B * S:B * S + P, :], blank[:, 0:D]).then_inc(spare_blank, 16)
            for n in range(NE // 2):
                act.dma_start(experts[:, n * EXP_N:(n + 1) * EXP_N], experts_d[n]).then_inc(early_in[n], 16)
            act.wait_ge(keep_in, 16)
            act.wait_ge(fold_ok, 1)
            with act.Fori(0, NG // PAIR) as i:
                for j in range(PAIR):
                    n = PAIR * i + j
                    act.wait_ge(s["xT_ps"], n + 1)
                    act.copy(xT[j], ps[:, 4 * j:4 * j + 2, :]).then_inc(s["xT"], 1)
                for j in range(PAIR):
                    n = PAIR * i + j
                    act.wait_ge(s["q_ps"], n + 1)
                    for t in range(KD):
                        ins = act.activation(Q[j][:, t, :], bank(j, t), ACT.Identity, bias=q_col[:, t:t + 1],
                                             scale=kept("ln2_g")[:, t:t + 1])
                    ins.then_inc(s["q"], 1)
                for j in range(PAIR):
                    n = PAIR * i + j
                    act.wait_ge(s["nm"], n + 1)
                    for t in range(GB):
                        ins = act.activation(PR[j][:, t, :], bank(j, 0)[:, t * S:(t + 1) * S], ACT.Exp, bias=nm[j][:, t:t + 1],
                                             scale=float(D) ** -0.5, accum_out=sm[j][:, t:t + 1])
                    ins.then_inc(s["p"], 1)
                for j in range(PAIR):
                    n = PAIR * i + j
                    act.wait_ge(s["pT_ps"], n + 1)
                    act.copy(PT[j], bank(j, 1).rearrange("p (t n) -> p t n", t=GB)).then_inc(s["pT"], 1)
                for j in range(PAIR):
                    n = PAIR * i + j
                    act.wait_ge(s["xT2_ps"], n + 1)
                    act.copy(xT[j], ps[:, 4 * j:4 * j + 2, :]).then_inc(s["xT2"], 1)
                for j in range(PAIR):
                    n = PAIR * i + j
                    act.wait_ge(s["h_ps"], n + 1)
                    act.activation(HT[j], bank(j, 2), ACT.Gelu, bias=b1_col[:, 0:1], scale=1.0).then_inc(s["h"], 1)
                for j in range(PAIR):
                    n = PAIR * i + j
                    act.wait_ge(s["top"], n + 1)
                    for t in range(GB):
                        ins = act.activation(EX[j][:, t, :], LG[j][:, t, :], ACT.Exp, bias=nm[j][:, t:t + 1], scale=inv_tau[:, 0:1])
                    ins.then_inc(s["ex"], 1)
                for j in range(PAIR):
                    n = PAIR * i + j
                    act.wait_ge(s["aT_ps"], n + 1)
                    for o in range(2):
                        ins = act.activation(AT[j][:, :, o, :], bank(j, 0)[:, 0:2 * P].rearrange("p (h n) -> p h n", h=2),
                                             ACT.Copy, scale=kept("half_mask")[:, o:o + 1])
                    ins.then_inc(s["aT"], 1)
                for j in range(PAIR):
                    n = PAIR * i + j
                    act.wait_ge(s["rz"], n + 1)
                    act.activation(RZ[j], RZ[j], ACT.Sigmoid).then_inc(s["rz_act"], 1)
                for j in range(PAIR):
                    n = PAIR * i + j
                    act.wait_ge(s["n_pre"], n + 1)
                    for t in range(KD):
                        ins = act.activation(NN[j][:, t, :], NN[j][:, t, :], ACT.Tanh, bias=kept("bih")[:, 4 + t:5 + t], scale=1.0)
                    ins.then_inc(s["n_act"], 1)
                for j in range(PAIR):
                    n = PAIR * i + j
                    act.wait_ge(s["xT3_ps"], n + 1)
                    act.copy(xT[j], ps[:, 4 * j:4 * j + 2, :]).then_inc(s["xT3"], 1)
                for j in range(PAIR):
                    n = PAIR * i + j
                    act.wait_ge(s["q1_ps"], n + 1)
                    for t in range(KD):
                        ins = act.activation(Q1[j][:, t, :], bank(j, t), ACT.Identity, bias=kept("abq")[:, t:t + 1], scale=1.0)
                    ins.then_inc(s["q1"], 1)
                for j in range(PAIR):
                    n = PAIR * i + j
                    for u in range(2 * GB):
                        unit = 2 * GB * n + u
                        act.wait_ge(s["sub"], unit + 1)
                        act.activation(PP[u % 2], PP[u % 2], ACT.Exp, scale=float(HD) ** -0.5).then_inc(s["exp"], 1)
                        act.wait_ge(s["pt_ps"], unit + 1)
                        if j or u >= 2:
                            act.wait_ge(s["ot_ps"], unit - 1)
                        act.copy(PQ[u % 2], ps[:, 2:4, :].rearrange("p t (h n) -> p (t h) n", h=4)).then_inc(s["pt"], 1)
                for j in range(PAIR):
                    n = PAIR * i + j
                    act.wait_ge(s["f_ps"], n + 1)
                    for m in range(H1 // P):
                        ins = act.activation(HF[j][:, m, :], bank(j, m), ACT.Relu, bias=kept("ab1")[:, m:m + 1], scale=1.0)
                    ins.then_inc(s["f"], 1)
                for j in range(PAIR):
                    n = PAIR * i + j
                    act.wait_ge(s["xT4_ps"], n + 1)
                    act.copy(xT[j], ps[:, 4 * j + 2:4 * j + 4, :]).then_inc(s["xT4"], 1)
            act.wait_ge(g_diff, 1)
            act.activation(prob, prob, ACT.Exp).then_inc(g_exp, 1)

            def turned(t, u):
                act.wait_ge(xt_ps, t + 1)
                act.copy(XIT[u], XT_PS.rearrange("p (k n) -> p k n", k=KD)).then_inc(xt, 1)

            def gate(t, u):
                act.wait_ge(gu_ps, t + 1)
                act.activation(HA[u], ps[:, 2 * u, :], ACT.Silu).then_inc(silu, 1)

            def answer(t, u):
                act.wait_ge(y_ps, t + 1)
                act.wait_ge(turns, t + 1)
                act.copy(YO[u], Y_PS[u]).then_inc(y_ok, 1)

            def step(t, u, half):
                turned(t + 2, u)
                gate(t + 1, 1 - u)
                answer(t - 1, 1 - u)

            turned(0, 0)
            turned(1, 1)
            gate(0, 0)
            turned(2, 0)
            gate(1, 1)
            tiles_of(act, step)
            gate(NT - 1, 0)
            for t in range(NT - 3, NT):
                answer(t, t % 2)

        @block.tensor
        def _(pe):
            def mm(out, pairs):
                for k, (w, m) in enumerate(pairs):
                    ins = pe.matmul(out, w, m, start=(k == 0), stop=(k == len(pairs) - 1))
                return ins

            def turn(out, t):
                return pe.transpose(out, t, ident)

            pe.wait_ge(fold_in, 16)
            pe.wait_ge(keep_in, 16)
            WqT, WkT, Wq, Wo, WvT, Wv = (fold(t) for t in ("WqT", "WkT", "Wq", "Wo", "WvT", "Wv"))
            w1 = kept("w1", 4)
            for m in range(KD):
                mm(ps[:, 0, m * D:(m + 1) * D], [(WqT[:, k, m * P:(m + 1) * P], WkT[:, k, :]) for k in range(KD)])
                mm(ps[:, 1, m * D:(m + 1) * D], [(WvT[:, k, m * P:(m + 1) * P], Wo[:, k, :]) for k in range(KD)])
                mm(ps[:, 2, m:m + 1], [(Wq[:, k, m * P:(m + 1) * P], kept("ln1_b")[:, k:k + 1]) for k in range(KD)])
                mm(ps[:, 2, 2 + m:3 + m], [(Wv[:, k, m * P:(m + 1) * P], kept("ln2_b")[:, k:k + 1]) for k in range(KD)])
                ins = mm(ps[:, 3, m * D:(m + 1) * D], [(fold("fwv")[:, k, m * P:(m + 1) * P], fold("fwoT")[:, k, :]) for k in range(KD)])
            ins.then_inc(fold_ps, 1)
            pe.wait_ge(fold_ok, 1)
            for m in range(KD):
                mm(ps[:, 4, m:m + 1], [(WkT[:, k, m * P:(m + 1) * P], u_col[:, k:k + 1]) for k in range(KD)])
            mm(ps[:, 4, 4:5], [(w1[:, 2 + k, :], slot_mean[:, k:k + 1]) for k in range(KD)])
            mm(ps[:, 5, 0:D], [(spread[:, k, :], Wo[:, k, :]) for k in range(KD)])
            mm(ps[:, 5, D:2 * D], [(spread[:, 2 + k, :], fold("fwoT")[:, k, :]) for k in range(KD)])
            for m in range(6):
                ins = mm(ps[:, 6, m * NSLOT:(m + 1) * NSLOT], [(fold("whh")[:, k, m * P:(m + 1) * P], slots[:, k, :]) for k in range(KD)])
            ins.then_inc(fold_ps, 1)
            pe.wait_ge(fold_ok, 2)
            with pe.Fori(0, NG // PAIR) as i:
                for j in range(PAIR):
                    n = PAIR * i + j
                    pe.wait_ge(s["xh"], n + 1)
                    for k in range(KD):
                        for t in range(GB):
                            ins = turn(bank(j, k)[:, t * S:(t + 1) * S], XH[j][:, t, k * P:(k + 1) * P])
                    ins.then_inc(s["xT_ps"], 1)
                for j in range(PAIR):
                    n = PAIR * i + j
                    pe.wait_ge(s["ch"], n + 1)
                    pe.wait_ge(s["ch_pad"], n + 1)
                    for k in range(KD):
                        for t in range(GB):
                            ins = turn(bank(j, 2 + k)[:, t * S:(t + 1) * S], CH[j][:, t, k * P:(k + 1) * P])
                    ins.then_inc(s["cT_ps"], 1)
                for j in range(PAIR):
                    n = PAIR * i + j
                    pe.wait_ge(s["xT"], n + 1)
                    for m in range(KD):
                        ins = mm(bank(j, m), [(qk[:, k, m * P:(m + 1) * P], xT[j][:, k, :]) for k in range(KD)])
                    ins.then_inc(s["q_ps"], 1)
                for j in range(PAIR):
                    n = PAIR * i + j
                    pe.wait_ge(s["cT"], n + 1)
                    for t in range(GB):
                        ins = mm(bank(j, 2 + t // 2)[:, t % 2 * D:(t % 2 + 1) * D],
                                 [(CT[j][:, k, t * S:(t + 1) * S], vo[:, k, :]) for k in range(KD)])
                    ins.then_inc(s["v_ps"], 1)
                for j in range(PAIR):
                    n = PAIR * i + j
                    pe.wait_ge(s["q"], n + 1)
                    for t in range(GB):
                        tok = slice(t * S, (t + 1) * S)
                        ins = mm(bank(j, 0)[:, tok], [(Q[j][:, k, tok], CT[j][:, k, tok]) for k in range(KD)])
                    ins.then_inc(s["s_ps"], 1)
                for j in range(PAIR):
                    n = PAIR * i + j
                    pe.wait_ge(s["p"], n + 1)
                    for t in range(GB):
                        ins = turn(bank(j, 1)[:, t * S:(t + 1) * S], PR[j][:, t, :])
                    ins.then_inc(s["pT_ps"], 1)
                for j in range(PAIR):
                    n = PAIR * i + j
                    pe.wait_ge(s["pT"], n + 1)
                    pe.wait_ge(s["v"], n + 1)
                    for t in range(GB):
                        ins = mm(bank(j, 2 + t // 2)[:, t % 2 * D:(t % 2 + 1) * D], [(PT[j][:, t, :], V[j][:, t, :])])
                    ins.then_inc(s["o_ps"], 1)
                for j in range(PAIR):
                    n = PAIR * i + j
                    pe.wait_ge(s["xh2"], n + 1)
                    for k in range(KD):
                        for t in range(GB):
                            ins = turn(bank(j, k)[:, t * S:(t + 1) * S], XH[j][:, t, k * P:(k + 1) * P])
                    ins.then_inc(s["xT2_ps"], 1)
                for j in range(PAIR):
                    n = PAIR * i + j
                    pe.wait_ge(s["xT2"], n + 1)
                    mm(bank(j, 2), [(w1[:, k, :], xT[j][:, k, :]) for k in range(KD)]).then_inc(s["h_ps"], 1)
                for j in range(PAIR):
                    n = PAIR * i + j
                    pe.wait_ge(s["h"], n + 1)
                    for t in range(GB):
                        ins = mm(bank(j, 3)[:, t * NSLOT:(t + 1) * NSLOT], [(HT[j][:, t * S:(t + 1) * S], kept("w2"))])
                    ins.then_inc(s["lg_ps"], 1)
                for j in range(PAIR):
                    n = PAIR * i + j
                    pe.wait_ge(s["al"], n + 1)
                    for h in range(2):
                        ins = turn(bank(j, 0)[:, h * P:(h + 1) * P], AL[j][:, 2 * h:2 * h + 2, :].rearrange("p t n -> p (t n)"))
                    ins.then_inc(s["aT_ps"], 1)
                    for k in range(KD):
                        for t in range(GB):
                            at = (k * GB + t) * NSLOT
                            mm(bank(j, 1)[:, at:at + NSLOT], [(XH[j][:, t, k * P:(k + 1) * P], AL[j][:, t, :])])
                    mm(bank(j, 2)[:, 0:GB * NSLOT], [(ones, AL[j].rearrange("p t n -> p (t n)"))]).then_inc(s["si_ps"], 1)
                for j in range(PAIR):
                    n = PAIR * i + j
                    pe.wait_ge(s["aT"], n + 1)
                    pe.wait_ge(s["gi"], n + 1)
                    for g, o in enumerate((0, 3, 1)):
                        for m in range(KD):
                            at = (g * KD + m) * P
                            ins = mm(bank(j, o)[:, m * 256:(m + 1) * 256],
                                     [(kept("wih", KD)[:, k, at:at + P], GI[j][:, k, :]) for k in range(KD)])
                    ins.then_inc(s["gx_ps"], 1)
                for j in range(PAIR):
                    n = PAIR * i + j
                    pe.wait_ge(s["sn"], n + 1)
                    for h in range(2):
                        ins = mm(bank(j, 2)[:, h * D:(h + 1) * D], [(SN[j][:, k, h * P:(h + 1) * P], fvo[:, k, :]) for k in range(KD)])
                    ins.then_inc(s["sv_ps"], 1)
                for j in range(PAIR):
                    n = PAIR * i + j
                    pe.wait_ge(s["sv"], n + 1)
                    for t in range(GB):
                        ins = mm(bank(j, 0 if t < 2 else 1)[:, t % 2 * D:(t % 2 + 1) * D], [(AT[j][:, t // 2, t % 2, :], SV[j][:, t // 2, :])])
                    ins.then_inc(s["fo_ps"], 1)
                for j in range(PAIR):
                    n = PAIR * i + j
                    pe.wait_ge(y_in[j], 16 * (i + 1))
                    for m in range(KD):
                        ins = mm(bank(j, 2 + m), [(kept("aWk", KD)[:, k, m * P:(m + 1) * P], YT[j][:, k, :]) for k in range(KD)])
                    ins.then_inc(s["k_ps"], 1)
                for j in range(PAIR):
                    n = PAIR * i + j
                    pe.wait_ge(s["k"], n + 1)
                    for t in range(GB):
                        ins = mm(bank(j, 2 + t // 2)[:, t % 2 * D:(t % 2 + 1) * D],
                                 [(YT[j][:, k, t * S:(t + 1) * S], kept("aWv", KD)[:, k, :]) for k in range(KD)])
                    ins.then_inc(s["v1_ps"], 1)
                for j in range(PAIR):
                    n = PAIR * i + j
                    pe.wait_ge(s["xh3"], n + 1)
                    for k in range(KD):
                        for t in range(GB):
                            ins = turn(bank(j, k)[:, t * S:(t + 1) * S], XH[j][:, t, k * P:(k + 1) * P])
                    ins.then_inc(s["xT3_ps"], 1)
                for j in range(PAIR):
                    n = PAIR * i + j
                    pe.wait_ge(s["xT3"], n + 1)
                    for m in range(KD):
                        ins = mm(bank(j, m), [(kept("aWq", KD)[:, k, m * P:(m + 1) * P], xT[j][:, k, :]) for k in range(KD)])
                    ins.then_inc(s["q1_ps"], 1)
                pe.wait_ge(s["q1"], PAIR * i + PAIR)
                pe.wait_ge(s["v1"], PAIR * i + PAIR)
                for j in range(PAIR):
                    n = PAIR * i + j

                    def score(u):
                        unit = 2 * GB * n + u
                        bb, t = u // 2, u % 2
                        pe.wait_ge(s["kb"], unit + 1)
                        if j or u >= 2:
                            pe.wait_ge(s["sub"], unit - 1)
                        for h in range(2):
                            ins = mm(ps[:, 4 * (u % 2) + h, :], [(Q1[j][:, t, bb * S:(bb + 1) * S],
                                                                 KB[u % 2][:, 4 * h:4 * h + 4, :].rearrange("p h n -> p (h n)"))])
                        ins.then_inc(s["sc_ps"], 1)

                    def attend(u):
                        unit = 2 * GB * n + u
                        bb, t = u // 2, u % 2
                        pe.wait_ge(s["exp"], unit + 1)
                        if j or u:
                            pe.wait_ge(s["pt"], unit)
                        for h in range(HT8):
                            ins = turn(ps[:, 2 + h // 4, h % 4 * S:(h % 4 + 1) * S], PP[u % 2][:, h, :])
                        ins.then_inc(s["pt_ps"], 1)

                    def gather(u):
                        unit = 2 * GB * n + u
                        bb, t = u // 2, u % 2
                        pe.wait_ge(s["pt"], unit + 1)
                        if j or u >= 2:
                            pe.wait_ge(s["ot"], unit - 1)
                        for st in range(4):
                            out = ps[32 * st:32 * st + 32, 6 + u % 2, :]
                            mm(out[:, 0:S], [(V1[j][:, bb, o, 32 * (4 * t + st):32 * (4 * t + st) + 32], PQ[u % 2][:, 2 * st + o, :]) for o in range(2)])
                            ins = mm(out[:, S:2 * S], [(kept("ones_half", 2)[:, o, :], PQ[u % 2][:, 2 * st + o, :]) for o in range(2)])
                        ins.then_inc(s["ot_ps"], 1)

                    score(0)
                    for u in range(2 * GB):
                        if u + 1 < 2 * GB:
                            score(u + 1)
                        attend(u)
                        if u:
                            gather(u - 1)
                    gather(2 * GB - 1)
                pe.wait_ge(s["ot"], 2 * GB * PAIR * (i + 1))
                for j in range(PAIR):
                    n = PAIR * i + j
                    for m in range(H1 // P):
                        ins = mm(bank(j, m), [(kept("aW1", KD)[:, k, m * P:(m + 1) * P], OT[j][:, k, :]) for k in range(KD)])
                    ins.then_inc(s["f_ps"], 1)
                for j in range(PAIR):
                    n = PAIR * i + j
                    pe.wait_ge(s["f"], n + 1)
                    for t in range(GB):
                        ins = mm(bank(j, t // 2)[:, t % 2 * D:(t % 2 + 1) * D],
                                 [(HF[j][:, k, t * S:(t + 1) * S], kept("aW2", H1 // P)[:, k, :]) for k in range(H1 // P)])
                    ins.then_inc(s["y_ps"], 1)
                for j in range(PAIR):
                    n = PAIR * i + j
                    pe.wait_ge(s["xh4"], n + 1)
                    for k in range(KD):
                        for t in range(GB):
                            ins = turn(bank(j, 2 + k)[:, t * S:(t + 1) * S], XH[j][:, t, k * P:(k + 1) * P])
                    ins.then_inc(s["xT4_ps"], 1)
                for j in range(PAIR):
                    n = PAIR * i + j
                    pe.wait_ge(s["xT4"], n + 1)
                    for t in range(GB):
                        ins = mm(bank(j, 0)[:, t * NE:(t + 1) * NE], [(xT[j][:, k, t * S:(t + 1) * S], kept("gate", KD)[:, k, :]) for k in range(KD)])
                    ins.then_inc(s["gl_ps"], 1)
            pe.wait_ge(picks, 1)
            flat = picked.rearrange("p b e -> p (b e)")
            mm(ps[:, 0, 0:B * NE], [(kept("upper"), flat)])
            mm(ps[:, 1, 0:B * NE], [(ones, flat)]).then_inc(counted, 1)
            for n in range(NE // 2):
                pe.wait_ge(early_in[n], 16)
                pe.wait_ge(late_in[n], 16)
            pe.wait_ge(routed, 1)

            def turn_in(t, u, half):
                pe.wait_ge(xi_in[u], 16 * (half + 1))
                if not isinstance(t, int) or t:
                    pe.wait_ge(xt, t)
                for k in range(KD):
                    ins = turn(XT_PS[:, k * P:(k + 1) * P], XI[u][:, k * P:(k + 1) * P])
                ins.then_inc(xt_ps, 1)

            def gate_up(t, u):
                at = pe.value_load(e_id[0:1, bass.ds(t, 1)], min_val=0, max_val=NE - 1) * EXP_N
                pe.wait_ge(xt, t + 1)
                for g in range(2):
                    for k in range(KD):
                        ins = pe.matmul(ps[:, 2 * u + g, :], XIT[u][:, k, :], experts[:, bass.ds(at + (2 * k + g) * INTER, INTER)],
                                        start=(k == 0), stop=(k == KD - 1))
                ins.then_inc(gu_ps, 1)

            def turn_act(t, u):
                pe.wait_ge(act_ok, t + 1)
                for k in range(INTER // P):
                    ins = turn(ps[:, 7, k * P:(k + 1) * P], HA[u][:, k * P:(k + 1) * P])
                ins.then_inc(ha_ps, 1)

            def down(t, u):
                at = pe.value_load(e_id[0:1, bass.ds(t, 1)], min_val=0, max_val=NE - 1) * EXP_N
                pe.wait_ge(y_ok, t + 1)
                pe.wait_ge(ha, t + 1)
                for k in range(INTER // P):
                    ins = pe.matmul(Y_PS[u], HAT[u][:, k, :], experts[:, bass.ds(at + 2 * KD * INTER + k * D, D)],
                                    start=(k == 0), stop=(k == INTER // P - 1))
                ins.then_inc(y_ps, 1)

            def step(t, u, half):
                turn_in(t + 2, u, half + 1)
                gate_up(t + 1, 1 - u)
                down(t - 1, 1 - u)
                turn_act(t, u)

            turn_in(0, 0, 0)
            turn_in(1, 1, 0)
            gate_up(0, 0)
            turn_in(2, 0, 1)
            gate_up(1, 1)
            turn_act(0, 0)
            tiles_of(pe, step)
            gate_up(NT - 1, 0)
            down(NT - 3, 0)
            turn_act(NT - 2, 1)
            down(NT - 2, 1)
            turn_act(NT - 1, 0)
            down(NT - 1, 0)

        @block.vector
        def _(dve):
            settle = dve.drain

            def spread_of(j, src, width, name, scale=1.0, eps=EPS):
                for t in range(GB):
                    dve.bn_stats(stat[j][:, t, :], src[:, t, 0:width])
                settle()
                for t in range(GB):
                    dve.bn_aggr(mv[name][j][:, t, :], stat[j][:, t, :])
                settle()
                dve.tensor_scalar(var[name][j][:, :], mv[name][j][:, :, 1], scale, eps, ALU.mult, ALU.add).then_inc(s["var_" + name], 1)

            def norm(j, n, src, out, width, name):
                dve.wait_ge(s["rs_" + name], n + 1)
                for t in range(GB):
                    ins = dve.tensor_scalar(out[:, t, 0:width], src[:, t, 0:width], mv[name][j][:, t, 0:1], var[name][j][:, t:t + 1],
                                            ALU.subtract, ALU.mult)
                ins.then_inc(s[name], 1)

            dve.wait_ge(rows_in, 16)
            dve.wait_ge(fold_in, 16)
            dve.wait_ge(keep_in, 16)
            dve.tensor_tensor(slots[:, :, :], fold("slots"), row("slot_scale").unsqueeze(1).broadcast_to([P, KD, NSLOT]), ALU.mult)
            dve.tensor_scalar(inv_tau[:, :], row("tau"), -1.0, None, ALU.mult)
            dve.tensor_copy(b_rz[:, :], kept("bhh"))
            settle()
            dve.tensor_tensor(inv_tau[:, :], inv_tau[:, :], row("tau"), ALU.max)
            settle()
            dve.tensor_scalar(inv_tau[:, :], inv_tau[:, :], 0.1, None, ALU.add)
            settle()
            dve.tensor_reduce(slot_mean[:, :], slots[:, :, :], AXX, ALU.add)
            dve.reciprocal(inv_tau[:, :], inv_tau[:, :])
            dve.tensor_tensor(b_rz[:, 0:4], b_rz[:, 0:4], kept("bih")[:, 0:4], ALU.add)
            settle()
            dve.tensor_scalar(slot_mean[:, :], slot_mean[:, :], 1.0 / NSLOT, None, ALU.mult)
            dve.wait_ge(fold_ps, 1)
            for m in range(KD):
                dve.tensor_scalar(qk[:, m, :], ps[:, 0, m * D:(m + 1) * D], kept("ln1_g")[:, m:m + 1], None, ALU.mult)
                dve.tensor_scalar(vo[:, m, :], ps[:, 1, m * D:(m + 1) * D], kept("ln2_g")[:, m:m + 1], None, ALU.mult)
            dve.tensor_copy(fvo[:, :, :], ps[:, 3, :].rearrange("p (k n) -> p k n", k=KD))
            dve.tensor_tensor(u_col[:, :], ps[:, 2, 0:KD], kept("bq"), ALU.add)
            dve.tensor_tensor(w_col[:, :], ps[:, 2, 2:2 + KD], kept("bv"), ALU.add)
            settle()
            for k in range(KD):
                dve.tensor_scalar(spread[:, k, :], ones, w_col[:, k:k + 1], None, ALU.mult)
                ins = dve.tensor_scalar(spread[:, 2 + k, :], ones, kept("fbv")[:, k:k + 1], None, ALU.mult)
            settle()
            dve.tensor_copy(rt[0][:, 0:1], w_col[:, 0:1]).then_inc(fold_ok, 1)
            dve.wait_ge(fold_ps, 2)
            dve.tensor_tensor(q_col[:, :], ps[:, 4, 0:KD], kept("ln2_g"), ALU.mult)
            dve.tensor_tensor(b1_col[:, :], ps[:, 4, 4:5], kept("b1"), ALU.add)
            dve.tensor_tensor(vo_row[:, :], ps[:, 5, 0:D], row("bo"), ALU.add)
            dve.tensor_tensor(fvo_row[:, :], ps[:, 5, D:2 * D], row("fbo"), ALU.add)
            dve.tensor_tensor(gh[:, :, :], ps[:, 6, 0:6 * NSLOT].rearrange("p (m n) -> p m n", m=6),
                              b_rz[:, :].unsqueeze(2).broadcast_to([P, 6, NSLOT]), ALU.add)
            settle()
            dve.tensor_copy(rt[0][:, 0:1], w_col[:, 0:1]).then_inc(fold_ok, 1)
            settle()

            with dve.Fori(0, NG // PAIR) as i:
                for j in range(PAIR):
                    n = PAIR * i + j
                    dve.wait_ge(x_in[j], 16 * (i + 1))
                    spread_of(j, X[j], D, "xh", 1.0 + EPS, EPS * EPS)
                    settle()
                    dve.wait_ge(c_in[j], 16 * (i + 1))
                    spread_of(j, C[j], DC, "ch")
                    norm(j, n, X[j], XH[j], D, "xh")
                    norm(j, n, C[j], CH[j], DC, "ch")
                    settle()
                for j in range(PAIR):
                    n = PAIR * i + j
                    dve.wait_ge(s["cT_ps"], n + 1)
                    dve.tensor_copy(CT[j], ps[:, 4 * j + 2:4 * j + 4, :]).then_inc(s["cT"], 1)
                for j in range(PAIR):
                    n = PAIR * i + j
                    dve.wait_ge(s["v_ps"], n + 1)
                    dve.tensor_tensor(V[j], ps[:, 4 * j + 2:4 * j + 4, :].rearrange("p t (h n) -> p (t h) n", h=2),
                                      vo_row[:, :].unsqueeze(1).broadcast_to([P, GB, D]), ALU.add).then_inc(s["v"], 1)
                for j in range(PAIR):
                    n = PAIR * i + j
                    dve.wait_ge(s["s_ps"], n + 1)
                    dve.tensor_reduce(nm[j][:, :], bank(j, 0).rearrange("p (t n) -> p t n", t=GB), AXX, ALU.max)
                    settle()
                    dve.tensor_scalar(nm[j][:, :], nm[j][:, :], -float(D) ** -0.5, None, ALU.mult).then_inc(s["nm"], 1)
                for j in range(PAIR):
                    n = PAIR * i + j
                    dve.wait_ge(s["p"], n + 1)
                    dve.reciprocal(sm[j][:, :], sm[j][:, :])
                    settle()
                    dve.wait_ge(s["o_ps"], n + 1)
                    for t in range(GB):
                        dve.scalar_tensor_tensor(X[j][:, t, :], bank(j, 2 + t // 2)[:, t % 2 * D:(t % 2 + 1) * D],
                                                 sm[j][:, t:t + 1], X[j][:, t, :], ALU.mult, ALU.add)
                    settle()
                    spread_of(j, X[j], D, "xh2")
                    settle()
                for j in range(PAIR):
                    norm(j, PAIR * i + j, X[j], XH[j], D, "xh2")
                settle()
                for j in range(PAIR):
                    n = PAIR * i + j
                    dve.wait_ge(s["lg_ps"], n + 1)
                    dve.tensor_tensor(LG[j], bank(j, 3)[:, 0:GB * NSLOT].rearrange("p (t n) -> p t n", t=GB),
                                      row("b2").unsqueeze(1).broadcast_to([P, GB, NSLOT]), ALU.add)
                    settle()
                    for t in range(GB):
                        dve.max(m8[j][:, t, :], LG[j][:, t, :])
                    settle()
                    for t in range(GB):
                        dve.match_replace(LK[j][:, t, :], m8[j][:, t, :], LG[j][:, t, :], NEG)
                    dve.tensor_scalar(nm[j][:, :], m8[j][:, :, 0], inv_tau[:, 0:1], -1.0, ALU.mult, ALU.mult).then_inc(s["top"], 1)
                for j in range(PAIR):
                    n = PAIR * i + j
                    settle()
                    dve.tensor_tensor(MK[j], LK[j], LG[j], ALU.is_lt)
                    settle()
                    dve.wait_ge(s["ex"], n + 1)
                    dve.tensor_tensor(EX[j], EX[j], MK[j], ALU.mult)
                    settle()
                    dve.tensor_reduce(sm[j][:, :], EX[j], AXX, ALU.add)
                    settle()
                    dve.reciprocal(sm[j][:, :], sm[j][:, :])
                    settle()
                    dve.tensor_tensor(AL[j], EX[j], sm[j][:, :].unsqueeze(2).broadcast_to([P, GB, NSLOT]), ALU.mult).then_inc(s["al"], 1)
                for j in range(PAIR):
                    n = PAIR * i + j
                    dve.wait_ge(s["si_ps"], n + 1)
                    dve.tensor_scalar(RW[j], bank(j, 2)[:, 0:256], 1e-8, None, ALU.add)
                    settle()
                    dve.reciprocal(RW[j], RW[j])
                    settle()
                    dve.tensor_tensor(GI[j], bank(j, 1).rearrange("p (k n) -> p k n", k=KD),
                                      RW[j].unsqueeze(1).broadcast_to([P, KD, 256]), ALU.mult).then_inc(s["gi"], 1)
                for j in range(PAIR):
                    n = PAIR * i + j
                    dve.wait_ge(s["gx_ps"], n + 1)
                    for g, o in enumerate((0, 3)):
                        for k in range(KD):
                            ins = dve.tensor_tensor(RZ[j][:, g, k * 256:(k + 1) * 256].rearrange("p (t n) -> p t n", t=GB),
                                                    bank(j, o)[:, k * 256:(k + 1) * 256].rearrange("p (t n) -> p t n", t=GB),
                                                    gh[:, g * KD + k, :].unsqueeze(1).broadcast_to([P, GB, NSLOT]), ALU.add)
                    ins.then_inc(s["rz"], 1)
                for j in range(PAIR):
                    n = PAIR * i + j
                    dve.wait_ge(s["rz_act"], n + 1)
                    for k in range(KD):
                        dve.tensor_tensor(NN[j][:, k, :].rearrange("p (t n) -> p t n", t=GB),
                                          RZ[j][:, 0, k * 256:(k + 1) * 256].rearrange("p (t n) -> p t n", t=GB),
                                          gh[:, 4 + k, :].unsqueeze(1).broadcast_to([P, GB, NSLOT]), ALU.mult)
                    settle()
                    dve.tensor_tensor(NN[j], NN[j], bank(j, 1).rearrange("p (k n) -> p k n", k=KD), ALU.add).then_inc(s["n_pre"], 1)
                for j in range(PAIR):
                    n = PAIR * i + j
                    dve.wait_ge(s["n_act"], n + 1)
                    for k in range(KD):
                        dve.tensor_tensor(DF[j][:, k, :].rearrange("p (t n) -> p t n", t=GB),
                                          slots[:, k, :].unsqueeze(1).broadcast_to([P, GB, NSLOT]),
                                          NN[j][:, k, :].rearrange("p (t n) -> p t n", t=GB), ALU.subtract)
                    settle()
                    dve.tensor_tensor(DF[j], DF[j], RZ[j][:, 1, :].rearrange("p (k n) -> p k n", k=KD), ALU.mult)
                    settle()
                    dve.tensor_tensor(SN[j], DF[j], NN[j], ALU.add).then_inc(s["sn"], 1)
                for j in range(PAIR):
                    n = PAIR * i + j
                    dve.wait_ge(s["sv_ps"], n + 1)
                    dve.tensor_tensor(SV[j], bank(j, 2).rearrange("p (h n) -> p h n", h=2),
                                      fvo_row[:, :].unsqueeze(1).broadcast_to([P, 2, D]), ALU.add).then_inc(s["sv"], 1)
                for j in range(PAIR):
                    n = PAIR * i + j
                    dve.wait_ge(s["fo_ps"], n + 1)
                    dve.tensor_tensor(X[j][:, :, :], X[j][:, :, :], ps[:, 4 * j:4 * j + 2, :].rearrange("p t (h n) -> p (t h) n", h=2), ALU.add)
                    settle()
                    spread_of(j, X[j], D, "xh3")
                    settle()
                for j in range(PAIR):
                    norm(j, PAIR * i + j, X[j], XH[j], D, "xh3")
                settle()
                for j in range(PAIR):
                    n = PAIR * i + j
                    dve.wait_ge(s["k_ps"], n + 1)
                    for k in range(KD):
                        ins = dve.tensor_scalar(KT[j][:, k, :], bank(j, 2 + k), kept("abk")[:, k:k + 1], None, ALU.add)
                    ins.then_inc(s["k"], 1)
                for j in range(PAIR):
                    n = PAIR * i + j
                    dve.wait_ge(s["v1_ps"], n + 1)
                    dve.wait_ge(v1_zero, PAIR)
                    for t in range(GB):
                        for o in range(2):
                            half = lambda v: v.rearrange("p (h n) -> p h n", n=32)[:, :, o * HD:(o + 1) * HD]
                            ins = dve.tensor_tensor(half(V1[j][:, t, o, :]), half(bank(j, 2 + t // 2)[:, t % 2 * D:(t % 2 + 1) * D]),
                                                    half(row("abv")), ALU.add)
                    ins.then_inc(s["v1"], 1)
                for j in range(PAIR):
                    n = PAIR * i + j

                    def shift(u):
                        unit = 2 * GB * n + u
                        sc = ps[:, 4 * (u % 2):4 * (u % 2) + 2, :].rearrange("p t (h n) -> p (t h) n", h=4)
                        dve.wait_ge(s["sc_ps"], unit + 1)
                        dve.tensor_reduce(mx[u % 2][:, :], sc, AXX, ALU.max)
                        settle()
                        if j or u >= 2:
                            dve.wait_ge(s["pt_ps"], unit - 1)
                        dve.tensor_tensor(PP[u % 2], sc, mx[u % 2][:, :].unsqueeze(2).broadcast_to([P, HT8, S]), ALU.subtract).then_inc(s["sub"], 1)

                    def divide(u):
                        unit = 2 * GB * n + u
                        bb, t = u // 2, u % 2
                        dve.wait_ge(s["ot_ps"], unit + 1)
                        dve.reciprocal(rc[u % 2][:, :], ps[:, 6 + u % 2, S:2 * S])
                        settle()
                        dve.tensor_tensor(OT[j][:, t, bb * S:(bb + 1) * S], ps[:, 6 + u % 2, 0:S], rc[u % 2][:, :], ALU.mult).then_inc(s["ot"], 1)

                    for u in range(2 * GB):
                        shift(u)
                        if u >= 2:
                            divide(u - 2)
                    divide(2 * GB - 2)
                    divide(2 * GB - 1)
                for j in range(PAIR):
                    n = PAIR * i + j
                    dve.wait_ge(s["xb"], n + 1)
                    dve.wait_ge(s["y_ps"], n + 1)
                    dve.tensor_tensor(X[j][:, :, :], X[j][:, :, :], ps[:, 4 * j:4 * j + 2, :].rearrange("p t (h n) -> p (t h) n", h=2), ALU.add)
                    settle()
                    spread_of(j, X[j], D, "xh4")
                    settle()
                for j in range(PAIR):
                    norm(j, PAIR * i + j, X[j], XH[j], D, "xh4")
                settle()
                for j in range(PAIR):
                    n = PAIR * i + j
                    dve.wait_ge(stored[j], 32 * (i + 1))
                    dve.wait_ge(s["gl_ps"], n + 1)
                    dve.tensor_copy(gl[:, bass.ds(n * GB, GB), :], bank(j, 0)[:, 0:GB * NE].rearrange("p (t n) -> p t n", t=GB)).then_inc(through[j], 1)
            settle()
            def over(v, n):
                return v.unsqueeze(2).broadcast_to([P, B, n])

            def ranks(v, n, before, out):
                one, two_ = (t[:, 0:B * n * n].rearrange("p (b e o) -> p b e o", b=B, e=n) for t in (cmp1, cmp2))
                other, own = v.unsqueeze(2).broadcast_to([P, B, n, n]), v.unsqueeze(3).broadcast_to([P, B, n, n])
                dve.tensor_tensor(one, other, own, ALU.is_gt)
                dve.tensor_tensor(two_, other, own, ALU.is_equal)
                settle()
                dve.tensor_tensor(two_, two_, kept(before, n).unsqueeze(1).broadcast_to([P, B, n, n]), ALU.mult)
                settle()
                dve.tensor_tensor(one, one, two_, ALU.add)
                settle()
                dve.tensor_reduce(out, one, AXX, ALU.add)
                settle()

            dve.tensor_reduce(g_max, gl[:, :, :], AXX, ALU.max)
            settle()
            dve.tensor_tensor(prob, gl[:, :, :], over(g_max, NE), ALU.subtract).then_inc(g_diff, 1)
            dve.wait_ge(g_exp, 1)
            dve.tensor_reduce(g_max, prob, AXX, ALU.add)
            settle()
            dve.reciprocal(g_max, g_max)
            settle()
            dve.tensor_tensor(prob, prob, over(g_max, NE), ALU.mult)
            settle()
            in_groups = lambda v: v.rearrange("p b (g e) -> p b g e", g=NGRP)
            dve.tensor_reduce(g_top, in_groups(prob), AXX, ALU.max)
            settle()
            ranks(g_top, NGRP, "before_group", r4)
            dve.tensor_scalar(g_ok, r4, float(NPICK), None, ALU.is_lt)
            settle()
            dve.tensor_tensor(in_groups(masked), in_groups(prob), g_ok.unsqueeze(3).broadcast_to([P, B, NGRP, NE // NGRP]), ALU.mult)
            settle()
            ranks(masked, NE, "before_expert", work)
            dve.tensor_scalar(picked, work, float(NPICK), None, ALU.is_lt).then_inc(picks, 1)
            dve.tensor_scalar(first, work, 0.0, None, ALU.is_equal)
            dve.tensor_scalar(second, work, 1.0, None, ALU.is_equal)
            settle()
            dve.tensor_tensor(prob, masked, picked, ALU.mult)
            settle()
            dve.tensor_reduce(w_sum, prob, AXX, ALU.add)
            settle()
            dve.reciprocal(w_sum, w_sum)
            settle()
            dve.tensor_tensor(XA[:, :, D + 1:D + 1 + NE], prob, over(w_sum, NE), ALU.mult)
            dve.memset(XA[:, :, D + 1 + NE:ROW], 0.0)
            dve.tensor_copy(XA[:, :, D:D + 1], kept("row_no").unsqueeze(2)).then_inc(xa_ok, 1)
            dve.wait_ge(counted, 1)
            dve.tensor_copy(total, ps[:, 1, 0:B * NE].rearrange("p (b e) -> p b e", b=B))
            settle()
            here, there, step = total, sums, 1
            while step < B:
                dve.tensor_copy(there[:, 0:step, :], here[:, 0:step, :])
                dve.tensor_tensor(there[:, step:B, :], here[:, step:B, :], here[:, 0:B - step, :], ALU.add)
                settle()
                here, there, step = there, (sums2 if there is sums else sums), 2 * step
            c816 = cmp1[:, 0:NE * B].rearrange("p (e t) -> p e t", e=NE)
            dve.tensor_tensor(c816, here[:, B - 1, :].unsqueeze(2).broadcast_to([P, NE, B]),
                              kept("tile_start").unsqueeze(1).broadcast_to([P, NE, B]), ALU.is_gt)
            settle()
            dve.tensor_reduce(n_tiles, c816, AXX, ALU.add)
            settle()
            c88 = cmp1[:, 0:NE * NE].rearrange("p (e o) -> p e o", e=NE)
            dve.tensor_tensor(c88, kept("before_expert", NE), n_tiles.unsqueeze(1).broadcast_to([P, NE, NE]), ALU.mult)
            settle()
            dve.tensor_reduce(t_off, c88, AXX, ALU.add)
            settle()
            dve.tensor_tensor(t_end, t_off, n_tiles, ALU.add)
            dve.tensor_scalar(t_off, t_off, float(P), None, ALU.mult)
            settle()
            ct8 = cmp1[:, 0:NT * NE].rearrange("p (t e) -> p t e", t=NT)
            dve.tensor_tensor(ct8, t_end.unsqueeze(1).broadcast_to([P, NT, NE]), kept("tile_no").unsqueeze(2).broadcast_to([P, NT, NE]), ALU.is_le)
            dve.tensor_tensor(place, here, total, ALU.subtract)
            settle()
            dve.tensor_reduce(e_flt, ct8, AXX, ALU.add)
            dve.tensor_tensor(place, place, ps[:, 0, 0:B * NE].rearrange("p (b e) -> p b e", b=B), ALU.add)
            settle()
            dve.tensor_scalar(e_id[:, :], e_flt, float(NE - 1), None, ALU.min)
            dve.tensor_scalar(e_min, e_flt, float(NE - 1), None, ALU.min)
            dve.tensor_tensor(place, place, t_off.unsqueeze(1).broadcast_to([P, B, NE]), ALU.add)
            settle()
            for k, which in enumerate((first, second)):
                dve.tensor_tensor(work, place, which, ALU.mult)
                settle()
                dve.tensor_reduce(pos[:, k, :], work, AXX, ALU.add)
                settle()
            dve.tensor_copy(pos_i[:, :, :], pos).then_inc(routed, 1)

            dve.tensor_tensor(tile_hot[:, :, :], e_min.unsqueeze(2).broadcast_to([P, NT, NE]),
                              kept("expert_no").unsqueeze(1).broadcast_to([P, NT, NE]), ALU.is_equal)
            settle()

            def pick(t, u, half):
                dve.wait_ge(xi_in[u], 16 * (half + 1))
                dve.tensor_tensor(row_w8[u][:, :], tile_hot[:, bass.ds(t, 1), :].rearrange("p t e -> p (t e)"), XI[u][:, D + 1:D + 1 + NE], ALU.mult)
                dve.tensor_copy(row_no[:, bass.ds(t, 1)], XI[u][:, D:D + 1])
                settle()
                dve.tensor_reduce(row_w[u][:, :], row_w8[u][:, :], AXX, ALU.add).then_inc(picked_ok, 1)

            def gated(t, u):
                dve.wait_ge(silu, t + 1)
                dve.wait_ge(picked_ok, t + 1)
                dve.scalar_tensor_tensor(HA[u], HA[u], row_w[u][:, 0:1], ps[:, 2 * u + 1, :], ALU.mult, ALU.mult).then_inc(act_ok, 1)

            def turned(t, u):
                dve.wait_ge(ha_ps, t + 1)
                dve.tensor_copy(HAT[u], ps[:, 7, :].rearrange("p (k n) -> p k n", k=INTER // P)).then_inc(ha, 1)

            def number(t, u):
                dve.wait_ge(turns, t + 1)
                dve.tensor_copy(row_i[u][:, :], row_no[:, bass.ds(t, 1)]).then_inc(no_ok, 1)

            def step(t, u, half):
                pick(t + 2, u, half + 1)
                gated(t + 1, 1 - u)
                turned(t, u)
                number(t - 1, 1 - u)

            pick(0, 0, 0)
            pick(1, 1, 0)
            gated(0, 0)
            pick(2, 0, 1)
            gated(1, 1)
            turned(0, 0)
            tiles_of(dve, step)
            gated(NT - 1, 0)
            for t in range(NT - 3, NT):
                if t > NT - 3:
                    turned(t, t % 2)
                number(t, t % 2)


def packed(parts, width, arrays):
    out = np.zeros((P, width), np.float32)
    for name, (at, n) in parts.items():
        out[:, at:at + n] = np.reshape(arrays[name], (P, n))
    return out


def tiles(w):
    k = -(-w.shape[0] // P)
    full = np.zeros((k * P, w.shape[1]), w.dtype)
    full[:w.shape[0]] = w
    return full.reshape(k, P, w.shape[1]).transpose(1, 0, 2)


def wide(w, n):
    full = np.zeros((w.shape[0], n), w.dtype)
    full[:, :w.shape[1]] = w
    return full


def kernel(**inputs):
    import concourse.bacc as bacc
    from concourse.bass_utils import run_bass_kernel_spmd

    v = {k: np.asarray(a) for k, a in inputs.items()}
    A, Fn, L, M = (lambda n: v["L0_xattn_" + n]), (lambda n: v["L0_ffn_" + n]), (lambda n: v["L1_xattn_" + n]), (lambda n: v["L1_ffn_" + n])
    col = lambda w: tiles(w.reshape(-1, 1))[:, :, 0]
    half = np.zeros((P, 2, 32), np.float32)
    half[:, 0, :HD] = 1
    half[:, 1, HD:] = 1
    keep = packed(KEEP, KEEP_N, {
        "ident": np.eye(P, dtype=np.float32), "ones": np.ones((P, P), np.float32), "ones_half": half,
        "head_mask": np.kron(np.eye(HT8, dtype=np.float32), np.ones((HD, 1), np.float32)),
        "half_mask": np.kron(np.eye(2, dtype=np.float32), np.ones((NSLOT, 1), np.float32)),
        "w1": tiles(Fn("w1").T), "w2": Fn("w2").T, "wih": tiles(Fn("gru_wih").T),
        "aWq": tiles(L("Wq")), "aWk": tiles(L("Wk")), "aWv": tiles(L("Wv")), "aW1": tiles(L("W1")), "aW2": tiles(L("W2")),
        "gate": tiles(M("gate_w").T),
        "upper": np.triu(np.ones((P, P), np.float32), 1),
        "before_group": np.tile(np.tril(np.ones((NGRP, NGRP), np.float32), -1).reshape(1, -1), (P, 1)),
        "before_expert": np.tile(np.tril(np.ones((NE, NE), np.float32), -1).reshape(1, -1), (P, 1)),
        "tile_start": np.tile(P * np.arange(B, dtype=np.float32), (P, 1)), "tile_no": np.tile(np.arange(NT, dtype=np.float32), (P, 1)),
        "expert_no": np.tile(np.arange(NE, dtype=np.float32), (P, 1)),
        "row_no": np.arange(B * S, dtype=np.float32).reshape(B, S).T, "spare_no": B * S + np.arange(P, dtype=np.float32),
        "ln1_g": col(A("ln1_g")), "ln1_b": col(A("ln1_b")), "ln2_g": col(A("ln2_g")), "ln2_b": col(A("ln2_b")),
        "bq": col(A("bq")), "bv": col(A("bv")), "b1": col(Fn("b1")), "bih": col(Fn("gru_bih")), "bhh": col(Fn("gru_bhh")),
        "fbv": col(Fn("bv")), "abq": col(L("bq")), "abk": col(L("bk")), "ab1": col(L("b1")),
    })
    fold = packed(FOLD, FOLD_N, {
        "WqT": tiles(A("Wq").T), "WkT": tiles(wide(A("Wk").T, D)), "Wq": tiles(A("Wq")), "Wo": tiles(A("Wo")),
        "WvT": tiles(wide(A("Wv").T, D)), "Wv": tiles(A("Wv")), "whh": tiles(Fn("gru_whh").T),
        "fwv": tiles(Fn("wv")), "fwoT": tiles(Fn("wo").T), "slots": tiles(Fn("slot_init").T),
    })
    rows = np.zeros((ROWS_N,), np.float32)
    for name, a in (("bo", A("bo")), ("slot_scale", Fn("slot_scale")), ("b2", Fn("b2")), ("tau", Fn("tau")),
                    ("fbo", Fn("bo")), ("abv", L("bv")), ("ab2", L("b2"))):
        at, n = ROWS[name]
        rows[at:at + n] = a.reshape(-1)
    ctx = v["ctx_768"]
    ctxT = tiles(ctx.reshape(B * S, DC).T).reshape(P, KD, NG, GT).transpose(2, 0, 1, 3)
    experts = np.concatenate([
        M("w13_weight").transpose(0, 2, 1).reshape(NE, KD, P, 2 * INTER).transpose(0, 2, 1, 3).reshape(NE, P, -1),
        M("w2_weight").transpose(0, 2, 1).reshape(NE, INTER // P, P, D).transpose(0, 2, 1, 3).reshape(NE, P, -1)], axis=2)
    arrays = {"x": v["x"], "ctx": ctx, "ctxT": ctxT, "keep": keep, "fold": fold, "rows": rows, "experts": experts}

    nc = bacc.Bacc("TRN2", target_bir_lowering=False, num_devices=1)
    args, feed = [], {}
    for name, a in arrays.items():
        a = np.ascontiguousarray(a)
        feed["in_" + name] = a
        args.append(nc.dram_tensor("in_" + name, a.shape, mybir.dt.from_np(a.dtype), kind="ExternalInput").ap())
    out = nc.dram_tensor("out_x", (B, S, D), F32, kind="ExternalOutput").ap()
    scratch = [nc.dram_tensor(name, shape, F32, kind="Internal").ap()
               for name, shape in (("rows3", (B * S + P, D)), ("normed3", (B, S, D)), ("dispatched", (NT * P, ROW)))]
    build(nc, *args, *scratch, out)
    r = run_bass_kernel_spmd(nc, [feed], core_ids=[0])
    return r.results[0]["out_x"]
```

```python
from contextlib import ExitStack

import numpy as np
import concourse.bass as bass
from concourse import mybir

F32 = mybir.dt.float32
ALU = mybir.AluOpType
ACT = mybir.ActivationFunctionType
AXX = mybir.AxisListType.X

P = 128
B, S, D = 16, 128, 256
DC = 192
KD = D // P
GB = 4
GT = GB * S
NG = B // GB
NSLOT, TOPK = 64, 8
NH, HD = 16, 16
HT8 = P // HD
HT4 = HT8 // 2
H1 = 2 * D
NE, INTER = 8, 512
NGRP, NPICK = 4, 2
ROW = D + NE
NT = B * S * NPICK // P + NE - 1
EPS = 1e-5
NEG = -3.0e38


def columns(parts):
    at, out = 0, {}
    for name, n in parts:
        out[name] = (at, n)
        at += n
    return out, at


KEEP, KEEP_N = columns([
    ("ident", P), ("ones", P), ("ones_half", 2 * 32), ("head_mask", HT4), ("half_mask", 2),
    ("ln1_g", KD), ("ln1_b", KD), ("ln2_g", KD), ("ln2_b", KD), ("bq", KD), ("bv", KD),
    ("b1", 1), ("bih", 6), ("bhh", 6), ("fbv", KD), ("abq", KD), ("abk", KD), ("abv", KD), ("ab1", H1 // P), ("row_next", 1), ("hole_row", 1),
    ("w1", 4 * P), ("w2", NSLOT), ("wih", KD * 3 * D), ("aWq", KD * D), ("aWk", KD * D), ("aWv", KD * D),
    ("aW1", KD * H1), ("aW2", H1 // P * D), ("gate", KD * NE),
    ("upper", P), ("col_no", P), ("before_group", NGRP * NGRP), ("before_expert", NE * NE), ("tile_start", B), ("tile_no", NT), ("tile_first", NT), ("expert_no", NE),
])
KEEP_A = KEEP["w1"][0]
FOLD, FOLD_N = columns([
    ("WqT", KD * D), ("WkT", KD * D), ("Wq", KD * D), ("Wo", KD * D), ("WvT", KD * D), ("Wv", KD * D),
    ("whh", KD * 3 * D), ("fwv", KD * D), ("fwoT", KD * D), ("slots", KD * NSLOT),
])
FOLD_A = FOLD["Wo"][0]
ROWS, ROWS_N = columns([
    ("bo", D), ("slot_scale", NSLOT), ("b2", NSLOT), ("tau", 1), ("fbo", D), ("ab2", D),
])


def build(nc, x_d, ctx_d, ctxT_d, keep_d, fold_d, rows_d, experts_d, xh_d, out_d):
    with ExitStack() as stack:
        def sb(name, shape, dt=F32):
            return stack.enter_context(nc.sbuf_tensor(name, shape, dt))

        def sem(name):
            return stack.enter_context(nc.semaphore(name))

        ps = stack.enter_context(nc.psum_tensor("ps", [P, 8, 512], F32))

        EXP_N = KD * 2 * INTER + INTER // P * D
        experts = sb("experts", [P, NE * EXP_N])
        carve_at = [NE // 2 * EXP_N]

        def carve(n):
            at = carve_at[0]
            carve_at[0] += n
            assert carve_at[0] <= NE * EXP_N
            return experts[:, at:at + n]

        keep = sb("keep", [P, KEEP_N])
        rows = sb("rows", [P, ROWS_N])
        ring = sb("ring", [P, 6 * 1024])

        def kept(name, t=1):
            at, n = KEEP[name]
            v = keep[:, at:at + n]
            return v.rearrange("p (t n) -> p t n", t=t) if t > 1 else v

        def fold(name, t=KD):
            at, n = FOLD[name]
            return ring[:, at:at + n].rearrange("p (t n) -> p t n", t=t)

        def row(name):
            at, n = ROWS[name]
            return rows[:, at:at + n]

        assert FOLD_N <= 6 * 1024
        ident, ones = kept("ident"), kept("ones")

        qk = sb("qk", [P, KD, D])
        vo = sb("vo", [P, KD, D])
        vo_row = sb("vo_row", [P, D])
        q_col = sb("q_col", [P, KD])
        u_col = sb("u_col", [P, KD])
        w_col = sb("w_col", [P, KD])
        spread = sb("spread", [P, 2 * KD, P])
        slots = sb("slots", [P, KD, NSLOT])
        slot_mean = sb("slot_mean", [P, KD])
        b1_col = sb("b1_col", [P, 1])
        inv_tau = sb("inv_tau", [P, 1])
        ab1_col = sb("ab1_col", [P, H1 // P])
        b_rz = sb("b_rz", [P, 6])
        gh = sb("gh", [P, 6, NSLOT])
        fvo = sb("fvo", [P, KD, D])
        fvo_row = sb("fvo_row", [P, D])

        a, b, c, d, e, f, XT0, X0, XH0 = (carve(1024) for _ in range(9))
        KT, Q1, YT = (carve(1024).rearrange("p (t n) -> p t n", t=KD) for _ in range(3))
        X0, XH0 = (v.rearrange("p (t n) -> p t n", t=GB) for v in (X0, XH0))
        X1, XH3, X4, XH4 = (sb(t, [P, GB, D]) for t in ("X1", "XH3", "X4", "XH4"))
        V1 = sb("V1", [P, GB, 2, D])
        spare_hf = sb("HF", [P, H1 // P * GT])
        spare_ot = sb("OT", [P, KD * GT])

        def split(v, t):
            return v.rearrange("p (t n) -> p t n", t=t)

        HF, OT, xT0 = split(spare_hf[:, :], H1 // P), split(spare_ot[:, :], KD), split(XT0, KD)
        xT1 = sb("xT1", [P, KD, GT])
        C = split(a[:, 0:GB * DC], GB)
        CH, CT, Q, V = split(b, GB), split(c, KD), split(d, KD), split(e, GB)
        PR, PT = split(f[:, 0:512], GB), split(f[:, 512:1024], GB)
        HT = f[:, 0:512]
        LG, LK, EX, MK = (split(a[:, 256 * n:256 * n + 256], GB) for n in range(4))
        AL, RW = split(b[:, 0:256], GB), b[:, 256:512]
        AT = b[:, 512:1024].rearrange("p (h o n) -> p h o n", h=2, o=2)
        GI, NN = split(c[:, 0:512], KD), split(c[:, 512:1024], KD)
        RZ = split(d, 2)
        DF, SN = split(e[:, 0:512], KD), split(e[:, 512:1024], KD)
        SV = split(f[:, 512:1024], 2)
        KB = [split(ring[:, 1024 * n:1024 * n + HT4 * S], HT4) for n in range(2)]
        PP = [split(ring[:, 1024 * n:1024 * n + 1024], HT8) for n in range(2, 4)]
        PQ = [split(ring[:, 1024 * n:1024 * n + 1024], HT8) for n in range(4, 6)]

        norms = ("xh", "ch", "xh2", "xh3", "xh4")
        stat = {m: sb(f"stat_{m}", [P, GB, 6]) for m in norms}
        mv = {m: sb(f"mv_{m}", [P, GB, 2]) for m in norms}
        var = {m: sb(f"var_{m}", [P, GB]) for m in norms}
        minus_half = sb("minus_half", [P, GB])
        mark = sb("mark", [P, 1])
        nm = sb("nm", [P, GB])
        sm = sb("sm", [P, GB])
        m8 = sb("m8", [P, GB, 8])
        mx = [sb(f"mx{n}", [P, HT8]) for n in range(2)]
        rc = [sb(f"rc{n}", [P, P]) for n in range(2)]
        gl = sb("gl", [P, B, NE])

        PICKS = NPICK * B
        BF16 = mybir.dt.bfloat16
        hot = ring[:, 0:PICKS * P // 2].bitcast(BF16).rearrange("p (k n) -> p k n", k=PICKS)
        hot_tile = ring[:, PICKS * P // 2:PICKS * P // 2 + PICKS * NT].bitcast(BF16).rearrange("p (k v t) -> p k v t", k=PICKS, v=2)
        cmp1, cmp2 = (V1[:, 2 * h:2 * h + 2, :, :].rearrange("p t o n -> p (t o n)") for h in range(2))
        spare = ([XH3[:, n // 2, n % 2 * P:(n % 2 + 1) * P] for n in range(2 * GB)]
                 + [ring[:, 4864 + P * n:4864 + P * (n + 1)] for n in range(2 * GB)])
        prob, masked, first, second, picked, sums, sums2, total, place, work = (v.rearrange("p (b e) -> p b e", b=B) for v in spare[:10])
        one_hot = ring[:, 4096:4096 + PICKS * NT // 2].bitcast(BF16).rearrange("p (k t) -> p k t", k=PICKS)
        g_top, r4, g_ok = (v[:, 0:B * NGRP].rearrange("p (b g) -> p b g", b=B) for v in spare[10:13])
        cols = spare[13]
        g_max, n_tiles, t_off, t_end, e_flt = cols[:, 0:B], cols[:, B:B + NE], cols[:, 24:32], cols[:, 32:40], cols[:, 40:40 + NT]
        pos = spare[14][:, 0:2 * B].rearrange("p (k b) -> p k b", k=2)
        w_sum = spare[14][:, 2 * B:3 * B]
        col_at, tile_at = (spare[14][:, n * B:(n + 2) * B] for n in (3, 5))
        hole = spare[15][:, NT:2 * NT]
        e_min = spare[15][:, 0:NT]
        at_i = sb("at_i", [P, PICKS], mybir.dt.int32)
        e_id = sb("e_id", [P, NT], mybir.dt.int32)
        blank = sb("blank", [P, ROW])
        tile_hot = sb("tile_hot", [P, NT, NE])
        row_no = sb("row_no", [P, NT + 2], mybir.dt.int32)
        row_w = [sb(f"row_w{u}", [P, 1]) for u in range(2)]
        row_w8 = [sb(f"row_w8{u}", [P, NE]) for u in range(2)]
        row_in, row_out = ([sb(f"{t}{u}", [P, 1], mybir.dt.int32) for u in range(2)] for t in ("row_in", "row_out"))
        at = KEEP["wih"][0]
        assert KEEP["aW2"][0] + KEEP["aW2"][1] - at >= 2 * (ROW + D + 2 * INTER)
        XI = [keep[:, at + ROW * n:at + ROW * (n + 1)] for n in range(2)]
        at += 2 * ROW
        XIT = [keep[:, at + D * n:at + D * n + D].rearrange("p (k n) -> p k n", k=KD) for n in range(2)]
        at += 2 * D
        HA = [keep[:, at + INTER * n:at + INTER * n + INTER] for n in range(2)]
        HAT = [keep[:, at + INTER * n:at + INTER * n + INTER].rearrange("p (k n) -> p k n", k=INTER // P) for n in range(2, 4)]
        YO = [spare_ot[:, D * n:D * n + D] for n in range(2)]

        keep_in, fold_in, rows_in = sem("keep_in"), sem("fold_in"), sem("rows_in")
        keep_in2, fold_in2 = sem("keep_in2"), sem("fold_in2")
        x_in, c_in, y_in, stored = (sem(t) for t in ("x_in", "c_in", "y_in", "stored"))
        names = ("xh xv ch ch_pad xT_ps xT cT_ps cT q_ps q v_ps v s_ps nm p pT_ps pT o_ps "
                 "xh2 xT2_ps xT2 h_ps h lg_ps top ex al aT_ps aT ws_ps si_ps gi gx_ps rz rz_act n_pre n_act sn sv_ps sv fo_ps x2 "
                 "xh3 xb xT3_ps xT3 k_ps k v1_ps v1 q1_ps q1 f_ps f y_ps xh4 xT4_ps xT4 gl_ps gl "
                 "kb sc_ps sub exp pt_ps pt ot_ps ot")
        names += "".join(f" var_{m} rs_{m}" for m in norms)
        s = {n: sem("s_" + n) for n in names.split()}
        fold_ps, fold_ok = sem("fold_ps"), sem("fold_ok")
        v1_zero, half_set = sem("v1_zero"), sem("half_set")

        blank_set, hot_ok, placed = sem("blank_set"), sem("hot_ok"), sem("placed")
        tiles_hot, starts_hot = sem("tiles_hot"), sem("starts_hot")
        early_in, late_in = ([sem(f"expert_in{n}") for n in range(h * NE // 2, (h + 1) * NE // 2)] for h in range(2))
        weights_ok, weights_in, asked = sem("weights_ok"), sem("weights_in"), sem("asked")
        g_diff, g_exp, picks, counted, routed = (sem(t) for t in ("g_diff", "g_exp", "picks", "counted", "routed"))
        xi_in = [sem(f"xi_in{u}") for u in range(2)]
        xt_ps, xt, gu_ps, silu, act_ok, ha_ps, ha, y_ps, y_ok, picked_ok, no_ok, turns, added = (
            sem("e_" + t) for t in ("xt_ps", "xt", "gu_ps", "silu", "act_ok", "ha_ps", "ha", "y_ps", "y_ok", "picked_ok", "no_ok", "turns", "added"))

        x_g = x_d.rearrange("(g b) p d -> g p b d", b=GB)
        c_g = ctx_d.rearrange("(g b) p d -> g p b d", b=GB)
        out_g, xh_g = (t.rearrange("(g b) p d -> g p b d", b=GB)
                       for t in (v[0:B * S, 0:D].rearrange("(b p) d -> b p d", b=B) for v in (out_d, xh_d)))
        LAST, UNITS = NG - 1, 2 * GB

        AHEAD = 4
        XT_PS, Y_PS = ps[:, 4, 0:D], [ps[:, 5 + u, 0:D] for u in range(2)]

        def tiles_of(eng, step):
            with eng.Fori(0, (NT - 3) // 2) as m:
                step(2 * m + 1, 1, m)
                step(2 * m + 2, 0, m + 1)

        def bank(k):
            return ps[:, k, :]

        def attend_bank(u):
            return 7 if u < UNITS - 1 else 0

        def halves(k, n=2):
            return ps[:, k:k + n, :].rearrange("p t (h n) -> p (t h) n", h=2)


        block = stack.enter_context(nc.Block())

        @block.sync
        def _(sp):
            def rows_of(m):
                sp.wait_ge(s["al"], m)
                sp.dma_start(C, c_g[m]).then_inc(c_in, 16)
                sp.wait_ge(s["x2"], m)
                sp.dma_start(X0, x_g[m]).then_inc(x_in, 16)

            def context_of(m, first=False):
                if not first:
                    sp.wait_ge(s["v1_ps"], m)
                sp.dma_start(YT, ctxT_d[m]).then_inc(y_in, 16)

            sp.dma_start(X0, x_g[0]).then_inc(x_in, 16)
            sp.dma_start(C, c_g[0]).then_inc(c_in, 16)
            sp.dma_start(keep[:, 0:KEEP_A], keep_d[:, 0:KEEP_A]).then_inc(keep_in, 16)
            sp.dma_start(ring[:, 0:FOLD_A], fold_d[:, 0:FOLD_A]).then_inc(fold_in, 16)
            sp.dma_start(ring[:, FOLD_A:FOLD_N], fold_d[:, FOLD_A:FOLD_N]).then_inc(fold_in2, 16)
            sp.dma_start(rows[:, :], rows_d.partition_broadcast(P)).then_inc(rows_in, 16)
            sp.dma_start(keep[:, KEEP_A:KEEP_N], keep_d[:, KEEP_A:KEEP_N]).then_inc(keep_in2, 16)
            context_of(0, first=True)
            for n in range(NE // 2):
                sp.dma_start(experts[:, n * EXP_N:(n + 1) * EXP_N], experts_d[n]).then_inc(early_in[n], 16)
            with sp.Fori(0, LAST) as n:
                rows_of(n + 1)
                context_of(n + 1)
            sp.wait_ge(s["x2"], NG)
            for n in range(NE // 2):
                if n == NE // 2 - 2:
                    sp.wait_ge(s["q1_ps"], NG)
                if n == NE // 2 - 1:
                    sp.wait_ge(s["sc_ps"], UNITS * NG)
                sp.dma_start(experts[:, (NE // 2 + n) * EXP_N:(NE // 2 + n + 1) * EXP_N], experts_d[NE // 2 + n]).then_inc(late_in[n], 16)
            sp.wait_ge(weights_ok, 2)
            sp.dma_start(xh_d[0:B * S, D:ROW].rearrange("(b p) e -> p b e", b=B), prob).then_inc(weights_in, 16)
            sp.wait_ge(added, 16 * NT)

        @block.gpsimd
        def _(pool):
            def root(n, name):
                pool.wait_ge(s["var_" + name], n + 1)
                pool.tensor_tensor(var[name][:, :], var[name][:, :], minus_half[:, :], ALU.pow).then_inc(s["rs_" + name], 1)

            def roots_in(m):
                root(m, "xh")
                pool.memset(CH[:, :, DC:D], 0.0).then_inc(s["ch_pad"], 1)
                root(m, "ch")

            def spread_keys(n, u):
                bb, t = u // 2, u % 2
                if u == 0:
                    pool.wait_ge(s["k"], n + 1)
                if u >= 2:
                    pool.wait_ge(s["sc_ps"], UNITS * n + u - 1)
                pool.tensor_tensor(KB[u % 2], KT[:, t, bb * S:(bb + 1) * S].unsqueeze(1).broadcast_to([P, HT4, S]),
                                   kept("head_mask").unsqueeze(2).broadcast_to([P, HT4, S]), ALU.mult).then_inc(s["kb"], 1)

            def add_value_row(m):
                pool.wait_ge(s["xh"], m + 1)
                pool.tensor_tensor(X0, X0, vo_row[:, :].unsqueeze(1).broadcast_to([P, GB, D]), ALU.add).then_inc(s["xv"], 1)

            def add_bias(n):
                pool.wait_ge(s["xh3"], n + 1)
                pool.tensor_tensor(X1[:, :, :], X1[:, :, :],
                                   row("ab2").unsqueeze(1).broadcast_to([P, GB, D]), ALU.add).then_inc(s["xb"], 1)

            pool.memset(minus_half[:, :], -0.5).then_inc(half_set, 1)
            pool.wait_ge(half_set, 1)
            pool.memset(blank[:, :], 0.0).then_inc(blank_set, 1)
            roots_in(0)
            pool.memset(V1[:, :, :, :], 0.0).then_inc(v1_zero, 1)
            pool.wait_ge(rows_in, 16)
            pool.wait_ge(fold_ok, 4)
            add_value_row(0)
            root(0, "xh2")
            root(0, "xh3")
            with pool.Fori(0, LAST) as n:
                spread_keys(n, 0)
                roots_in(n + 1)
                spread_keys(n, 1)
                spread_keys(n, 2)
                add_value_row(n + 1)
                spread_keys(n, 3)
                spread_keys(n, 4)
                spread_keys(n, 5)
                spread_keys(n, 6)
                root(n + 1, "xh2")
                spread_keys(n, 7)
                add_bias(n)
                root(n, "xh4")
                root(n + 1, "xh3")
            for u in range(UNITS):
                spread_keys(LAST, u)
            add_bias(LAST)
            root(LAST, "xh4")
            pool.wait_ge(tiles_hot, 1)
            for k in range(NPICK):
                of_k = slice(k * B, (k + 1) * B)
                pool.tensor_tensor(hot_tile[:, of_k, 1, :], one_hot[:, of_k, :], kept("tile_start").unsqueeze(2).broadcast_to([P, B, NT]), ALU.mult).then_inc(starts_hot, 1)

            def fetch(t, u):
                if not isinstance(t, int) or t >= 2:
                    pool.wait_ge(picked_ok, t - 1)
                    pool.wait_ge(xt_ps, t - 1)
                    pool.sem_inc(asked, 1)
                pool.indirect_dma_start(out=XI[u], out_offset=None, in_=xh_d,
                                        in_offset=bass.IndirectOffsetOnAxis(ap=row_in[u][:, 0:1], axis=0)).then_inc(xi_in[u], 16)

            def add(t, u):
                pool.wait_ge(y_ok, t + 3)
                if not isinstance(t, int) or t:
                    pool.wait_ge(added, 16 * t)
                pool.wait_ge(no_ok, t + 1)
                pool.sem_inc(turns, 1)
                pool.indirect_dma_start(out=out_d, out_offset=bass.IndirectOffsetOnAxis(ap=row_out[u][:, 0:1], axis=0),
                                        in_=YO[u], in_offset=None, compute_op=ALU.add).then_inc(added, 16)

            pool.wait_ge(stored, 32 * (NG + 1))
            pool.wait_ge(weights_in, 16)
            pool.wait_ge(routed, 1)
            for t in range(AHEAD + 1):
                fetch(t, t % 2)
            add(0, 0)
            with pool.Fori(0, (NT - 1 - AHEAD) // 2) as m:
                for t, u in ((2 * m + AHEAD + 1, 1), (2 * m + AHEAD + 2, 0)):
                    fetch(t, u)
                    add(t - AHEAD, u)
            for t in range(NT - AHEAD, NT):
                add(t, t % 2)

        @block.scalar
        def _(act):
            def rows_turned(m):
                act.wait_ge(s["xT_ps"], m + 1)
                act.copy(xT0, ps[:, 0:2, :]).then_inc(s["xT"], 1)

            def context_turned(m):
                act.wait_ge(s["cT_ps"], m + 1)
                act.copy(CT[:, 0, :], bank(2))
                act.copy(CT[:, 1, :], bank(7)).then_inc(s["cT"], 1)

            def query(m):
                act.wait_ge(s["q_ps"], m + 1)
                for t in range(KD):
                    ins = act.activation(Q[:, t, :], bank(1 + t), ACT.Identity, bias=q_col[:, t:t + 1], scale=kept("ln2_g")[:, t:t + 1])
                ins.then_inc(s["q"], 1)

            def value(m):
                act.wait_ge(s["v_ps"], m + 1)
                act.copy(V, halves(0)).then_inc(s["v"], 1)

            def exp_scores(m):
                act.wait_ge(s["nm"], m + 1)
                for t in range(GB):
                    ins = act.activation(PR[:, t, :], bank(2)[:, t * S:(t + 1) * S], ACT.Exp, bias=nm[:, t:t + 1],
                                         scale=float(D) ** -0.5, accum_out=sm[:, t:t + 1])
                ins.then_inc(s["p"], 1)

            def probs_turned(m):
                act.wait_ge(s["pT_ps"], m + 1)
                act.copy(PT, split(bank(2), GB)).then_inc(s["pT"], 1)

            def rows2_turned(m):
                act.wait_ge(s["xT2_ps"], m + 1)
                act.copy(xT0[:, 0, :], bank(2))
                act.copy(xT0[:, 1, :], bank(0)).then_inc(s["xT2"], 1)

            def hidden(m):
                act.wait_ge(s["h_ps"], m + 1)
                act.activation(HT, bank(1), ACT.Gelu, bias=b1_col[:, 0:1], scale=1.0).then_inc(s["h"], 1)

            def exp_logits(m):
                act.wait_ge(s["top"], m + 1)
                for t in range(GB):
                    ins = act.activation(EX[:, t, :], LG[:, t, :], ACT.Exp, bias=nm[:, t:t + 1], scale=inv_tau[:, 0:1])
                ins.then_inc(s["ex"], 1)

            def shares_turned(m):
                act.wait_ge(s["aT_ps"], m + 1)
                for o in range(2):
                    ins = act.activation(AT[:, :, o, :], bank(0)[:, 0:2 * P].rearrange("p (h n) -> p h n", h=2),
                                         ACT.Copy, scale=kept("half_mask")[:, o:o + 1])
                ins.then_inc(s["aT"], 1)

            def gates(m):
                act.wait_ge(s["rz"], m + 1)
                act.activation(RZ, RZ, ACT.Sigmoid).then_inc(s["rz_act"], 1)

            def candidate(m):
                act.wait_ge(s["n_pre"], m + 1)
                for t in range(KD):
                    ins = act.activation(NN[:, t, :], NN[:, t, :], ACT.Tanh, bias=kept("bih")[:, 4 + t:5 + t], scale=1.0)
                ins.then_inc(s["n_act"], 1)

            def key(n):
                act.wait_ge(s["k_ps"], n + 1)
                for k in range(KD):
                    ins = act.activation(KT[:, k, :], bank(5 + k), ACT.Identity, bias=kept("abk")[:, k:k + 1], scale=1.0)
                ins.then_inc(s["k"], 1)

            def rows3_turned(n):
                act.wait_ge(s["xT3_ps"], n + 1)
                act.copy(xT0, ps[:, 1:3, :]).then_inc(s["xT3"], 1)

            def value1(n):
                act.wait_ge(s["v1_ps"], n + 1)
                for o in range(2):
                    half = lambda v: v.rearrange("p t (h n) -> p t h n", n=32)[:, :, :, o * HD:(o + 1) * HD]
                    ins = act.copy(half(V1[:, :, o, :]), half(halves(5)))
                ins.then_inc(s["v1"], 1)

            def query1(n):
                act.wait_ge(s["q1_ps"], n + 1)
                for t in range(KD):
                    ins = act.activation(Q1[:, t, :], bank(3 + t), ACT.Identity, bias=kept("abq")[:, t:t + 1], scale=1.0)
                ins.then_inc(s["q1"], 1)

            def exp1(n, u):
                act.wait_ge(s["sub"], UNITS * n + u + 1)
                act.activation(PP[u % 2], PP[u % 2], ACT.Exp, scale=float(HD) ** -0.5).then_inc(s["exp"], 1)

            def probs1_turned(n, u):
                act.wait_ge(s["pt_ps"], UNITS * n + u + 1)
                if u >= 2:
                    act.wait_ge(s["ot_ps"], UNITS * n + u - 1)
                act.copy(PQ[u % 2], ps[:, 5:7, :].rearrange("p t (h n) -> p (t h) n", h=4)).then_inc(s["pt"], 1)

            def hidden1(n):
                for m in range(H1 // P):
                    act.wait_ge(s["f_ps"], H1 // P * n + m + 1)
                    ins = act.activation(HF[:, m, :], bank(3 + m), ACT.Relu, bias=ab1_col[:, m:m + 1], scale=1.0)
                ins.then_inc(s["f"], 1)

            def rows4_turned(n):
                act.wait_ge(s["xT4_ps"], n + 1)
                act.copy(xT1[:, :, :], ps[:, 3:5, :]).then_inc(s["xT4"], 1)

            def gate_logits(n):
                act.wait_ge(s["gl_ps"], n + 1)
                act.copy(gl[:, bass.ds(n * GB, GB), :], split(bank(7)[:, 0:GB * NE], GB)).then_inc(s["gl"], 1)

            def exp_gate(lo, hi):
                act.wait_ge(g_diff, 1 if hi < B else 2)
                act.activation(prob[:, lo:hi], prob[:, lo:hi], ACT.Exp).then_inc(g_exp, 1)

            def store(n):
                act.wait_ge(s["xh4"], n + 1)
                act.dma_start(out_g[n], X4[:, :, :]).then_inc(stored, 16)
                act.dma_start(xh_g[n], XH4[:, :, :]).then_inc(stored, 16)

            act.wait_ge(keep_in, 16)
            rows_turned(0)
            context_turned(0)
            act.wait_ge(blank_set, 1)
            act.dma_start(out_d[B * S:B * S + P, :], blank[:, 0:D]).then_inc(stored, 16)
            act.dma_start(xh_d[B * S:B * S + P, :], blank[:, :]).then_inc(stored, 16)
            act.wait_ge(v1_zero, 1)
            act.wait_ge(fold_ok, 2)
            query(0)
            exp_scores(0)
            value(0)
            probs_turned(0)
            act.wait_ge(keep_in2, 16)
            key(0)
            rows2_turned(0)
            hidden(0)
            exp_logits(0)
            shares_turned(0)
            gates(0)
            candidate(0)
            rows3_turned(0)
            with act.Fori(0, LAST) as n:
                query1(n)
                rows_turned(n + 1)
                value1(n)
                context_turned(n + 1)
                exp1(n, 0)
                query(n + 1)
                probs1_turned(n, 0)
                exp1(n, 1)
                exp_scores(n + 1)
                probs1_turned(n, 1)
                value(n + 1)
                probs_turned(n + 1)
                for u in (2, 3, 4):
                    exp1(n, u)
                    probs1_turned(n, u)
                rows2_turned(n + 1)
                exp1(n, 5)
                probs1_turned(n, 5)
                hidden(n + 1)
                exp1(n, 6)
                probs1_turned(n, 6)
                exp1(n, 7)
                exp_logits(n + 1)
                probs1_turned(n, 7)
                hidden1(n)
                shares_turned(n + 1)
                gates(n + 1)
                candidate(n + 1)
                key(n + 1)
                rows4_turned(n)
                rows3_turned(n + 1)
                gate_logits(n)
                store(n)
            query1(LAST)
            value1(LAST)
            for u in range(UNITS):
                exp1(LAST, u)
                probs1_turned(LAST, u)
            exp_gate(0, B - GB)
            hidden1(LAST)
            rows4_turned(LAST)
            gate_logits(LAST)
            store(LAST)
            act.sem_inc(turns, 1)
            act.sem_inc(y_ok, 2)
            exp_gate(B - GB, B)

            def turned(t, u):
                act.wait_ge(xt_ps, t + 1)
                act.copy(XIT[u], XT_PS.rearrange("p (k n) -> p k n", k=KD)).then_inc(xt, 1)

            def gate(t, u):
                act.wait_ge(gu_ps, t + 1)
                act.activation(HA[u], ps[:, 2 * u, :], ACT.Silu).then_inc(silu, 1)

            def answer(t, u):
                act.wait_ge(y_ps, t + 1)
                act.wait_ge(turns, t + 1)
                act.copy(YO[u], Y_PS[u]).then_inc(y_ok, 1)

            def step(t, u, half):
                turned(t + 2, u)
                gate(t + 1, 1 - u)
                answer(t - 1, 1 - u)

            turned(0, 0)
            turned(1, 1)
            gate(0, 0)
            turned(2, 0)
            gate(1, 1)
            tiles_of(act, step)
            gate(NT - 1, 0)
            for t in range(NT - 3, NT):
                answer(t, t % 2)

        @block.tensor
        def _(pe):
            def mm(out, pairs):
                for k, (w, m) in enumerate(pairs):
                    ins = pe.matmul(out, w, m, start=(k == 0), stop=(k == len(pairs) - 1))
                return ins

            def turn(out, t):
                return pe.transpose(out, t, ident)

            def turn_rows(src, banks):
                for k, o in enumerate(banks):
                    for t in range(GB):
                        ins = turn(bank(o)[:, t * S:(t + 1) * S], src[:, t, k * P:(k + 1) * P])
                return ins

            def turn_x(m):
                pe.wait_ge(s["xh"], m + 1)
                turn_rows(XH0, (0, 1)).then_inc(s["xT_ps"], 1)

            def turn_context(m):
                pe.wait_ge(s["xT"], m + 1)
                pe.wait_ge(s["ch"], m + 1)
                pe.wait_ge(s["ch_pad"], m + 1)
                turn_rows(CH, (2, 7)).then_inc(s["cT_ps"], 1)

            def query(m):
                pe.wait_ge(s["xT"], m + 1)
                pe.wait_ge(s["cT"], m + 1)
                for h in range(KD):
                    ins = mm(bank(1 + h), [(qk[:, k, h * P:(h + 1) * P], xT0[:, k, :]) for k in range(KD)])
                ins.then_inc(s["q_ps"], 1)

            def value(m):
                pe.wait_ge(s["q"], m + 1)
                for t in range(GB):
                    ins = mm(halves(0)[:, t, :], [(CT[:, k, t * S:(t + 1) * S], vo[:, k, :]) for k in range(KD)])
                ins.then_inc(s["v_ps"], 1)

            def score(m):
                pe.wait_ge(s["q"], m + 1)
                for t in range(GB):
                    tok = slice(t * S, (t + 1) * S)
                    ins = mm(bank(2)[:, tok], [(Q[:, k, tok], CT[:, k, tok]) for k in range(KD)])
                ins.then_inc(s["s_ps"], 1)

            def turn_probs(m):
                pe.wait_ge(s["p"], m + 1)
                for t in range(GB):
                    ins = turn(bank(2)[:, t * S:(t + 1) * S], PR[:, t, :])
                ins.then_inc(s["pT_ps"], 1)

            def attend(m):
                pe.wait_ge(s["pT"], m + 1)
                pe.wait_ge(s["v"], m + 1)
                for t in range(GB):
                    ins = mm(halves(0)[:, t, :], [(PT[:, t, :], V[:, t, :])])
                    if t % 2:
                        ins.then_inc(s["o_ps"], 1)

            def turn_x2(m):
                pe.wait_ge(s["xh2"], m + 1)
                turn_rows(XH0, (2, 0)).then_inc(s["xT2_ps"], 1)

            def hidden(m):
                pe.wait_ge(s["xT2"], m + 1)
                mm(bank(1), [(w1[:, k, :], xT0[:, k, :]) for k in range(KD)]).then_inc(s["h_ps"], 1)

            def logits(m):
                pe.wait_ge(s["h"], m + 1)
                for t in range(GB):
                    ins = mm(bank(2)[:, t * NSLOT:(t + 1) * NSLOT], [(HT[:, t * S:(t + 1) * S], kept("w2"))])
                ins.then_inc(s["lg_ps"], 1)

            def slot_inputs(m):
                pe.wait_ge(s["al"], m + 1)
                mm(bank(2)[:, 0:GB * NSLOT], [(ones, AL.rearrange("p t n -> p (t n)"))]).then_inc(s["ws_ps"], 1)
                for h in range(2):
                    ins = turn(bank(0)[:, h * P:(h + 1) * P], AL[:, 2 * h:2 * h + 2, :].rearrange("p t n -> p (t n)"))
                ins.then_inc(s["aT_ps"], 1)
                for k in range(KD):
                    for t in range(GB):
                        at = (k * GB + t) * NSLOT
                        ins = mm(bank(1)[:, at:at + NSLOT], [(XH0[:, t, k * P:(k + 1) * P], AL[:, t, :])])
                ins.then_inc(s["si_ps"], 1)

            def gates(m):
                pe.wait_ge(s["aT"], m + 1)
                pe.wait_ge(s["gi"], m + 1)
                for g, o in enumerate((0, 2, 1)):
                    for h in range(KD):
                        at = (g * KD + h) * P
                        ins = mm(bank(o)[:, h * 256:(h + 1) * 256], [(kept("wih", KD)[:, k, at:at + P], GI[:, k, :]) for k in range(KD)])
                    ins.then_inc(s["gx_ps"], 1)

            def slot_values(m):
                pe.wait_ge(s["sn"], m + 1)
                for h in range(2):
                    ins = mm(bank(0)[:, h * D:(h + 1) * D], [(SN[:, k, h * P:(h + 1) * P], fvo[:, k, :]) for k in range(KD)])
                ins.then_inc(s["sv_ps"], 1)

            def slot_outputs(m):
                pe.wait_ge(s["sv"], m + 1)
                for t in range(GB):
                    ins = mm(halves(1)[:, t, :], [(AT[:, t // 2, t % 2, :], SV[:, t // 2, :])])
                    if t % 2:
                        ins.then_inc(s["fo_ps"], 1)

            def key(n):
                pe.wait_ge(y_in, 16 * (n + 1))
                for h in range(KD):
                    ins = mm(bank(5 + h), [(kept("aWk", KD)[:, k, h * P:(h + 1) * P], YT[:, k, :]) for k in range(KD)])
                ins.then_inc(s["k_ps"], 1)

            def turn_x3(n):
                pe.wait_ge(s["xh3"], n + 1)
                turn_rows(XH3, (1, 2)).then_inc(s["xT3_ps"], 1)

            def value1(n):
                pe.wait_ge(s["k"], n + 1)
                for t in range(GB):
                    ins = mm(halves(5)[:, t, :], [(YT[:, k, t * S:(t + 1) * S], kept("aWv", KD)[:, k, :]) for k in range(KD)])
                ins.then_inc(s["v1_ps"], 1)

            def query1(n):
                pe.wait_ge(s["xT3"], n + 1)
                for h in range(KD):
                    ins = mm(bank(3 + h), [(kept("aWq", KD)[:, k, h * P:(h + 1) * P], xT0[:, k, :]) for k in range(KD)])
                ins.then_inc(s["q1_ps"], 1)

            def score1(n, u, at=3, ahead=1):
                bb, t = u // 2, u % 2
                pe.wait_ge(s["kb"], UNITS * n + u + 1)
                if u >= ahead:
                    pe.wait_ge(s["sub"], UNITS * n + u + 1 - ahead)
                elif not u:
                    pe.wait_ge(s["q1"], n + 1)
                for h in range(2):
                    own = slice(P // 2 * h, P // 2 * (h + 1))
                    ins = mm(bank(at + h), [(Q1[own, t, bb * S:(bb + 1) * S], KB[u % 2][own, :, :].rearrange("p h n -> p (h n)"))])
                ins.then_inc(s["sc_ps"], 1)

            def turn_probs1(n, u):
                pe.wait_ge(s["exp"], UNITS * n + u + 1)
                if u:
                    pe.wait_ge(s["pt"], UNITS * n + u)
                else:
                    pe.wait_ge(s["v1"], n + 1)
                for h in range(HT8):
                    ins = turn(ps[:, 5 + h // 4, h % 4 * S:(h % 4 + 1) * S], PP[u % 2][:, h, :])
                ins.then_inc(s["pt_ps"], 1)

            def attend1(n, u):
                bb, t = u // 2, u % 2
                pe.wait_ge(s["pt"], UNITS * n + u + 1)
                if 0 < u < UNITS - 1:
                    pe.wait_ge(s["ot"], UNITS * n + u)
                for st in range(4):
                    out = ps[32 * st:32 * st + 32, attend_bank(u), :]
                    mm(out[:, 0:S], [(V1[:, bb, o, 32 * (4 * t + st):32 * (4 * t + st) + 32], PQ[u % 2][:, 2 * st + o, :]) for o in range(2)])
                    ins = mm(out[:, S:2 * S], [(kept("ones_half", 2)[:, o, :], PQ[u % 2][:, 2 * st + o, :]) for o in range(2)])
                ins.then_inc(s["ot_ps"], 1)

            def hidden1(n):
                for own in (slice(0, GT - S), slice(GT - S, GT)):
                    pe.wait_ge(s["ot"], UNITS * (n + 1) - (0 if own.stop == GT else 2))
                    for m in range(H1 // P):
                        ins = mm(bank(3 + m)[:, own], [(kept("aW1", KD)[:, k, m * P:(m + 1) * P], OT[:, k, own]) for k in range(KD)])
                        if own.stop == GT:
                            ins.then_inc(s["f_ps"], 1)

            def outputs1(n, half):
                if not half:
                    pe.wait_ge(s["f"], n + 1)
                for t in (2 * half, 2 * half + 1):
                    ins = mm(halves(3)[:, t, :], [(HF[:, k, t * S:(t + 1) * S], kept("aW2", H1 // P)[:, k, :]) for k in range(H1 // P)])
                ins.then_inc(s["y_ps"], 1)

            def turn_x4(n):
                pe.wait_ge(s["xh4"], n + 1)
                turn_rows(XH4, (3, 4)).then_inc(s["xT4_ps"], 1)

            def gate_logits(n):
                pe.wait_ge(s["xT4"], n + 1)
                for t in range(GB):
                    ins = mm(bank(7)[:, t * NE:(t + 1) * NE], [(xT1[:, k, t * S:(t + 1) * S], kept("gate", KD)[:, k, :]) for k in range(KD)])
                ins.then_inc(s["gl_ps"], 1)

            w1 = kept("w1", 4)
            pe.wait_ge(keep_in, 16)
            turn_x(0)
            WqT, WkT, Wq, Wo, WvT, Wv = (fold(t) for t in ("WqT", "WkT", "Wq", "Wo", "WvT", "Wv"))
            pe.wait_ge(fold_in, 16)
            for m in range(KD):
                mm(ps[:, 3, m * D:(m + 1) * D], [(WqT[:, k, m * P:(m + 1) * P], WkT[:, k, :]) for k in range(KD)])
                ins = mm(ps[:, 5, m:m + 1], [(Wq[:, k, m * P:(m + 1) * P], kept("ln1_b")[:, k:k + 1]) for k in range(KD)])
            ins.then_inc(fold_ps, 1)
            turn_context(0)
            pe.wait_ge(fold_ok, 1)
            pe.wait_ge(s["cT"], 1)
            for m in range(KD):
                ins = mm(ps[:, 7, m:m + 1], [(WkT[:, k, m * P:(m + 1) * P], u_col[:, k:k + 1]) for k in range(KD)])
            ins.then_inc(fold_ps, 1)
            query(0)
            pe.wait_ge(fold_in2, 16)
            for m in range(KD):
                mm(ps[:, 4, m * D:(m + 1) * D], [(WvT[:, k, m * P:(m + 1) * P], Wo[:, k, :]) for k in range(KD)])
                ins = mm(ps[:, 0, m:m + 1], [(Wv[:, k, m * P:(m + 1) * P], kept("ln2_b")[:, k:k + 1]) for k in range(KD)])
            ins.then_inc(fold_ps, 1)
            score(0)
            for m in range(KD):
                mm(ps[:, 6, m * D:(m + 1) * D], [(fold("fwv")[:, k, m * P:(m + 1) * P], fold("fwoT")[:, k, :]) for k in range(KD)])
            pe.wait_ge(fold_ok, 3)
            mm(ps[:, 5, 0:D], [(spread[:, k, :], Wo[:, k, :]) for k in range(KD)]).then_inc(fold_ps, 1)
            value(0)
            turn_probs(0)
            pe.wait_ge(keep_in2, 16)
            pe.wait_ge(fold_ok, 4)
            mm(ps[:, 6, 0:1], [(w1[:, 2 + k, :], slot_mean[:, k:k + 1]) for k in range(KD)])
            mm(ps[:, 3, 0:D], [(spread[:, 2 + k, :], fold("fwoT")[:, k, :]) for k in range(KD)]).then_inc(fold_ps, 1)
            attend(0)
            pe.wait_ge(fold_ok, 5)
            key(0)
            turn_x2(0)
            hidden(0)
            logits(0)
            for m in range(6):
                ins = mm(ps[:, 4, m * NSLOT:(m + 1) * NSLOT], [(fold("whh")[:, k, m * P:(m + 1) * P], slots[:, k, :]) for k in range(KD)])
            ins.then_inc(fold_ps, 1)
            slot_inputs(0)
            gates(0)
            value1(0)
            slot_values(0)
            slot_outputs(0)
            for m in range(H1 // P):
                ins = mm(ps[:, 7, m:m + 1], [(kept("aW1", KD)[:, k, m * P:(m + 1) * P], kept("abv")[:, k:k + 1]) for k in range(KD)])
            ins.then_inc(fold_ps, 1)
            turn_x3(0)
            with pe.Fori(0, LAST) as n:
                query1(n)
                turn_x(n + 1)
                score1(n, 0)
                turn_context(n + 1)
                query(n + 1)
                score1(n, 1)
                score(n + 1)
                value(n + 1)
                turn_probs1(n, 0)
                score1(n, 2)
                turn_probs1(n, 1)
                attend1(n, 0)
                turn_probs(n + 1)
                score1(n, 3)
                attend(n + 1)
                turn_probs1(n, 2)
                attend1(n, 1)
                score1(n, 4)
                turn_probs1(n, 3)
                attend1(n, 2)
                score1(n, 5)
                turn_probs1(n, 4)
                turn_x2(n + 1)
                attend1(n, 3)
                score1(n, 6)
                turn_probs1(n, 5)
                attend1(n, 4)
                hidden(n + 1)
                score1(n, 7)
                logits(n + 1)
                turn_probs1(n, 6)
                attend1(n, 5)
                turn_probs1(n, 7)
                attend1(n, 6)
                attend1(n, 7)
                hidden1(n)
                slot_inputs(n + 1)
                outputs1(n, 0)
                gates(n + 1)
                outputs1(n, 1)
                key(n + 1)
                slot_values(n + 1)
                slot_outputs(n + 1)
                value1(n + 1)
                turn_x4(n)
                turn_x3(n + 1)
                gate_logits(n)
            query1(LAST)
            score1(LAST, 0, 3, 2)
            for u in range(UNITS):
                if u + 1 < UNITS:
                    score1(LAST, u + 1, 0 if u % 2 == 0 else 3, 2)
                turn_probs1(LAST, u)
                if u:
                    attend1(LAST, u - 1)
            attend1(LAST, UNITS - 1)
            hidden1(LAST)
            outputs1(LAST, 0)
            outputs1(LAST, 1)
            turn_x4(LAST)
            gate_logits(LAST)
            pe.wait_ge(picks, 2)
            flat = picked.rearrange("p b e -> p (b e)")
            mm(ps[:, 0, 0:B * NE], [(kept("upper"), flat)])
            mm(ps[:, 1, 0:B * NE], [(ones, flat)]).then_inc(counted, 1)
            for k in range(PICKS):
                if k % B == 0:
                    pe.wait_ge(hot_ok, k // B + 1)
                    pe.wait_ge(starts_hot, k // B + 1)
                ins = pe.matmul(ps[:, 2, 0:2 * NT], hot[:, k, :], hot_tile[:, k, :, :].rearrange("p v t -> p (v t)"), start=(k == 0), stop=(k == PICKS - 1))
            ins.then_inc(placed, 1)
            for n in range(NE // 2):
                pe.wait_ge(early_in[n], 16)
                pe.wait_ge(late_in[n], 16)
            pe.wait_ge(routed, 1)

            def turn_in(t, u, half):
                pe.wait_ge(xi_in[u], 16 * (half + 1))
                if not isinstance(t, int) or t:
                    pe.wait_ge(xt, t)
                for k in range(KD):
                    ins = turn(XT_PS[:, k * P:(k + 1) * P], XI[u][:, k * P:(k + 1) * P])
                ins.then_inc(xt_ps, 1)

            def gate_up(t, u):
                at = pe.value_load(e_id[0:1, bass.ds(t, 1)], min_val=0, max_val=NE - 1) * EXP_N
                pe.wait_ge(xt, t + 1)
                for g in range(2):
                    for k in range(KD):
                        ins = pe.matmul(ps[:, 2 * u + g, :], XIT[u][:, k, :], experts[:, bass.ds(at + (2 * k + g) * INTER, INTER)],
                                        start=(k == 0), stop=(k == KD - 1))
                ins.then_inc(gu_ps, 1)

            def turn_act(t, u):
                pe.wait_ge(act_ok, t + 1)
                for k in range(INTER // P):
                    ins = turn(ps[:, 7, k * P:(k + 1) * P], HA[u][:, k * P:(k + 1) * P])
                ins.then_inc(ha_ps, 1)

            def down(t, u):
                at = pe.value_load(e_id[0:1, bass.ds(t, 1)], min_val=0, max_val=NE - 1) * EXP_N
                pe.wait_ge(y_ok, t + 1)
                pe.wait_ge(ha, t + 1)
                for k in range(INTER // P):
                    ins = pe.matmul(Y_PS[u], HAT[u][:, k, :], experts[:, bass.ds(at + 2 * KD * INTER + k * D, D)],
                                    start=(k == 0), stop=(k == INTER // P - 1))
                ins.then_inc(y_ps, 1)

            def step(t, u, half):
                turn_in(t + 2, u, half + 1)
                gate_up(t + 1, 1 - u)
                down(t - 1, 1 - u)
                turn_act(t, u)

            turn_in(0, 0, 0)
            turn_in(1, 1, 0)
            gate_up(0, 0)
            turn_in(2, 0, 1)
            gate_up(1, 1)
            turn_act(0, 0)
            tiles_of(pe, step)
            gate_up(NT - 1, 0)
            down(NT - 3, 0)
            turn_act(NT - 2, 1)
            down(NT - 2, 1)
            turn_act(NT - 1, 0)
            down(NT - 1, 0)

        @block.vector
        def _(dve):
            settle = dve.drain

            def spread_of(src, width, name, scale=1.0, eps=EPS):
                for t in range(GB):
                    dve.bn_stats(stat[name][:, t, :], src[:, t, 0:width])
                gather_stats(name, scale, eps)

            def gather_stats(name, scale=1.0, eps=EPS):
                settle()
                for t in range(GB):
                    dve.bn_aggr(mv[name][:, t, :], stat[name][:, t, :])
                settle()
                dve.tensor_scalar(var[name][:, :], mv[name][:, :, 1], scale, eps, ALU.mult, ALU.add).then_inc(s["var_" + name], 1)

            def norm(n, src, out, width, name):
                dve.wait_ge(s["rs_" + name], n + 1)
                for t in range(GB):
                    ins = dve.tensor_scalar(out[:, t, 0:width], src[:, t, 0:width], mv[name][:, t, 0:1], var[name][:, t:t + 1],
                                            ALU.subtract, ALU.mult)
                ins.then_inc(s[name], 1)

            def norm_in(m):
                dve.wait_ge(x_in, 16 * (m + 1))
                spread_of(X0, D, "xh", 1.0 + EPS, EPS * EPS)
                norm(m, X0, XH0, D, "xh")
                dve.wait_ge(c_in, 16 * (m + 1))
                spread_of(C, DC, "ch")
                norm(m, C, CH, DC, "ch")

            def most(m):
                dve.wait_ge(s["s_ps"], m + 1)
                dve.tensor_reduce(nm[:, :], split(bank(2), GB), AXX, ALU.max)
                settle()
                dve.tensor_scalar(nm[:, :], nm[:, :], -float(D) ** -0.5, None, ALU.mult).then_inc(s["nm"], 1)

            def over_sum(m):
                dve.wait_ge(s["p"], m + 1)
                dve.reciprocal(sm[:, :], sm[:, :])
                settle()

            def add_attention(m):
                dve.wait_ge(s["xv"], m + 1)
                for half in range(2):
                    dve.wait_ge(s["o_ps"], 2 * m + half + 1)
                    own = range(GB)[GB // 2 * half:GB // 2 * (half + 1)]
                    for t in own:
                        dve.scalar_tensor_tensor(X0[:, t, :], halves(0)[:, t, :], sm[:, t:t + 1], X0[:, t, :], ALU.mult, ALU.add)
                    settle()
                    for t in own:
                        dve.bn_stats(stat["xh2"][:, t, :], X0[:, t, :])

            def top(m):
                dve.wait_ge(s["lg_ps"], m + 1)
                dve.tensor_tensor(LG, split(bank(2)[:, 0:GB * NSLOT], GB), row("b2").unsqueeze(1).broadcast_to([P, GB, NSLOT]), ALU.add)
                settle()
                for t in range(GB):
                    dve.max(m8[:, t, :], LG[:, t, :])
                settle()
                for t in range(GB):
                    dve.match_replace(LK[:, t, :], m8[:, t, :], LG[:, t, :], NEG)
                dve.tensor_scalar(nm[:, :], m8[:, :, 0], inv_tau[:, 0:1], -1.0, ALU.mult, ALU.mult).then_inc(s["top"], 1)
                settle()
                dve.tensor_tensor(MK, LK, LG, ALU.is_lt)

            def shares(m):
                settle()
                dve.wait_ge(s["ex"], m + 1)
                dve.tensor_tensor(EX, EX, MK, ALU.mult)
                settle()
                dve.tensor_reduce(sm[:, :], EX, AXX, ALU.add)
                settle()
                dve.reciprocal(sm[:, :], sm[:, :])
                settle()
                dve.tensor_tensor(AL, EX, sm[:, :].unsqueeze(2).broadcast_to([P, GB, NSLOT]), ALU.mult).then_inc(s["al"], 1)

            def slot_inputs(m):
                dve.wait_ge(s["ws_ps"], m + 1)
                dve.tensor_scalar(RW, bank(2)[:, 0:256], 1e-8, None, ALU.add)
                settle()
                dve.reciprocal(RW, RW)
                settle()
                dve.wait_ge(s["si_ps"], m + 1)
                dve.tensor_tensor(GI, split(bank(1), KD), RW.unsqueeze(1).broadcast_to([P, KD, 256]), ALU.mult).then_inc(s["gi"], 1)

            def per_batch(v):
                return v.rearrange("p (t n) -> p t n", t=GB)

            def for_batches(v):
                return v.unsqueeze(1).broadcast_to([P, GB, NSLOT])

            def gates(m):
                for g, o in enumerate((0, 2)):
                    dve.wait_ge(s["gx_ps"], 3 * m + g + 1)
                    for k in range(KD):
                        ins = dve.tensor_tensor(per_batch(RZ[:, g, k * 256:(k + 1) * 256]), per_batch(bank(o)[:, k * 256:(k + 1) * 256]),
                                                for_batches(gh[:, g * KD + k, :]), ALU.add)
                ins.then_inc(s["rz"], 1)

            def candidate(m):
                dve.wait_ge(s["rz_act"], m + 1)
                for k in range(KD):
                    dve.tensor_tensor(per_batch(NN[:, k, :]), per_batch(RZ[:, 0, k * 256:(k + 1) * 256]), for_batches(gh[:, 4 + k, :]), ALU.mult)
                settle()
                dve.wait_ge(s["gx_ps"], 3 * m + 3)
                dve.tensor_tensor(NN, NN, split(bank(1), KD), ALU.add).then_inc(s["n_pre"], 1)

            def new_slots(m):
                dve.wait_ge(s["n_act"], m + 1)
                for k in range(KD):
                    dve.tensor_tensor(per_batch(DF[:, k, :]), for_batches(slots[:, k, :]), per_batch(NN[:, k, :]), ALU.subtract)
                settle()
                dve.tensor_tensor(DF, DF, split(RZ[:, 1, :], KD), ALU.mult)
                settle()
                dve.tensor_tensor(SN, DF, NN, ALU.add).then_inc(s["sn"], 1)

            def slot_values(m):
                dve.wait_ge(s["sv_ps"], m + 1)
                dve.tensor_tensor(SV, split(bank(0), 2), fvo_row[:, :].unsqueeze(1).broadcast_to([P, 2, D]), ALU.add).then_inc(s["sv"], 1)

            def add_slots(m):
                for half in range(2):
                    own = slice(GB // 2 * half, GB // 2 * (half + 1))
                    dve.wait_ge(s["fo_ps"], 2 * m + half + 1)
                    ins = dve.tensor_tensor(X1[:, own, :], X0[:, own, :], halves(1 + half, 1), ALU.add)
                    settle()
                    for t in range(GB)[own]:
                        dve.bn_stats(stat["xh3"][:, t, :], X1[:, t, :])
                ins.then_inc(s["x2"], 1)

            def shift(n, u, at=3):
                sc = ps[:, at:at + 2, :].rearrange("p t (h n) -> p (t h) n", h=4)
                dve.wait_ge(s["sc_ps"], UNITS * n + u + 1)
                dve.tensor_reduce(mx[u % 2][:, :], sc, AXX, ALU.max)
                settle()
                if u >= 2:
                    dve.wait_ge(s["pt_ps"], UNITS * n + u - 1)
                dve.tensor_tensor(PP[u % 2], sc, mx[u % 2][:, :].unsqueeze(2).broadcast_to([P, HT8, S]), ALU.subtract).then_inc(s["sub"], 1)

            def divide(n, u):
                bb, t = u // 2, u % 2
                dve.wait_ge(s["ot_ps"], UNITS * n + u + 1)
                o = attend_bank(u)
                dve.reciprocal(rc[u % 2][:, :], bank(o)[:, S:2 * S])
                settle()
                dve.tensor_tensor(OT[:, t, bb * S:(bb + 1) * S], bank(o)[:, 0:S], rc[u % 2][:, :], ALU.mult).then_inc(s["ot"], 1)

            def add_outputs(n, half):
                if not half:
                    dve.wait_ge(s["xb"], n + 1)
                    dve.wait_ge(stored, 32 * (n + 1))
                dve.wait_ge(s["y_ps"], 2 * n + half + 1)
                own = slice(GB // 2 * half, GB // 2 * (half + 1))
                dve.tensor_tensor(X4[:, own, :], X1[:, own, :], halves(3 + half, 1), ALU.add)
                settle()
                for t in range(GB)[own]:
                    dve.bn_stats(stat["xh4"][:, t, :], X4[:, t, :])

            def route(lo, hi):
                n_b, part = hi - lo, lambda v: v[:, lo:hi]
                over = lambda v: part(v).unsqueeze(2).broadcast_to([P, n_b, NE])
                in_groups = lambda v: part(v).rearrange("p b (g e) -> p b g e", g=NGRP)

                def ranks(v, n, before, out):
                    one, two_ = (t[:, 0:n_b * n * n].rearrange("p (b e o) -> p b e o", b=n_b, e=n) for t in (cmp1, cmp2))
                    other, own = part(v).unsqueeze(2).broadcast_to([P, n_b, n, n]), part(v).unsqueeze(3).broadcast_to([P, n_b, n, n])
                    dve.tensor_tensor(one, other, own, ALU.is_gt)
                    dve.tensor_tensor(two_, other, own, ALU.is_equal)
                    settle()
                    dve.tensor_tensor(two_, two_, kept(before, n).unsqueeze(1).broadcast_to([P, n_b, n, n]), ALU.mult)
                    settle()
                    dve.tensor_tensor(one, one, two_, ALU.add)
                    settle()
                    dve.tensor_reduce(part(out), one, AXX, ALU.add)
                    settle()

                dve.wait_ge(s["gl"], hi // GB)
                dve.tensor_reduce(part(g_max), part(gl), AXX, ALU.max)
                settle()
                dve.tensor_tensor(part(prob), part(gl), over(g_max), ALU.subtract).then_inc(g_diff, 1)
                dve.wait_ge(g_exp, 1 if hi < B else 2)
                dve.tensor_reduce(part(g_max), part(prob), AXX, ALU.add)
                settle()
                dve.reciprocal(part(g_max), part(g_max))
                settle()
                dve.tensor_tensor(part(prob), part(prob), over(g_max), ALU.mult)
                settle()
                dve.tensor_reduce(part(g_top), in_groups(prob), AXX, ALU.max)
                settle()
                ranks(g_top, NGRP, "before_group", r4)
                dve.tensor_scalar(part(g_ok), part(r4), float(NPICK), None, ALU.is_lt)
                settle()
                dve.tensor_tensor(in_groups(masked), in_groups(prob), part(g_ok).unsqueeze(3).broadcast_to([P, n_b, NGRP, NE // NGRP]), ALU.mult)
                settle()
                ranks(masked, NE, "before_expert", work)
                dve.tensor_scalar(part(picked), part(work), float(NPICK), None, ALU.is_lt).then_inc(picks, 1)
                dve.tensor_scalar(part(first), part(work), 0.0, None, ALU.is_equal)
                dve.tensor_scalar(part(second), part(work), 1.0, None, ALU.is_equal)
                settle()
                dve.tensor_tensor(part(prob), part(masked), part(picked), ALU.mult)
                settle()
                dve.tensor_reduce(part(w_sum), part(prob), AXX, ALU.add)
                settle()
                dve.reciprocal(part(w_sum), part(w_sum))
                settle()
                dve.tensor_tensor(part(prob), part(prob), over(w_sum), ALU.mult).then_inc(weights_ok, 1)

            norm_in(0)
            def folded():
                settle()
                dve.tensor_copy(mark[:, :], kept("bq")[:, 0:1]).then_inc(fold_ok, 1)

            dve.wait_ge(keep_in, 16)
            dve.wait_ge(fold_ps, 1)
            dve.tensor_tensor(u_col[:, :], ps[:, 5, 0:KD], kept("bq"), ALU.add)
            for m in range(KD):
                dve.tensor_scalar(qk[:, m, :], ps[:, 3, m * D:(m + 1) * D], kept("ln1_g")[:, m:m + 1], None, ALU.mult)
            folded()
            dve.wait_ge(fold_ps, 2)
            dve.tensor_tensor(q_col[:, :], ps[:, 7, 0:KD], kept("ln2_g"), ALU.mult)
            folded()
            dve.wait_ge(fold_ps, 3)
            dve.tensor_tensor(w_col[:, :], ps[:, 0, 0:KD], kept("bv"), ALU.add)
            for m in range(KD):
                dve.tensor_scalar(vo[:, m, :], ps[:, 4, m * D:(m + 1) * D], kept("ln2_g")[:, m:m + 1], None, ALU.mult)
            settle()
            for k in range(KD):
                dve.tensor_scalar(spread[:, k, :], ones, w_col[:, k:k + 1], None, ALU.mult)
                dve.tensor_scalar(spread[:, 2 + k, :], ones, kept("fbv")[:, k:k + 1], None, ALU.mult)
            folded()
            dve.wait_ge(rows_in, 16)
            dve.tensor_tensor(slots[:, :, :], fold("slots"), row("slot_scale").unsqueeze(1).broadcast_to([P, KD, NSLOT]), ALU.mult)
            dve.tensor_scalar(inv_tau[:, :], row("tau"), -1.0, None, ALU.mult)
            dve.tensor_copy(b_rz[:, :], kept("bhh"))
            most(0)
            dve.tensor_tensor(inv_tau[:, :], inv_tau[:, :], row("tau"), ALU.max)
            dve.tensor_reduce(slot_mean[:, :], slots[:, :, :], AXX, ALU.add)
            dve.tensor_tensor(b_rz[:, 0:4], b_rz[:, 0:4], kept("bih")[:, 0:4], ALU.add)
            settle()
            dve.tensor_scalar(inv_tau[:, :], inv_tau[:, :], 0.1, None, ALU.add)
            dve.tensor_scalar(slot_mean[:, :], slot_mean[:, :], 1.0 / NSLOT, None, ALU.mult)
            settle()
            dve.reciprocal(inv_tau[:, :], inv_tau[:, :])
            dve.wait_ge(fold_ps, 4)
            dve.tensor_tensor(vo_row[:, :], ps[:, 5, 0:D], row("bo"), ALU.add)
            dve.tensor_copy(fvo[:, :, :], split(ps[:, 6, :], KD))
            folded()
            over_sum(0)
            dve.wait_ge(fold_ps, 5)
            dve.tensor_tensor(b1_col[:, :], ps[:, 6, 0:1], kept("b1"), ALU.add)
            dve.tensor_tensor(fvo_row[:, :], ps[:, 3, 0:D], row("fbo"), ALU.add)
            folded()
            add_attention(0)
            gather_stats("xh2")
            norm(0, X0, XH0, D, "xh2")
            top(0)
            shares(0)
            dve.wait_ge(fold_ps, 6)
            dve.tensor_tensor(gh[:, :, :], ps[:, 4, 0:6 * NSLOT].rearrange("p (m n) -> p m n", m=6),
                              b_rz[:, :].unsqueeze(2).broadcast_to([P, 6, NSLOT]), ALU.add)
            slot_inputs(0)
            gates(0)
            candidate(0)
            new_slots(0)
            slot_values(0)
            add_slots(0)
            gather_stats("xh3")
            norm(0, X1, XH3, D, "xh3")
            dve.wait_ge(fold_ps, 7)
            dve.tensor_tensor(ab1_col[:, :], ps[:, 7, 0:H1 // P], kept("ab1"), ALU.add)
            with dve.Fori(0, LAST) as n:
                norm_in(n + 1)
                shift(n, 0)
                shift(n, 1)
                most(n + 1)
                shift(n, 2)
                divide(n, 0)
                over_sum(n + 1)
                shift(n, 3)
                add_attention(n + 1)
                divide(n, 1)
                gather_stats("xh2")
                shift(n, 4)
                norm(n + 1, X0, XH0, D, "xh2")
                divide(n, 2)
                shift(n, 5)
                divide(n, 3)
                shift(n, 6)
                divide(n, 4)
                shift(n, 7)
                top(n + 1)
                divide(n, 5)
                divide(n, 6)
                divide(n, 7)
                shares(n + 1)
                slot_inputs(n + 1)
                gates(n + 1)
                candidate(n + 1)
                new_slots(n + 1)
                add_outputs(n, 0)
                add_outputs(n, 1)
                slot_values(n + 1)
                gather_stats("xh4")
                add_slots(n + 1)
                gather_stats("xh3")
                norm(n, X4, XH4, D, "xh4")
                norm(n + 1, X1, XH3, D, "xh3")
            for u in range(UNITS):
                shift(LAST, u, 0 if u % 2 else 3)
                if u >= 2:
                    divide(LAST, u - 2)
            divide(LAST, UNITS - 2)
            divide(LAST, UNITS - 1)
            route(0, B - GB)
            add_outputs(LAST, 0)
            add_outputs(LAST, 1)
            gather_stats("xh4")
            norm(LAST, X4, XH4, D, "xh4")
            route(B - GB, B)
            dve.wait_ge(counted, 1)
            dve.tensor_copy(total, ps[:, 1, 0:B * NE].rearrange("p (b e) -> p b e", b=B))
            settle()
            here, there, step = total, sums, 1
            while step < B:
                dve.tensor_copy(there[:, 0:step, :], here[:, 0:step, :])
                dve.tensor_tensor(there[:, step:B, :], here[:, step:B, :], here[:, 0:B - step, :], ALU.add)
                settle()
                here, there, step = there, (sums2 if there is sums else sums), 2 * step
            c816 = cmp1[:, 0:NE * B].rearrange("p (e t) -> p e t", e=NE)
            dve.tensor_tensor(c816, here[:, B - 1, :].unsqueeze(2).broadcast_to([P, NE, B]),
                              kept("tile_start").unsqueeze(1).broadcast_to([P, NE, B]), ALU.is_gt)
            settle()
            dve.tensor_reduce(n_tiles, c816, AXX, ALU.add)
            settle()
            c88 = cmp1[:, 0:NE * NE].rearrange("p (e o) -> p e o", e=NE)
            dve.tensor_tensor(c88, kept("before_expert", NE), n_tiles.unsqueeze(1).broadcast_to([P, NE, NE]), ALU.mult)
            settle()
            dve.tensor_reduce(t_off, c88, AXX, ALU.add)
            settle()
            dve.tensor_tensor(t_end, t_off, n_tiles, ALU.add)
            dve.tensor_scalar(t_off, t_off, float(P), None, ALU.mult)
            settle()
            ct8 = cmp1[:, 0:NT * NE].rearrange("p (t e) -> p t e", t=NT)
            dve.tensor_tensor(ct8, t_end.unsqueeze(1).broadcast_to([P, NT, NE]), kept("tile_no").unsqueeze(2).broadcast_to([P, NT, NE]), ALU.is_le)
            dve.tensor_tensor(place, here, total, ALU.subtract)
            settle()
            dve.tensor_reduce(e_flt, ct8, AXX, ALU.add)
            dve.tensor_tensor(place, place, ps[:, 0, 0:B * NE].rearrange("p (b e) -> p b e", b=B), ALU.add)
            settle()
            dve.tensor_scalar(e_id[:, :], e_flt, float(NE - 1), None, ALU.min)
            dve.tensor_scalar(e_min, e_flt, float(NE - 1), None, ALU.min)
            dve.tensor_tensor(place, place, t_off.unsqueeze(1).broadcast_to([P, B, NE]), ALU.add)
            settle()
            for k, which in enumerate((first, second)):
                dve.tensor_tensor(work, place, which, ALU.mult)
                settle()
                dve.tensor_reduce(pos[:, k, :], work, AXX, ALU.add)
                settle()
            at = pos.rearrange("p k b -> p (k b)")
            dve.tensor_copy(at_i[:, :], at)
            settle()
            dve.tensor_scalar(at_i[:, :], at_i[:, :], P - 1, None, ALU.bitwise_and)
            settle()
            dve.tensor_copy(col_at, at_i[:, :])
            settle()
            dve.tensor_tensor(tile_at, at, col_at, ALU.subtract)
            settle()
            dve.tensor_tensor(one_hot, kept("tile_first").unsqueeze(1).broadcast_to([P, PICKS, NT]),
                              tile_at.unsqueeze(2).broadcast_to([P, PICKS, NT]), ALU.is_equal)
            settle()
            dve.tensor_scalar(hot_tile[:, :, 0, :], one_hot, kept("row_next"), None, ALU.mult).then_inc(tiles_hot, 1)
            for k in range(NPICK):
                dve.tensor_tensor(hot[:, k * B:(k + 1) * B, :], kept("col_no").unsqueeze(1).broadcast_to([P, B, P]),
                                  col_at[:, k * B:(k + 1) * B].unsqueeze(2).broadcast_to([P, B, P]), ALU.is_equal).then_inc(hot_ok, 1)
            dve.tensor_tensor(tile_hot[:, :, :], e_min.unsqueeze(2).broadcast_to([P, NT, NE]),
                              kept("expert_no").unsqueeze(1).broadcast_to([P, NT, NE]), ALU.is_equal)
            dve.memset(row_no[:, NT:NT + 2], 0)
            dve.wait_ge(placed, 1)
            dve.tensor_scalar(hole, ps[:, 2, 0:NT], 0.0, kept("hole_row"), ALU.is_equal, ALU.mult)
            settle()
            dve.scalar_tensor_tensor(hole, ps[:, 2, 0:NT], -1.0, hole, ALU.add, ALU.add)
            settle()
            dve.tensor_tensor(row_no[:, 0:NT], hole, ps[:, 2, NT:2 * NT], ALU.add)
            settle()
            dve.tensor_copy(row_in[0][:, :], row_no[:, 0:1])
            dve.tensor_copy(row_in[1][:, :], row_no[:, 1:2])
            settle()
            dve.tensor_copy(mark[:, :], w_sum[:, 0:1]).then_inc(routed, 1)

            def pick(t, u, half):
                dve.wait_ge(xi_in[u], 16 * (half + 1))
                dve.tensor_tensor(row_w8[u][:, :], tile_hot[:, bass.ds(t, 1), :].rearrange("p t e -> p (t e)"), XI[u][:, D:ROW], ALU.mult)
                dve.tensor_copy(row_in[u][:, :], row_no[:, bass.ds(t + 2, 1)])
                settle()
                dve.tensor_reduce(row_w[u][:, :], row_w8[u][:, :], AXX, ALU.add).then_inc(picked_ok, 1)

            def gated(t, u):
                dve.wait_ge(silu, t + 1)
                dve.wait_ge(picked_ok, t + 1)
                dve.scalar_tensor_tensor(HA[u], HA[u], row_w[u][:, 0:1], ps[:, 2 * u + 1, :], ALU.mult, ALU.mult).then_inc(act_ok, 1)

            def turned(t, u):
                dve.wait_ge(ha_ps, t + 1)
                dve.tensor_copy(HAT[u], ps[:, 7, :].rearrange("p (k n) -> p k n", k=INTER // P)).then_inc(ha, 1)

            def number(t, u):
                dve.wait_ge(turns, t + 1)
                dve.tensor_copy(row_out[u][:, :], row_no[:, bass.ds(t, 1)]).then_inc(no_ok, 1)

            def step(t, u, half):
                pick(t + 2, u, half + 1)
                gated(t + 1, 1 - u)
                turned(t, u)
                number(t - 1, 1 - u)

            pick(0, 0, 0)
            pick(1, 1, 0)
            gated(0, 0)
            pick(2, 0, 1)
            gated(1, 1)
            turned(0, 0)
            tiles_of(dve, step)
            gated(NT - 1, 0)
            for t in range(NT - 3, NT):
                if t > NT - 3:
                    turned(t, t % 2)
                number(t, t % 2)


def packed(parts, width, arrays):
    out = np.zeros((P, width), np.float32)
    for name, (at, n) in parts.items():
        out[:, at:at + n] = np.reshape(arrays[name], (P, n))
    return out


def tiles(w):
    k = -(-w.shape[0] // P)
    full = np.zeros((k * P, w.shape[1]), w.dtype)
    full[:w.shape[0]] = w
    return full.reshape(k, P, w.shape[1]).transpose(1, 0, 2)


def wide(w, n):
    full = np.zeros((w.shape[0], n), w.dtype)
    full[:, :w.shape[1]] = w
    return full


def kernel(**inputs):
    import concourse.bacc as bacc
    from concourse.bass_utils import run_bass_kernel_spmd

    v = {k: np.asarray(a) for k, a in inputs.items()}
    A, Fn, L, M = (lambda n: v["L0_xattn_" + n]), (lambda n: v["L0_ffn_" + n]), (lambda n: v["L1_xattn_" + n]), (lambda n: v["L1_ffn_" + n])
    col = lambda w: tiles(w.reshape(-1, 1))[:, :, 0]
    half = np.zeros((P, 2, 32), np.float32)
    half[:, 0, :HD] = 1
    half[:, 1, HD:] = 1
    keep = packed(KEEP, KEEP_N, {
        "ident": np.eye(P, dtype=np.float32), "ones": np.ones((P, P), np.float32), "ones_half": half,
        "head_mask": np.tile(np.kron(np.eye(HT4, dtype=np.float32), np.ones((HD, 1), np.float32)), (2, 1)),
        "half_mask": np.kron(np.eye(2, dtype=np.float32), np.ones((NSLOT, 1), np.float32)),
        "w1": tiles(Fn("w1").T), "w2": Fn("w2").T, "wih": tiles(Fn("gru_wih").T),
        "aWq": tiles(L("Wq")), "aWk": tiles(L("Wk")), "aWv": tiles(L("Wv")), "aW1": tiles(L("W1")), "aW2": tiles(L("W2")),
        "gate": tiles(M("gate_w").T),
        "upper": np.triu(np.ones((P, P), np.float32), 1),
        "before_group": np.tile(np.tril(np.ones((NGRP, NGRP), np.float32), -1).reshape(1, -1), (P, 1)),
        "before_expert": np.tile(np.tril(np.ones((NE, NE), np.float32), -1).reshape(1, -1), (P, 1)),
        "tile_start": np.tile(P * np.arange(B, dtype=np.float32), (P, 1)), "tile_no": np.tile(np.arange(NT, dtype=np.float32), (P, 1)),
        "expert_no": np.tile(np.arange(NE, dtype=np.float32), (P, 1)),
        "col_no": np.tile(np.arange(P, dtype=np.float32), (P, 1)), "tile_first": np.tile(P * np.arange(NT, dtype=np.float32), (P, 1)),
        "row_next": 1 + np.arange(P, dtype=np.float32), "hole_row": B * S + 1 + np.arange(P, dtype=np.float32),
        "ln1_g": col(A("ln1_g")), "ln1_b": col(A("ln1_b")), "ln2_g": col(A("ln2_g")), "ln2_b": col(A("ln2_b")),
        "bq": col(A("bq")), "bv": col(A("bv")), "b1": col(Fn("b1")), "bih": col(Fn("gru_bih")), "bhh": col(Fn("gru_bhh")),
        "fbv": col(Fn("bv")), "abq": col(L("bq")), "abk": col(L("bk")), "abv": col(L("bv")), "ab1": col(L("b1")),
    })
    fold = packed(FOLD, FOLD_N, {
        "WqT": tiles(A("Wq").T), "WkT": tiles(wide(A("Wk").T, D)), "Wq": tiles(A("Wq")), "Wo": tiles(A("Wo")),
        "WvT": tiles(wide(A("Wv").T, D)), "Wv": tiles(A("Wv")), "whh": tiles(Fn("gru_whh").T),
        "fwv": tiles(Fn("wv")), "fwoT": tiles(Fn("wo").T), "slots": tiles(Fn("slot_init").T),
    })
    rows = np.zeros((ROWS_N,), np.float32)
    for name, a in (("bo", A("bo")), ("slot_scale", Fn("slot_scale")), ("b2", Fn("b2")), ("tau", Fn("tau")),
                    ("fbo", Fn("bo")), ("ab2", L("b2"))):
        at, n = ROWS[name]
        rows[at:at + n] = a.reshape(-1)
    ctx = v["ctx_768"]
    ctxT = tiles(ctx.reshape(B * S, DC).T).reshape(P, KD, NG, GT).transpose(2, 0, 1, 3)
    experts = np.concatenate([
        M("w13_weight").transpose(0, 2, 1).reshape(NE, KD, P, 2 * INTER).transpose(0, 2, 1, 3).reshape(NE, P, -1),
        M("w2_weight").transpose(0, 2, 1).reshape(NE, INTER // P, P, D).transpose(0, 2, 1, 3).reshape(NE, P, -1)], axis=2)
    arrays = {"x": v["x"], "ctx": ctx, "ctxT": ctxT, "keep": keep, "fold": fold, "rows": rows, "experts": experts}

    nc = bacc.Bacc("TRN2", target_bir_lowering=False, num_devices=1)
    args, feed = [], {}
    for name, a in arrays.items():
        a = np.ascontiguousarray(a)
        feed["in_" + name] = a
        args.append(nc.dram_tensor("in_" + name, a.shape, mybir.dt.from_np(a.dtype), kind="ExternalInput").ap())
    out = nc.dram_tensor("out_x", (B * S + P, D), F32, kind="ExternalOutput").ap()
    scratch = [nc.dram_tensor(name, shape, F32, kind="Internal").ap()
               for name, shape in (("normed3", (B * S + P, ROW)),)]
    build(nc, *args, *scratch, out)
    r = run_bass_kernel_spmd(nc, [feed], core_ids=[0])
    return r.results[0]["out_x"][:B * S].reshape(B, S, D)
```
